# Optimizing a Trainium2 kernel written in Bass

```python
import numpy as np
import jax
import jax.numpy as jnp

def _softmax(x, axis=-1):
    return jax.nn.softmax(x, axis=axis)

def _gelu(x):
    return jax.nn.gelu(x, approximate=True)

def _silu(x):
    return jax.nn.silu(x)

def _sigmoid(x):
    return jax.nn.sigmoid(x)

def _layernorm(x, axis=-1, eps=1e-05):
    m = jnp.mean(x, axis=axis, keepdims=True)
    v = jnp.var(x, axis=axis, keepdims=True)
    return (x - m) / jnp.sqrt(v + eps)

def _scatter_add(tgt, idx, src, axis=0):
    return tgt.at[idx].add(src)

def _segment_sum(src, seg, n):
    return jax.ops.segment_sum(src, seg, n)
kernel_name = 'mk_decoder_preln_d2_seqx_r4_01ad80'

def setup_inputs(seed: int=0):
    np.random.seed(seed)
    _w = jnp.asarray

    def _rec_inputs():
        import jax
        import jax.numpy as jnp
        _rk = jax.random.key(seed)
        x = -0.0003929 + 0.9999 * jax.random.normal(jax.random.fold_in(_rk, 1), (2, 1024, 256), jnp.float32)
        _lenS = 1024 - jax.random.randint(jax.random.fold_in(_rk, 7), (2,), 0, max(1, 1024 // 4) + 1, jnp.int32)
        _lenS2 = 77 - jax.random.randint(jax.random.fold_in(_rk, 8), (2,), 0, max(1, 77 // 4) + 1, jnp.int32)
        _ctx_768P = jax.random.normal(jax.random.fold_in(_rk, 11), (2, 16, 192), jnp.float32)
        _ctx_768c = jax.random.dirichlet(jax.random.fold_in(_rk, 511), 0.3 * jnp.ones((16,), jnp.float32), (2, 77))
        _ctx_768t = jnp.einsum('bsk,bkd->bsd', _ctx_768c, _ctx_768P)
        _ctx_768t = _ctx_768t * jax.lax.rsqrt(jnp.mean(jnp.square(_ctx_768t)) + 1e-12) * 0.953939
        ctx_768 = 0.00095986 + 0.999812 * (_ctx_768t + 0.3 * jax.random.normal(jax.random.fold_in(_rk, 611), (2, 77, 192), jnp.float32))
        _validS = jnp.arange(1024)[None, :] < _lenS[:, None]
        _validS2 = jnp.arange(77)[None, :] < _lenS2[:, None]
        _causal = jnp.tril(jnp.ones((1024, 1024), dtype=bool))
        mask_BxS2_bf1 = jnp.ones((2, 77), dtype=bool)
        return (x, ctx_768, mask_BxS2_bf1)
    x, ctx_768, mask_BxS2_bf1 = _rec_inputs()

    def _L0_attn_setup():
        import jax, jax.numpy as jnp
        import numpy as np
        D = 256
        H = 16
        DH = D // H
        key = jax.random.key(seed)
        k1, k2, k3 = jax.random.split(key, 3)
        x = jax.random.normal(k1, (2, 512, D), dtype=jnp.float32)
        w_qkv = jax.random.normal(k2, (3 * D, D), dtype=jnp.float32) * D ** (-0.5)
        w_proj = jax.random.normal(k3, (D, D), dtype=jnp.float32) * D ** (-0.5)
        return {'x': x, 'w_qkv': w_qkv, 'w_proj': w_proj}
    _L0_attn_all = _L0_attn_setup()
    _L0_attn_in = {k: v for k, v in _L0_attn_all.items() if k in ('w_qkv', 'w_proj')}
    del _L0_attn_all

    def _L0_xattn_setup():
        import jax, jax.numpy as jnp
        import numpy as np
        DIM = 256
        CTX_DIM = 192
        HEADS = 16
        key = jax.random.key(seed)
        ks = jax.random.split(key, 7)
        B, N, M = (4, 1024, 64)
        x = jax.random.normal(ks[0], (B, N, DIM), dtype=jnp.float32)
        context = jax.random.normal(ks[1], (B, M, CTX_DIM), dtype=jnp.float32)
        context_mask = jnp.ones((B, M), dtype=bool)
        s_d = 1.0 / np.sqrt(DIM)
        s_c = 1.0 / np.sqrt(CTX_DIM)
        Wq = jax.random.normal(ks[2], (DIM, DIM), dtype=jnp.float32) * s_d
        Wk = jax.random.normal(ks[3], (CTX_DIM, DIM), dtype=jnp.float32) * s_c
        Wv = jax.random.normal(ks[4], (CTX_DIM, DIM), dtype=jnp.float32) * s_c
        Wo = jax.random.normal(ks[5], (DIM, DIM), dtype=jnp.float32) * s_d
        return {'x': x, 'context': context, 'context_mask': context_mask, 'Wq': Wq, 'Wk': Wk, 'Wv': Wv, 'Wo': Wo}
    _L0_xattn_all = _L0_xattn_setup()
    _L0_xattn_in = {k: v for k, v in _L0_xattn_all.items() if k in ('Wq', 'Wk', 'Wv', 'Wo')}
    del _L0_xattn_all

    def _L0_ffn_setup():
        import jax, jax.numpy as jnp
        import numpy as np
        B, S, D, E, K = (4, 512, 256, 8, 2)
        key = jax.random.key(seed)
        k1, k2, k3 = jax.random.split(key, 3)
        scale = 1.0 / np.sqrt(D)
        x = jax.random.normal(k1, (B, S, D), dtype=jnp.float32)
        Wg = jax.random.normal(k2, (D, E), dtype=jnp.float32) * scale
        bg = jnp.zeros((E,), dtype=jnp.float32)
        We = jax.random.normal(k3, (E, D, D), dtype=jnp.float32) * scale
        be = jnp.zeros((E, D), dtype=jnp.float32)
        return {'x': x, 'Wg': Wg, 'bg': bg, 'We': We, 'be': be}
    _L0_ffn_all = _L0_ffn_setup()
    _L0_ffn_in = {k: v for k, v in _L0_ffn_all.items() if k in ('Wg', 'bg', 'We', 'be')}
    del _L0_ffn_all

    def _L1_attn_setup():
        import jax, jax.numpy as jnp
        import numpy as np
        B, T, D, H = (64, 128, 256, 256)
        key = jax.random.key(seed)
        k1, k2, k3 = jax.random.split(key, 3)
        scale = 0.02
        return {'x': jax.random.normal(k1, (B, T, D), dtype=jnp.float32), 'Wi': jax.random.normal(k2, (H, D), dtype=jnp.float32) * scale, 'bi': jnp.zeros((H,), dtype=jnp.float32), 'Wh': jax.random.normal(k3, (H, H), dtype=jnp.float32) * scale, 'bh': jnp.zeros((H,), dtype=jnp.float32)}
    _L1_attn_all = _L1_attn_setup()
    _L1_attn_in = {k: v for k, v in _L1_attn_all.items() if k in ('Wi', 'bi', 'Wh', 'bh')}
    del _L1_attn_all

    def _L1_xattn_setup():
        import jax, jax.numpy as jnp
        import numpy as np
        N_HEADS = 16
        DIM_EMBED = 256
        DIM_CROSS = 192
        DIM_HEAD = DIM_EMBED // N_HEADS
        key = jax.random.key(seed)
        ks = jax.random.split(key, 10)
        B, Sq, Sk = (8, 1024, 77)
        s_e = 1.0 / np.sqrt(DIM_EMBED)
        s_c = 1.0 / np.sqrt(DIM_CROSS)
        return {'x': jax.random.normal(ks[0], (B, Sq, DIM_EMBED), jnp.float32), 'y': jax.random.normal(ks[1], (B, Sk, DIM_CROSS), jnp.float32), 'wq': jax.random.normal(ks[2], (DIM_EMBED, DIM_EMBED), jnp.float32) * s_e, 'bq': jax.random.normal(ks[3], (DIM_EMBED,), jnp.float32) * 0.01, 'wk': jax.random.normal(ks[4], (DIM_CROSS, DIM_EMBED), jnp.float32) * s_c, 'bk': jax.random.normal(ks[5], (DIM_EMBED,), jnp.float32) * 0.01, 'wv': jax.random.normal(ks[6], (DIM_CROSS, DIM_EMBED), jnp.float32) * s_c, 'bv': jax.random.normal(ks[7], (DIM_EMBED,), jnp.float32) * 0.01, 'wo': jax.random.normal(ks[8], (DIM_EMBED, DIM_EMBED), jnp.float32) * s_e, 'bo': jax.random.normal(ks[9], (DIM_EMBED,), jnp.float32) * 0.01}
    _L1_xattn_all = _L1_xattn_setup()
    _L1_xattn_in = {k: v for k, v in _L1_xattn_all.items() if k in ('wq', 'bq', 'wk', 'bk', 'wv', 'bv', 'wo', 'bo')}
    del _L1_xattn_all

    def _L1_ffn_setup():
        import jax, jax.numpy as jnp
        import numpy as np
        E = 16
        G = 4
        EPG = E // G
        K = 4
        TOPK_GROUP = 2
        PER_GROUP_K = K // TOPK_GROUP

        def _route(xf, router_w, correction_bias):
            S = xf.shape[0]
            logits = xf @ router_w.T
            scores = jax.nn.sigmoid(logits)
            sb = scores + correction_bias
            grp_top = jax.lax.top_k(sb.reshape(S, G, EPG), PER_GROUP_K)[0]
            group_scores = grp_top.sum(axis=-1)
            _, group_idx = jax.lax.top_k(group_scores, TOPK_GROUP)
            group_mask = jnp.zeros((S, G), sb.dtype).at[jnp.arange(S)[:, None], group_idx].set(1.0)
            score_mask = jnp.broadcast_to(group_mask[:, :, None], (S, G, EPG)).reshape(S, E)
            masked = jnp.where(score_mask > 0, sb, -jnp.inf)
            _, topk_idx = jax.lax.top_k(masked, K)
            w = jnp.take_along_axis(scores, topk_idx, axis=1)
            w = w / (w.sum(axis=-1, keepdims=True) + 1e-20)
            return (topk_idx, w, scores)
        key = jax.random.key(seed)
        ks = jax.random.split(key, 9)
        B, T, C, H, HS = (2, 256, 256, 64, 512)
        std = 0.02
        return {'x': jax.random.normal(ks[0], (B, T, C), jnp.float32), 'router_w': jax.random.normal(ks[1], (E, C), jnp.float32) * std, 'correction_bias': jnp.zeros((E,), jnp.float32), 'gate_w': jax.random.normal(ks[2], (E, C, H), jnp.float32) * std, 'up_w': jax.random.normal(ks[3], (E, C, H), jnp.float32) * std, 'down_w': jax.random.normal(ks[4], (E, H, C), jnp.float32) * std, 'shared_gate_w': jax.random.normal(ks[5], (HS, C), jnp.float32) * std, 'shared_up_w': jax.random.normal(ks[6], (HS, C), jnp.float32) * std, 'shared_down_w': jax.random.normal(ks[7], (C, HS), jnp.float32) * std}
    _L1_ffn_all = _L1_ffn_setup()
    _L1_ffn_in = {k: v for k, v in _L1_ffn_all.items() if k in ('router_w', 'correction_bias', 'gate_w', 'up_w', 'down_w', 'shared_gate_w', 'shared_up_w', 'shared_down_w')}
    del _L1_ffn_all
    return {'x': x, 'ctx_768': ctx_768, 'mask_BxS2_bf1': mask_BxS2_bf1, 'L0_attn_w_qkv': _L0_attn_in['w_qkv'], 'L0_attn_w_proj': _L0_attn_in['w_proj'], 'L0_xattn_Wq': _L0_xattn_in['Wq'], 'L0_xattn_Wk': _L0_xattn_in['Wk'], 'L0_xattn_Wv': _L0_xattn_in['Wv'], 'L0_xattn_Wo': _L0_xattn_in['Wo'], 'L0_ffn_Wg': _L0_ffn_in['Wg'], 'L0_ffn_bg': _L0_ffn_in['bg'], 'L0_ffn_We': _L0_ffn_in['We'], 'L0_ffn_be': _L0_ffn_in['be'], 'L1_attn_Wi': _L1_attn_in['Wi'], 'L1_attn_bi': _L1_attn_in['bi'], 'L1_attn_Wh': _L1_attn_in['Wh'], 'L1_attn_bh': _L1_attn_in['bh'], 'L1_xattn_wq': _L1_xattn_in['wq'], 'L1_xattn_bq': _L1_xattn_in['bq'], 'L1_xattn_wk': _L1_xattn_in['wk'], 'L1_xattn_bk': _L1_xattn_in['bk'], 'L1_xattn_wv': _L1_xattn_in['wv'], 'L1_xattn_bv': _L1_xattn_in['bv'], 'L1_xattn_wo': _L1_xattn_in['wo'], 'L1_xattn_bo': _L1_xattn_in['bo'], 'L1_ffn_router_w': _L1_ffn_in['router_w'], 'L1_ffn_correction_bias': _L1_ffn_in['correction_bias'], 'L1_ffn_gate_w': _L1_ffn_in['gate_w'], 'L1_ffn_up_w': _L1_ffn_in['up_w'], 'L1_ffn_down_w': _L1_ffn_in['down_w'], 'L1_ffn_shared_gate_w': _L1_ffn_in['shared_gate_w'], 'L1_ffn_shared_up_w': _L1_ffn_in['shared_up_w'], 'L1_ffn_shared_down_w': _L1_ffn_in['shared_down_w']}

def reference(x, ctx_768, mask_BxS2_bf1, L0_attn_w_qkv, L0_attn_w_proj, L0_xattn_Wq, L0_xattn_Wk, L0_xattn_Wv, L0_xattn_Wo, L0_ffn_Wg, L0_ffn_bg, L0_ffn_We, L0_ffn_be, L1_attn_Wi, L1_attn_bi, L1_attn_Wh, L1_attn_bh, L1_xattn_wq, L1_xattn_bq, L1_xattn_wk, L1_xattn_bk, L1_xattn_wv, L1_xattn_bv, L1_xattn_wo, L1_xattn_bo, L1_ffn_router_w, L1_ffn_correction_bias, L1_ffn_gate_w, L1_ffn_up_w, L1_ffn_down_w, L1_ffn_shared_gate_w, L1_ffn_shared_up_w, L1_ffn_shared_down_w):
    import jax
    import jax.numpy as jnp

    def _L0_attn_ref(x, w_qkv, w_proj):
        import jax, jax.numpy as jnp
        import numpy as np
        D = 256
        H = 16
        DH = D // H
        B, L, _ = x.shape
        qkv = x @ w_qkv.T
        q, k, v = jnp.split(qkv, 3, axis=-1)
        q = q.reshape(B, L, H, DH)
        k = k.reshape(B, L, H, DH)
        v = v.reshape(B, L, H, DH)
        scale = 1.0 / np.sqrt(DH)
        scores = jnp.einsum('blhd,bmhd->bhlm', q, k) * scale
        causal = jnp.arange(L)[:, None] < jnp.arange(L)[None, :]
        scores = jnp.where(causal[None, None, :, :], -jnp.inf, scores)
        att = jax.nn.softmax(scores, axis=-1)
        out = jnp.einsum('bhlm,bmhd->blhd', att, v)
        out = out.reshape(B, L, D)
        return out @ w_proj.T

    def _L0_xattn_ref(x, context, context_mask, Wq, Wk, Wv, Wo):
        import jax, jax.numpy as jnp
        import numpy as np
        DIM = 256
        CTX_DIM = 192
        HEADS = 16
        B, N, _ = x.shape
        M = context.shape[1]
        hd = DIM // HEADS
        scale = hd ** (-0.5)
        q = (x @ Wq).reshape(B, N, HEADS, hd).transpose(0, 2, 1, 3)
        k = (context @ Wk).reshape(B, M, HEADS, hd).transpose(0, 2, 1, 3)
        v = (context @ Wv).reshape(B, M, HEADS, hd).transpose(0, 2, 1, 3)
        scores = jnp.einsum('bhid,bhjd->bhij', q, k) * scale
        max_neg = -jnp.finfo(scores.dtype).max
        scores = jnp.where(context_mask[:, None, None, :], scores, max_neg)
        attn = jax.nn.softmax(scores, axis=-1)
        out = jnp.einsum('bhij,bhjd->bhid', attn, v)
        out = out.transpose(0, 2, 1, 3).reshape(B, N, DIM)
        return out @ Wo

    def _L0_ffn_ref(x, Wg, bg, We, be):
        import jax, jax.numpy as jnp
        import numpy as np
        B, S, D, E, K = (4, 512, 256, 8, 2)
        gate_scores = jnp.einsum('bsd,de->bse', x, Wg) + bg
        topk_values, topk_indices = jax.lax.top_k(gate_scores, K)
        sel = jax.nn.one_hot(topk_indices, E, dtype=jnp.bool_).any(axis=-2)
        masked = jnp.where(sel, gate_scores, -jnp.inf)
        gate_weights = jax.nn.softmax(masked, axis=-1)
        expert_outputs = jnp.einsum('bsd,edh->bseh', x, We) + be
        fused = jnp.einsum('bse,bseh->bsh', gate_weights, expert_outputs)
        return fused

    def _L1_attn_ref(x, Wi, bi, Wh, bh):
        import jax, jax.numpy as jnp
        import numpy as np
        B, T, D, H = (64, 128, 256, 256)
        xi = jnp.einsum('btd,hd->bth', x, Wi) + bi

        def step(h, xt):
            h_new = jnp.tanh(xt + h @ Wh.T + bh)
            return (h_new, h_new)
        h0 = jnp.zeros((x.shape[0], Wh.shape[0]), dtype=x.dtype)
        _, hs = jax.lax.scan(step, h0, jnp.swapaxes(xi, 0, 1))
        return jnp.swapaxes(hs, 0, 1)

    def _L1_xattn_ref(x, y, wq, bq, wk, bk, wv, bv, wo, bo):
        import jax, jax.numpy as jnp
        import numpy as np
        N_HEADS = 16
        DIM_EMBED = 256
        DIM_CROSS = 192
        DIM_HEAD = DIM_EMBED // N_HEADS
        B, Sq, E = x.shape
        H, D = (N_HEADS, DIM_HEAD)
        q = (x @ wq + bq).reshape(B, Sq, H, D).transpose(0, 2, 1, 3)
        k = (y @ wk + bk).reshape(B, -1, H, D).transpose(0, 2, 1, 3)
        v = (y @ wv + bv).reshape(B, -1, H, D).transpose(0, 2, 1, 3)
        scores = jnp.einsum('bhqd,bhkd->bhqk', q, k) / jnp.sqrt(jnp.asarray(D, x.dtype))
        attn = jax.nn.softmax(scores, axis=-1)
        out = jnp.einsum('bhqk,bhkd->bhqd', attn, v)
        out = out.transpose(0, 2, 1, 3).reshape(B, Sq, E)
        return out @ wo + bo

    def _L1_ffn_ref(x, router_w, correction_bias, gate_w, up_w, down_w, shared_gate_w, shared_up_w, shared_down_w):
        import jax, jax.numpy as jnp
        import numpy as np
        E = 16
        G = 4
        EPG = E // G
        K = 4
        TOPK_GROUP = 2
        PER_GROUP_K = K // TOPK_GROUP

        def _route(xf, router_w, correction_bias):
            S = xf.shape[0]
            logits = xf @ router_w.T
            scores = jax.nn.sigmoid(logits)
            sb = scores + correction_bias
            grp_top = jax.lax.top_k(sb.reshape(S, G, EPG), PER_GROUP_K)[0]
            group_scores = grp_top.sum(axis=-1)
            _, group_idx = jax.lax.top_k(group_scores, TOPK_GROUP)
            group_mask = jnp.zeros((S, G), sb.dtype).at[jnp.arange(S)[:, None], group_idx].set(1.0)
            score_mask = jnp.broadcast_to(group_mask[:, :, None], (S, G, EPG)).reshape(S, E)
            masked = jnp.where(score_mask > 0, sb, -jnp.inf)
            _, topk_idx = jax.lax.top_k(masked, K)
            w = jnp.take_along_axis(scores, topk_idx, axis=1)
            w = w / (w.sum(axis=-1, keepdims=True) + 1e-20)
            return (topk_idx, w, scores)
        B, T, C = x.shape
        S = B * T
        xf = x.reshape(S, C)
        sg = xf @ shared_gate_w.T
        su = xf @ shared_up_w.T
        shared_out = jax.nn.silu(sg) * su @ shared_down_w.T
        topk_idx, w, _scores = _route(xf, router_w, correction_bias)
        combine = jnp.zeros((S, E), xf.dtype).at[jnp.arange(S)[:, None], topk_idx].add(w)
        g = jnp.einsum('sc,ech->esh', xf, gate_w)
        u = jnp.einsum('sc,ech->esh', xf, up_w)
        h = jax.nn.silu(g) * u
        hw = h * combine.T[:, :, None]
        routed = jnp.einsum('esh,ehc->sc', hw, down_w)
        return (shared_out + routed).reshape(B, T, C)
    x = x + _L0_attn_ref(_layernorm(x, axis=-1), L0_attn_w_qkv, L0_attn_w_proj)
    x = x + _L0_xattn_ref(_layernorm(x, axis=-1), ctx_768, mask_BxS2_bf1, L0_xattn_Wq, L0_xattn_Wk, L0_xattn_Wv, L0_xattn_Wo)
    x = x + _L0_ffn_ref(_layernorm(x, axis=-1), L0_ffn_Wg, L0_ffn_bg, L0_ffn_We, L0_ffn_be)
    x = x + _L1_attn_ref(_layernorm(x, axis=-1), L1_attn_Wi, L1_attn_bi, L1_attn_Wh, L1_attn_bh)
    x = x + _L1_xattn_ref(_layernorm(x, axis=-1), ctx_768, L1_xattn_wq, L1_xattn_bq, L1_xattn_wk, L1_xattn_bk, L1_xattn_wv, L1_xattn_bv, L1_xattn_wo, L1_xattn_bo)
    x = x + _L1_ffn_ref(_layernorm(x, axis=-1), L1_ffn_router_w, L1_ffn_correction_bias, L1_ffn_gate_w, L1_ffn_up_w, L1_ffn_down_w, L1_ffn_shared_gate_w, L1_ffn_shared_up_w, L1_ffn_shared_down_w)
    return x

_drawn_inputs = setup_inputs


def setup_inputs(seed=0):
    import zlib

    import numpy as np

    out = dict(_drawn_inputs(seed))
    spreads = {'L0_ffn_bg': (0.0, 0.1),
     'L0_ffn_be': (0.0, 0.1),
     'L1_attn_bi': (0.0, 0.1),
     'L1_attn_bh': (0.0, 0.1),
     'L1_ffn_correction_bias': (0.0, 0.8)}
    factors = {'L1_xattn_bq': 8.0,
     'L1_xattn_bk': 8.0,
     'L1_xattn_bv': 8.0,
     'L1_xattn_bo': 8.0,
     'L1_ffn_router_w': 8.0,
     'L1_ffn_gate_w': 8.0,
     'L1_ffn_up_w': 8.0,
     'L1_ffn_down_w': 8.0,
     'L1_ffn_shared_gate_w': 3.668,
     'L1_ffn_shared_up_w': 3.557,
     'L1_ffn_shared_down_w': 3.56}
    for name, (base, spread) in spreads.items():
        noise = np.random.default_rng([zlib.crc32(name.encode()), seed]).standard_normal(out[name].shape)
        drawn = base * np.exp(spread * noise) if base else spread * noise
        out[name] = jnp.asarray(drawn.astype(out[name].dtype))
    for name, factor in factors.items():
        out[name] = (out[name] * factor).astype(out[name].dtype)
    return out
```

```python
from contextlib import ExitStack

import numpy as np

import concourse.bass as bass
from concourse import mybir

F32 = mybir.dt.float32
BF16 = mybir.dt.bfloat16
U8 = mybir.dt.uint8
ALU = mybir.AluOpType
ACT = mybir.ActivationFunctionType
AX = mybir.AxisListType

P = 128
B, S, D = 2, 1024, 256
KD = D // P
NT = B * S // P
TC = 4
NC = NT // TC
CH = TC * P
H, DH = 16, 16
HG = 4
NG = H // HG
QD = 32
M2, C2 = 77, 192
CK = C2 // 2
SCALE = float(DH) ** -0.5
BIG = float(2.0 ** 100)
EPS = 1e-5
COMBOS = [(0, 0), (0, 1), (1, 0), (0, 2), (1, 1), (2, 0)]
R_MASK = len(COMBOS) * DH
R_MAX = R_MASK + 1
R_ALL = R_MAX + 3
E0, TOP0 = 8, 2
E1, G1, TOP1 = 16, 4, 4
EPG = E1 // G1
HID = 512 + E1 * 64
MH = HID // P
MS = 512 // P


class Prog:

    def __init__(self, nc, ctx):
        self.nc, self.ctx, self.stage = nc, ctx, ""
        self.sems = []

    def sb(self, name, shape, dt=F32, ctx=None):
        return (ctx or self.ctx).enter_context(self.nc.sbuf_tensor(self.stage + name, shape, dt))

    def sem(self, name):
        self.sems.append(self.nc.alloc_semaphore(name=name))
        return self.sems[-1]

    def recycle(self):
        self.nc.clear_and_free_semaphores(self.sems)
        self.nc.all_engine_barrier()
        self.sems = []


def acc(pe, out, pairs):
    for n, (lhs, rhs) in enumerate(pairs):
        last = pe.matmul(out, lhs, rhs, start=(n == 0), stop=(n == len(pairs) - 1))
    return last


def constants(g):
    nc = g.nc
    g.ident = g.sb("ident", [P, P])
    g.identb = g.sb("identb", [P, P], BF16)
    g.mask_qk = g.sb("mask_qk", [P, P], BF16)
    g.mask_kq = g.sb("mask_kq", [P, P], BF16)
    g.sel_sum = g.sb("sel_sum", [P, P])
    g.neg_half = g.sb("neg_half", [P, NT])
    g.tie8 = g.sb("tie8", [P, E0, E0])
    g.tie16 = g.sb("tie16", [P, E1, E1])
    g.sel_pair = g.sb("sel_pair", [P, MH - MS, P], BF16)
    zeroed, filled = g.sem("zeroed"), g.sem("filled")
    with nc.Block() as block:
        @block.gpsimd
        def _(pool):
            for t, value in ((g.ident, 0.0), (g.identb, 0.0), (g.mask_qk, 0.0), (g.mask_kq, 0.0),
                             (g.sel_sum, 0.0), (g.neg_half, -0.5), (g.tie8, 1.0), (g.tie16, 1.0), (g.sel_pair, 1.0)):
                pool.memset(t[:], value).then_inc(zeroed, 1)
            pool.wait_ge(zeroed, 9)
            for t in (g.ident, g.identb):
                pool.affine_select(out=t[:], in_=t[:], compare_op=ALU.not_equal, fill=1.0, base=0,
                                   pattern=[[-1, P]], channel_multiplier=1).then_inc(filled, 1)
            pool.affine_select(out=g.mask_qk[:], in_=g.mask_qk[:], compare_op=ALU.is_ge, fill=-BIG, base=0,
                               pattern=[[-1, P]], channel_multiplier=1).then_inc(filled, 1)
            pool.affine_select(out=g.mask_kq[:], in_=g.mask_kq[:], compare_op=ALU.is_ge, fill=-BIG, base=0,
                               pattern=[[1, P]], channel_multiplier=-1).then_inc(filled, 1)
            pool.affine_select(out=g.sel_sum[:].rearrange("p (j c) -> p j c", c=QD),
                               in_=g.sel_sum[:].rearrange("p (j c) -> p j c", c=QD),
                               compare_op=ALU.not_equal, fill=1.0, base=-DH,
                               pattern=[[-QD, P // QD], [0, QD]], channel_multiplier=1).then_inc(filled, 1)
            for t, e in ((g.tie8, E0), (g.tie16, E1)):
                pool.affine_select(out=t[:], in_=t[:], compare_op=ALU.is_ge, fill=0.0, base=-1,
                                   pattern=[[1, e], [-1, e]], channel_multiplier=0).then_inc(filled, 1)
            pool.memset(g.sel_pair[:], 0.0).then_inc(zeroed, 1)
            pool.wait_ge(zeroed, 10)
            for n in range(3):
                v = g.sel_pair[:].rearrange("p m (a i) -> p m a i", a=2)
                pool.affine_select(out=v, in_=v, compare_op=ALU.not_equal, fill=1.0, base=-QD * n,
                                   pattern=[[-2, MH - MS], [-1, 2], [0, 64]], channel_multiplier=1).then_inc(filled, 1)
                pool.wait_ge(filled, 8 + n)


class Norm:

    def __init__(self, g, n):
        self.g = g
        self.stats, self.meanvar = g.sem(f"n{n}_stats"), g.sem(f"n{n}_meanvar")
        self.var_eps, self.rstd = g.sem(f"n{n}_var_eps"), g.sem(f"n{n}_rstd")
        self.xn, self.turned, self.xnT = g.sem(f"n{n}_xn"), g.sem(f"n{n}_turned"), g.sem(f"n{n}_xnT")

    def vector(self, v, chunk_ready):
        g = self.g
        for c in range(NC + 1):
            if c < NC:
                chunk_ready(c)
                for t in range(TC * c, TC * c + TC):
                    v.bn_stats(g.bn[:, t, :], g.x[:, t, :]).then_inc(self.stats, 1)
                for t in range(TC * c, TC * c + TC):
                    v.wait_ge(self.stats, t + 1)
                    v.bn_aggr(g.mv[:, t, :], g.bn[:, t, :]).then_inc(self.meanvar, 1)
                v.wait_ge(self.meanvar, TC * (c + 1))
                v.tensor_scalar(g.ve[:, TC * c:TC * c + TC], g.mv[:, TC * c:TC * c + TC, 1], EPS, None,
                                ALU.add).then_inc(self.var_eps, 1)
            if c:
                v.wait_ge(self.rstd, c)
                for t in range(TC * (c - 1), TC * c):
                    v.tensor_scalar(g.xn[:, t, :], g.x[:, t, :], g.mv[:, t, 0:1], g.rs[:, t:t + 1],
                                    ALU.subtract, ALU.mult).then_inc(self.xn, 1)

    def gpsimd(self, pool):
        g = self.g
        for c in range(NC):
            pool.wait_ge(self.var_eps, c + 1)
            pool.tensor_tensor(g.rs[:, TC * c:TC * c + TC], g.ve[:, TC * c:TC * c + TC],
                               g.neg_half[:, 0:TC], ALU.pow).then_inc(self.rstd, 1)

    def tensor(self, pe, c):
        g = self.g
        for t in range(TC * c, TC * c + TC):
            pe.wait_ge(self.xn, t + 1)
            if t >= 2:
                pe.wait_ge(self.xnT, t - 1)
            bank = (g.b4, g.b5)[t % 2]
            for k in range(KD):
                last = pe.transpose(bank[:, k * P:(k + 1) * P], g.xn[:, t, k * P:(k + 1) * P], g.ident[:])
            last.then_inc(self.turned, 1)

    def scalar(self, act, c):
        g = self.g
        for t in range(TC * c, TC * c + TC):
            act.wait_ge(self.turned, t + 1)
            bank = (g.b4, g.b5)[t % 2]
            act.activation(g.xnT[:, :, t * P:(t + 1) * P], bank[:, 0:KD * P].rearrange("p (k n) -> p k n", k=KD),
                           ACT.Copy).then_inc(self.xnT, 1)


def norm_buffers(g, ctx, pad=False):
    g.bn = g.sb("bn", [P, NT, 6], ctx=ctx)
    g.mv = g.sb("mv", [P, NT, 2], ctx=ctx)
    g.ve = g.sb("ve", [P, NT], ctx=ctx)
    g.rs = g.sb("rs", [P, NT], ctx=ctx)
    g.xn = g.sb("xn", [P, NT, D], ctx=ctx)
    g.xnT_flat = g.sb("xnT", [P, KD * B * S + (S if pad else 0)], ctx=ctx)
    g.xnT = g.xnT_flat[:, 0:KD * B * S].rearrange("p (k n) -> p k n", k=KD)


def project(g, n, w, causal):
    g.stage = f"p{n}_"
    nc = g.nc
    with ExitStack() as ctx:
        norm_buffers(g, ctx)
        NM = 4 if causal else 2
        if causal:
            wqkv = g.sb("wqkv", [P, KD, 3 * D], ctx=ctx)
        else:
            wq = g.sb("wq", [P, KD, D], ctx=ctx)
            wk = g.sb("wk", [CK, 2, D], ctx=ctx)
            wv = g.sb("wv", [CK, 2, D], ctx=ctx)
            cT = g.sb("cT", [CK, 2, B * M2], ctx=ctx)
            bq = g.sb("bq", [P, KD], ctx=ctx)
            bk = g.sb("bk", [P, KD], ctx=ctx)
            bv = g.sb("bv", [P, D], ctx=ctx)
        parts = g.sb("parts", [P, 3, 3, CH], BF16, ctx=ctx)
        rest = g.sb("rest", [P, 3, CH], ctx=ctx)
        ln = Norm(g, n)
        w_in, made, part1, left, part2, part3, vmade, vcopied, ones = (g.sem(f"p{n}_{s}") for s in (
            "w_in", "made", "part1", "left", "part2", "part3", "vmade", "vcopied", "ones"))
        x_in = [g.sem(f"p{n}_x_in{c}") for c in range(NC)] if causal else None
        stored = [g.sem(f"p{n}_stored{r}") for r in range(3)]
        banks = [g.big0[:, 0, :], g.big0[:, 1, :], g.big1[:, 0, :], g.big1[:, 1, :]]
        jobs = [("x", c, m) for c in range(NC) for m in range(NM)]
        if not causal:
            jobs = [("c", 0, m) for m in range(KD)] + jobs
        bias = not causal and w["bq"] is not None
        after_rnn = bias
        back, xup = g.sem(f"p{n}_back"), g.sem(f"p{n}_xup")

        def width(job):
            return CH if job[0] == "x" else B * M2

        with nc.Block() as block:
            @block.sync
            def _(sp):
                if causal:
                    xv = w["x"].rearrange("(t p) d -> p t d", p=P)
                    sp.dma_start(g.x[:, 0:TC, :], xv[:, 0:TC, :]).then_inc(x_in[0], 16)
                    sp.dma_start(wqkv[:], w["wqkv"].rearrange("(k p) n -> p k n", p=P)).then_inc(w_in, 16)
                    for c in range(1, NC):
                        sp.dma_start(g.x[:, TC * c:TC * c + TC, :], xv[:, TC * c:TC * c + TC, :]).then_inc(x_in[c], 16)
                else:
                    sp.dma_start(cT[:], w["ctxT"].rearrange("(k p) n -> p k n", p=CK)).then_inc(w_in, 16)
                    sp.dma_start(wk[:], w["wk"].rearrange("(k p) n -> p k n", p=CK)).then_inc(w_in, 16)
                    sp.dma_start(wv[:], w["wv"].rearrange("(k p) n -> p k n", p=CK)).then_inc(w_in, 16)
                    sp.dma_start(wq[:], w["wq"].rearrange("(k p) n -> p k n", p=P)).then_inc(w_in, 16)
                    if bias:
                        with nc.allow_non_contiguous_dma("256 biases"):
                            sp.dma_start(bq[:], w["bq"].rearrange("(k p) -> p k", p=P)).then_inc(w_in, 16)
                            sp.dma_start(bk[:], w["bk"].rearrange("(k p) -> p k", p=P)).then_inc(w_in, 16)
                        sp.dma_start(bv[:], w["bv"].partition_broadcast(P)).then_inc(w_in, 16)
                for i, job in enumerate(jobs):
                    sp.wait_ge(part3, i + 1)
                    N = width(job)
                    if job[0] == "x":
                        row, scr = (job[2] % KD) * P, (g.q_scr if job[2] < KD else g.k_scr)
                        dst = scr[:, row:row + P, CH * job[1]:CH * job[1] + N]
                    else:
                        dst = g.kc_scr[:, job[2] * P:(job[2] + 1) * P, :]
                    sp.dma_start(dst.rearrange("a p n -> p a n"), parts[:, i % 3, :, 0:N]).then_inc(stored[i % 3], 16)
                for r in range(3):
                    sp.wait_ge(stored[r], 16 * ((len(jobs) - r + 2) // 3))

            n_w = 1 if causal else (7 if bias else 4)

            @block.tensor
            def _(pe):
                pe.wait_ge(w_in, 16 * n_w)
                if after_rnn:
                    for t in range(NT):
                        if t >= 2:
                            pe.wait_ge(xup, t - 1)
                        for k in range(KD):
                            last = pe.transpose((g.b6, g.b7)[t % 2][:, k * P:(k + 1) * P],
                                                g.hist[:, k, t // (NT // B), P * (t % (NT // B)):P * (t % (NT // B)) + P],
                                                g.ident[:])
                        last.then_inc(back, 1)
                    pe.wait_ge(xup, NT)
                for i, job in enumerate(jobs):
                    if job[0] == "x" and job[2] == 0:
                        ln.tensor(pe, job[1])
                        pe.wait_ge(ln.xnT, TC * (job[1] + 1))
                    if i >= 4:
                        pe.wait_ge(left, i - 3)
                    out = banks[i % 4][:, 0:width(job)]
                    if job[0] == "x":
                        c, m = job[1], job[2]
                        wt = wqkv if causal else wq
                        acc(pe, out, [(wt[:, k, m * P:(m + 1) * P], g.xnT[:, k, CH * c:CH * c + CH])
                                      for k in range(KD)]).then_inc(made, 1)
                    else:
                        m = job[2]
                        acc(pe, out, [(wk[:, k, m * P:(m + 1) * P], cT[:, k, :]) for k in range(2)]).then_inc(made, 1)
                    if causal and job[2] == NM - 1:
                        for t in range(TC * job[1], TC * job[1] + TC):
                            if t >= 2:
                                pe.wait_ge(vcopied, t - 1)
                            acc(pe, (g.b6, g.b7)[t % 2][:, 0:D],
                                [(g.xnT[:, k, t * P:(t + 1) * P], wqkv[:, k, 2 * D:3 * D])
                                 for k in range(KD)]).then_inc(vmade, 1)
                    if not causal and i < B:
                        acc(pe, (g.b6, g.b7)[i][0:M2, 0:D], [(cT[:, k, M2 * i:M2 * i + M2], wv[:, k, :])
                                                            for k in range(2)]).then_inc(vmade, 1)

            @block.scalar
            def _(act):
                nv = 0
                for i, job in enumerate(jobs):
                    if job[0] == "x" and job[2] == 0:
                        ln.scalar(act, job[1])
                    N = width(job)
                    act.wait_ge(made, i + 1)
                    if i >= 3:
                        act.wait_ge(stored[i % 3], 16 * (i // 3))
                    out, src = parts[:, i % 3, 0, 0:N], banks[i % 4][:, 0:N]
                    if bias:
                        if i == 0:
                            act.wait_ge(w_in, 16 * n_w)
                        col = job[2]
                        act.activation(out, src, ACT.Identity,
                                       bias=(bq if job[0] == "x" else bk)[:, col:col + 1]).then_inc(part1, 1)
                    else:
                        act.activation(out, src, ACT.Copy).then_inc(part1, 1)
                    if causal and job[2] == NM - 1:
                        for t in range(TC * job[1], TC * job[1] + TC):
                            act.wait_ge(vmade, t + 1)
                            if t == 0:
                                act.wait_ge(ones, 1)
                            act.activation(g.va[:, t, :, 0:DH],
                                           (g.b6, g.b7)[t % 2][:, 0:D].rearrange("p (h d) -> p h d", d=DH),
                                           ACT.Copy).then_inc(vcopied, 1)
                    if not causal and i < B:
                        act.wait_ge(vmade, i + 1)
                        act.wait_ge(ones, 1)
                        act.activation(g.vc[0:M2, i, :, 0:DH],
                                       (g.b6, g.b7)[i][0:M2, 0:D].rearrange("p (h d) -> p h d", d=DH),
                                       ACT.Copy).then_inc(vcopied, 1)

            @block.vector
            def _(v):
                def chunk_ready(c):
                    if causal:
                        v.wait_ge(x_in[c], 16)
                    if after_rnn:
                        for t in range(TC * c, TC * c + TC):
                            v.wait_ge(xup, t + 1)

                def jobs_of(c):
                    for i, job in enumerate(jobs):
                        if (job[1] if job[0] == "x" else -1) != c:
                            continue
                        N = width(job)
                        v.wait_ge(part1, i + 1)
                        if i >= 3:
                            v.wait_ge(part3, i - 2)
                        src, p1, r = banks[i % 4][:, 0:N], parts[:, i % 3, 0, 0:N], rest[:, i % 3, 0:N]
                        if bias:
                            b = (bq if job[0] == "x" else bk)[:, job[2]:job[2] + 1]
                            v.scalar_tensor_tensor(out=r, in0=src, scalar=b, in1=p1, op0=ALU.add,
                                                   op1=ALU.subtract).then_inc(left, 1)
                        else:
                            v.tensor_tensor(r, src, p1, ALU.subtract).then_inc(left, 1)

                if after_rnn:
                    for t in range(NT):
                        v.wait_ge(back, t + 1)
                        v.tensor_tensor(g.x[:, t, :], (g.b6, g.b7)[t % 2][:, 0:D], g.x[:, t, :],
                                        ALU.add).then_inc(xup, 1)
                if bias:
                    v.wait_ge(w_in, 16 * n_w)
                jobs_of(-1)
                if bias:
                    for b in range(B):
                        v.wait_ge(vcopied, B)
                        vb = g.vc[0:M2, b, :, 0:DH]
                        v.tensor_tensor(vb, vb, bv[0:M2, :].rearrange("p (h d) -> p h d", d=DH), ALU.add)
                ln.vector(v, chunk_ready)
                for c in range(NC):
                    jobs_of(c)

            @block.gpsimd
            def _(pool):
                va = g.va[:, :, :, DH:QD] if causal else g.vc[:, :, :, DH:QD]
                pool.memset(va, 1.0).then_inc(ones, 1)
                order = [("n", None)] + [("j", i) for i in range(len(jobs))]
                if not causal:
                    order = [("j", 0), ("j", 1), ("n", None)] + [("j", i) for i in range(2, len(jobs))]
                for what, i in order:
                    if what == "n":
                        ln.gpsimd(pool)
                        continue
                    N = width(jobs[i])
                    r, p2, p3 = rest[:, i % 3, 0:N], parts[:, i % 3, 1, 0:N], parts[:, i % 3, 2, 0:N]
                    pool.wait_ge(left, i + 1)
                    pool.tensor_copy(p2, r).then_inc(part2, 1)
                    pool.wait_ge(part2, i + 1)
                    pool.tensor_tensor(p3, r, p2, ALU.subtract).then_inc(part3, 1)


def attention(g, n, causal, w=None):
    g.stage = f"a{n}_"
    nc = g.nc
    KP = P if causal else M2
    units = [(c, hg) for c in range(NC) for hg in range(NG)]

    def blocks(c):
        return TC * (c % 2) + TC if causal else 1

    first, steps, items_end = [], [], []
    for u, (c, hg) in enumerate(units):
        for qt in range(TC):
            if causal:
                keys = P * (TC * (c % 2) + qt + 1)
                for h in range(HG):
                    for half in range((keys + CH - 1) // CH):
                        first.append((u, qt, h, half, min(CH, keys - CH * half)))
            else:
                first.append((u, qt, None, 0, HG * M2))
        items_end.append(len(first))
        steps += [(u, kb) for kb in range(blocks(c))]
    LAG = 2
    order = []
    by_unit = [[i for i, it in enumerate(first) if it[0] == u] for u in range(len(units))]
    steps_of = [[s for s, st in enumerate(steps) if st[0] == u] for u in range(len(units))]
    turning, later = [], []

    def finishing(u):
        c, hg = units[u]
        return [("norm", u)] + ([("out", t) for t in range(TC * c, TC * c + TC)] if hg == NG - 1 else [])

    for u in range(-LAG, len(units)):
        a = by_unit[u + LAG] if u + LAG < len(units) else []
        b = steps_of[u] if u >= 0 else []
        parts = max(1, len(b))
        for j in range(parts):
            order += [("first", i) for i in a[len(a) * j // parts:len(a) * (j + 1) // parts]]
            order += turning
            turning = []
            if b:
                order.append(("scores", b[j]))
                order += later[:1] if causal else later
                later = later[1:] if causal else []
                if b[j]:
                    order.append(("values", b[j] - 1))
                    if steps[b[j] - 1][0] != u:
                        later += finishing(u - 1)
        if a:
            order.append(("max", u + LAG))
            turning = [("turn", u + LAG)]
    order.append(("values", len(steps) - 1))
    order += later + finishing(len(units) - 1)

    with ExitStack() as ctx:
        ks = g.sb("ks", [P, 2, H, S] if causal else [P, H, B, M2], BF16, ctx=ctx)
        qs = g.sb("qs", [P, 2, H, CH], BF16, ctx=ctx)
        mxp = g.sb("mxp", [P, 2, TC, HG, 2], ctx=ctx)
        nm = g.sb("nm", [P, 2, TC, HG], ctx=ctx)
        m1 = g.sb("m1", [HG, 2, 3, CH], BF16, ctx=ctx)
        mr = g.sb("mr", [HG, 2, CH], ctx=ctx)
        pr = g.sb("pr", [P, 4, 2, CH], ctx=ctx)
        osb = g.sb("osb", [P, 2, CH], ctx=ctx)
        rec = g.sb("rec", [P, 2, CH], ctx=ctx)
        on = g.sb("on", [P, NG, 2, CH], ctx=ctx)
        wo = g.sb("wo", [P, NG, D], ctx=ctx)
        va = g.va if causal else g.vc
        names = ("s1", "max", "nm", "nmT", "n1", "nr", "n2", "n3", "s2", "exp", "pv", "o", "oev", "d", "rec", "on",
                 "wo_in", "y", "xup", "rows", "kmul", "bo_in", "xbo")
        s = {k: g.sem(f"a{n}_{k}") for k in names}
        k_in = [g.sem(f"a{n}_k_in{b}") for b in range(B if causal else 1)]
        q_in = [g.sem(f"a{n}_q_in{r}") for r in range(2)]
        m_in = [g.sem(f"a{n}_m_in{r}") for r in range(2)]
        masked = not causal and w["mask"] is not None
        bias_o = not causal and w["bo"] is not None
        if masked:
            mrow8 = g.sb("mrow8", [P, B * M2], U8, ctx=ctx)
            mrow = g.sb("mrow", [P, B * M2], ctx=ctx)
            mneg = g.sb("mneg", [P, B * M2], ctx=ctx)
        if bias_o:
            bo = g.sb("bo", [P, D], ctx=ctx)
        n_k = len(COMBOS) * 16

        def kslice(c, h, lo, width, rows):
            if causal:
                return ks[0:rows, c // 2, h, lo:lo + width]
            return ks[0:rows, h, c // 2, lo:lo + width]

        def keys_ready(eng, c):
            if causal:
                eng.wait_ge(k_in[c // 2], n_k)
            elif masked:
                eng.wait_ge(s["kmul"], 1)
            else:
                eng.wait_ge(k_in[0], n_k)
            eng.wait_ge(s["rows"], 3)

        b7 = []
        for what, i in order:
            if what == "turn":
                b7.append(("m", i))
            if what == "norm":
                b7.append(("d", i))
            if what == "out":
                b7.append(("y", i))

        def wait_b7(pe, user):
            at = b7.index(user)
            if at:
                kind, u = b7[at - 1]
                pe.wait_ge(s[{"m": "nr", "d": "rec", "y": "xup"}[kind]], u + 1)

        def ends_unit(i):
            return i + 1 == len(steps) or steps[i + 1][0] != steps[i][0]

        with nc.Block() as block:
            @block.sync
            def _(sp):
                if masked:
                    sp.dma_start(mrow8[:], w["mask"].partition_broadcast(P)).then_inc(s["bo_in"], 16)
                if bias_o:
                    sp.dma_start(bo[:], w["bo"].partition_broadcast(P)).then_inc(s["bo_in"], 16)

                def load_q(c):
                    if c >= 2:
                        sp.wait_ge(s["pv"], 2 * (max(steps_of[NG * (c - 2) + NG - 1]) + 1))
                    for r, (qp, _) in enumerate(COMBOS):
                        sp.dma_start(qs[DH * r:DH * r + DH, c % 2, :, :],
                                     g.q_scr[qp, :, CH * c:CH * c + CH].rearrange("(h d) t -> d h t", d=DH)
                                     ).then_inc(q_in[c % 2], 16)

                def load_k(b):
                    for r, (_, kp) in enumerate(COMBOS):
                        if causal:
                            sp.dma_start(ks[DH * r:DH * r + DH, b, :, :],
                                         g.k_scr[kp, :, S * b:S * b + S].rearrange("(h d) t -> d h t", d=DH)
                                         ).then_inc(k_in[b], 16)
                        else:
                            sp.dma_start(ks[DH * r:DH * r + DH, :, :, :].rearrange("p h b t -> p h (b t)"),
                                         g.kc_scr[kp, :, :].rearrange("(h d) t -> d h t", d=DH)
                                         ).then_inc(k_in[0], 16)

                load_q(0)
                load_k(0)
                load_q(1)
                if causal:
                    load_k(1)
                sp.dma_start(wo[:], g.wo_dram[n].rearrange("(g p) n -> p g n", p=P)).then_inc(s["wo_in"], 16)
                for what, i in order:
                    if what == "turn":
                        sp.wait_ge(s["n3"], i + 1)
                        sp.wait_ge(s["n2"], i + 1)
                        c, hg = units[i]
                        for k in range(3):
                            sp.dma_start(qs[R_MAX + k:R_MAX + k + 1, c % 2, HG * hg:HG * hg + HG, :],
                                         m1[:, i % 2, k, :]).then_inc(m_in[i % 2], 16)
                    if what == "values" and ends_unit(i) and steps[i][0] % NG == NG - 1:
                        c = units[steps[i][0]][0]
                        if c + 2 < NC:
                            load_q(c + 2)

            @block.gpsimd
            def _(pool):
                pool.memset(ks[R_MASK:R_ALL].rearrange("p a b c -> p (a b c)"), 1.0).then_inc(s["rows"], 1)
                pool.memset(qs[R_MASK:R_ALL].rearrange("p a b c -> p (a b c)"), 1.0).then_inc(s["rows"], 1)
                pool.wait_ge(s["rows"], 2)
                if masked:
                    pool.wait_ge(s["bo_in"], 16 * (1 + bias_o))
                    pool.tensor_copy(mrow[:], mrow8[:]).then_inc(s["xbo"], 1)
                    pool.wait_ge(s["xbo"], 1)
                    pool.tensor_scalar(mneg[:], mrow[:], 1.0, BIG, ALU.subtract, ALU.mult).then_inc(s["xbo"], 1)
                    pool.wait_ge(s["xbo"], 2)
                    pool.tensor_copy(ks[R_MASK:R_MAX].rearrange("p h b t -> p h (b t)"),
                                     mneg[R_MASK:R_MAX, :].unsqueeze(1).broadcast_to([1, H, B * M2])
                                     ).then_inc(s["rows"], 1)
                else:
                    pool.memset(ks[R_MASK:R_MASK + 1].rearrange("p a b c -> p (a b c)"), 0.0).then_inc(s["rows"], 1)
                if bias_o:
                    pool.wait_ge(s["bo_in"], 16 * (1 + masked))
                    pool.wait_ge(s["rows"], 3)
                    for t in range(NT):
                        pool.tensor_tensor(g.x[:, t, :], g.x[:, t, :], bo[:], ALU.add).then_inc(s["xbo"], 1)
                for what, u in order:
                    if what == "turn":
                        pool.wait_ge(s["nr"], u + 1)
                        if u >= 2:
                            pool.wait_ge(m_in[u % 2], 48 * (u // 2))
                        pool.tensor_copy(m1[:, u % 2, 1, :], mr[:, u % 2, :]).then_inc(s["n2"], 1)
                        pool.wait_ge(s["n2"], u + 1)
                        pool.tensor_tensor(m1[:, u % 2, 2, :], mr[:, u % 2, :], m1[:, u % 2, 1, :],
                                           ALU.subtract).then_inc(s["n3"], 1)

            @block.tensor
            def _(pe):
                def first_pass(i):
                    u, qt, h, half, N = first[i]
                    c, hg = units[u]
                    bank = (g.b4, g.b5)[i % 2]
                    if u % NG == 0 and qt == 0 and not h and half == 0:
                        pe.wait_ge(q_in[c % 2], n_k * (c // 2 + 1))
                        keys_ready(pe, c)
                    if i >= 2:
                        pe.wait_ge(s["max"], i - 1)
                    if causal:
                        hh = HG * hg + h
                        diag = CH * half + N == P * (TC * (c % 2) + qt + 1)
                        last = pe.matmul(bank[:, 0:N], qs[0:R_MASK, c % 2, hh, P * qt:P * qt + P],
                                         kslice(c, hh, CH * half, N, R_MASK), start=True, stop=not diag)
                        if diag:
                            last = pe.matmul(bank[:, N - P:N], g.identb[:], g.mask_qk[:], start=False, stop=True)
                    else:
                        for h in range(HG):
                            hh = HG * hg + h
                            last = pe.matmul(bank[:, M2 * h:M2 * h + M2], qs[0:R_MAX, c % 2, hh, P * qt:P * qt + P],
                                             kslice(c, hh, 0, M2, R_MAX), start=True, stop=True)
                    last.then_inc(s["s1"], 1)

                def turn_max(u):
                    if causal:
                        pe.wait_ge(s["nm"], u + 1)
                    else:
                        pe.wait_ge(s["max"], items_end[u])
                    wait_b7(pe, ("m", u))
                    for qt in range(TC):
                        last = pe.transpose(g.b7[0:HG, P * qt:P * qt + P], nm[:, u % 2, qt, :], g.ident[:])
                    last.then_inc(s["nmT"], 1)

                def scores(i):
                    u, kb = steps[i]
                    c, hg = units[u]
                    if kb == 0:
                        pe.wait_ge(m_in[u % 2], 48 * (u // 2 + 1))
                    d = kb - TC * (c % 2) if causal else -1
                    off = P * max(d, 0)
                    for a in range(2):
                        k = 2 * i + a
                        if k >= 2:
                            pe.wait_ge(s["exp"], k - 1)
                        big = (g.big0, g.big1)[k % 2]
                        for e in range(2):
                            hh = HG * hg + 2 * a + e
                            last = pe.matmul(big[0:KP, e, off:CH], kslice(c, hh, P * kb, KP, R_ALL),
                                             qs[0:R_ALL, c % 2, hh, off:CH], start=True, stop=d < 0)
                            if d >= 0:
                                last = pe.matmul(big[:, e, off:off + P], g.identb[:], g.mask_kq[:],
                                                 start=False, stop=True)
                        last.then_inc(s["s2"], 1)

                def values(i):
                    u, kb = steps[i]
                    c, hg = units[u]
                    off = P * max(kb - TC * (c % 2), 0) if causal else 0
                    tile = TC * 2 * (c // 2) + kb if causal else c // 2
                    if kb == 0 and u:
                        pe.wait_ge(s["oev"], u)
                    pe.wait_ge(s["exp"], 2 * i + 2)
                    for h in range(HG):
                        k = 2 * i + h // 2
                        last = pe.matmul(g.b6[QD * h:QD * h + QD, off:CH], va[0:KP, tile, HG * hg + h, :],
                                         pr[0:KP, k % 4, h % 2, off:CH], start=(kb == 0), stop=ends_unit(i),
                                         tile_position=(0, QD * h))
                        if h % 2:
                            last.then_inc(s["pv"], 1)

                def spread_sums(u):
                    pe.wait_ge(s["oev"], u + 1)
                    wait_b7(pe, ("d", u))
                    pe.matmul(g.b7[:], g.sel_sum[:], osb[:, u % 2, :], start=True, stop=True).then_inc(s["d"], 1)

                def output(t):
                    if t == 0:
                        pe.wait_ge(s["wo_in"], 16)
                    pe.wait_ge(s["on"], NG * (t // TC + 1))
                    wait_b7(pe, ("y", t))
                    cols = slice(P * (t % TC), P * (t % TC) + P)
                    acc(pe, g.b7[:, 0:D], [(on[:, k, t // TC % 2, cols], wo[:, k, :])
                                           for k in range(NG)]).then_inc(s["y"], 1)

                for what, i in order:
                    if what == "first":
                        first_pass(i)
                    if what == "turn":
                        turn_max(i)
                    if what == "scores":
                        scores(i)
                    if what == "values":
                        values(i)
                    if what == "norm":
                        spread_sums(i)
                    if what == "out":
                        output(i)

            @block.scalar
            def _(act):
                for what, i in order:
                    if what == "scores":
                        u, kb = steps[i]
                        off = P * max(kb - TC * (units[u][0] % 2), 0) if causal else 0
                        for k in (2 * i, 2 * i + 1):
                            act.wait_ge(s["s2"], k + 1)
                            if k >= 4:
                                act.wait_ge(s["pv"], k - 3)
                            act.activation(pr[0:KP, k % 4, :, off:CH], (g.big0, g.big1)[k % 2][0:KP, :, off:CH],
                                           ACT.Exp, scale=SCALE).then_inc(s["exp"], 1)
                    if what == "values" and ends_unit(i):
                        u = steps[i][0]
                        act.wait_ge(s["pv"], 2 * i + 2)
                        if u >= 2:
                            act.wait_ge(s["on"], u - 1)
                        act.activation(osb[:, u % 2, :], g.b6[:], ACT.Copy).then_inc(s["oev"], 1)
                    if what == "turn":
                        act.wait_ge(s["nmT"], i + 1)
                        if i >= 2:
                            act.wait_ge(m_in[i % 2], 48 * (i // 2))
                        act.activation(m1[:, i % 2, 0, :], g.b7[0:HG, :], ACT.Copy).then_inc(s["n1"], 1)

            @block.vector
            def _(v):
                if masked:
                    v.wait_ge(k_in[0], n_k)
                    v.wait_ge(s["xbo"], 1)
                    kk = ks[0:R_MASK].rearrange("p h b t -> p h (b t)")
                    v.tensor_tensor(kk, kk, mrow[0:R_MASK, :].unsqueeze(1).broadcast_to([R_MASK, H, B * M2]),
                                    ALU.mult).then_inc(s["kmul"], 1)
                for what, i in order:
                    if what == "first":
                        u, qt, h, half, N = first[i]
                        bank = (g.b4, g.b5)[i % 2]
                        v.wait_ge(s["s1"], i + 1)
                        if causal:
                            v.tensor_reduce(mxp[:, u % 2, qt, h, half:half + 1], bank[:, 0:N], AX.X,
                                            ALU.max).then_inc(s["max"], 1)
                        else:
                            if qt == 0 and u >= 2:
                                v.wait_ge(s["nmT"], u - 1)
                            v.tensor_reduce(nm[:, u % 2, qt, :], bank[:, 0:N].rearrange("p (h t) -> p h t", h=HG),
                                            AX.X, ALU.max, negate=True).then_inc(s["max"], 1)
                    if what == "max" and causal:
                        v.wait_ge(s["max"], items_end[i])
                        if i >= 2:
                            v.wait_ge(s["nmT"], i - 1)
                        hh = 1 + units[i][0] % 2
                        v.tensor_reduce(nm[:, i % 2, :, :], mxp[:, i % 2, :, :, 0:hh], AX.X, ALU.max,
                                        negate=True).then_inc(s["nm"], 1)
                    if what == "turn":
                        v.wait_ge(s["n1"], i + 1)
                        if i >= 2:
                            v.wait_ge(s["n3"], i - 1)
                        v.tensor_tensor(mr[:, i % 2, :], g.b7[0:HG, :], m1[:, i % 2, 0, :],
                                        ALU.subtract).then_inc(s["nr"], 1)
                    if what == "norm":
                        u = i
                        c, hg = units[u]
                        v.wait_ge(s["d"], u + 1)
                        v.reciprocal(rec[:, u % 2, :], g.b7[:]).then_inc(s["rec"], 1)
                        v.wait_ge(s["rec"], u + 1)
                        if c >= 2:
                            v.wait_ge(s["y"], TC * (c - 1))
                        v.tensor_tensor(on[:, hg, c % 2, :], osb[:, u % 2, :], rec[:, u % 2, :],
                                        ALU.mult).then_inc(s["on"], 1)
                    if what == "out":
                        if bias_o and i == 0:
                            v.wait_ge(s["xbo"], 2 * masked + NT)
                        v.wait_ge(s["y"], i + 1)
                        v.tensor_tensor(g.x[:, i, :], g.b7[:, 0:D], g.x[:, i, :], ALU.add).then_inc(s["xup"], 1)


def rank_select(v, step, gates, tie, sel, cmp, eq, e, top):
    n = gates.shape[1]
    gj = gates.unsqueeze(2).broadcast_to([P, n, e, e])
    ge = gates.unsqueeze(3).broadcast_to([P, n, e, e])
    step(v.tensor_tensor(cmp, gj, ge, ALU.is_gt))
    step(v.tensor_tensor(eq, gj, ge, ALU.is_equal))
    step(v.tensor_tensor(eq, eq, tie.unsqueeze(1).broadcast_to([P, n, e, e]), ALU.mult))
    step(v.tensor_tensor(cmp, cmp, eq, ALU.add))
    step(v.tensor_reduce(sel, cmp, AX.X, ALU.add))
    return v.tensor_scalar(sel, sel, float(top), None, ALU.is_lt)


def linear_experts(g, n, w):
    g.stage = f"f{n}_"
    nc = g.nc
    with ExitStack() as ctx:
        norm_buffers(g, ctx)
        wg = g.sb("wg", [P, KD, E0], ctx=ctx)
        we = g.sb("we", [P, KD, E0 * D], ctx=ctx)
        be = g.sb("be", [E0, D], ctx=ctx)
        bg = g.sb("bg", [P, E0], ctx=ctx)
        gate = g.sb("gate", [P, TC, E0], ctx=ctx)
        sel = g.sb("sel", [P, TC, E0], ctx=ctx)
        top = g.sb("top", [P, TC], ctx=ctx)
        cmp = g.sb("cmp", [P, TC, E0, E0], ctx=ctx)
        eq = g.sb("eq", [P, TC, E0, E0], ctx=ctx)
        wts = g.sb("wts", [P, NT, E0], ctx=ctx)
        wtsT = g.sb("wtsT", [E0, 2, CH], ctx=ctx)
        ln = Norm(g, n)
        w_in, w_in2, gmade, chain, gexp, shifted, wready, wT, wTc, ymade, yused, xup = (g.sem(f"f{n}_{k}") for k in (
            "w_in", "w_in2", "gmade", "chain", "gexp", "shifted", "wready", "wT", "wTc", "ymade", "yused", "xup"))
        ybank = [g.big0[:, 0, :], g.big0[:, 1, :], g.big1[:, 0, :], g.big1[:, 1, :]]
        NE = E0 // 2
        with nc.Block() as block:
            @block.sync
            def _(sp):
                sp.dma_start(wg[:], w["Wg"].rearrange("(k p) e -> p k e", p=P)).then_inc(w_in, 16)
                sp.dma_start(bg[:], w["bg"].partition_broadcast(P)).then_inc(w_in, 16)
                sp.dma_start(be[:], w["be"]).then_inc(w_in, 16)
                for k in range(KD):
                    sp.dma_start(we[:, k, :].rearrange("p (e o) -> p e o", e=E0),
                                 w["We"][:, k * P:(k + 1) * P, :].rearrange("e p o -> p e o")).then_inc(w_in2, 16)

            @block.tensor
            def _(pe):
                pe.wait_ge(w_in, 48)
                for c in range(NC):
                    ln.tensor(pe, c)
                    pe.wait_ge(ln.xnT, TC * (c + 1))
                    if c:
                        pe.wait_ge(wTc, c)
                    for t in range(TC * c, TC * c + TC):
                        last = acc(pe, g.b6[:, E0 * (t % TC):E0 * (t % TC) + E0],
                                   [(g.xnT[:, k, t * P:(t + 1) * P], wg[:, k, :]) for k in range(KD)])
                    last.then_inc(gmade, 1)
                    if c == 0:
                        pe.wait_ge(w_in2, 32)
                    for t in range(TC * c, TC * c + TC):
                        for j in range(NE):
                            i = NE * t + j
                            if i >= NE:
                                pe.wait_ge(yused, i - NE + 1)
                            acc(pe, ybank[j], [(g.xnT[:, k, t * P:(t + 1) * P], we[:, k, 512 * j:512 * j + 512])
                                               for k in range(KD)]).then_inc(ymade, 1)
                        if t % TC == 0:
                            pe.wait_ge(wready, c + 1)
                            for q in range(TC):
                                last = pe.transpose(g.b6[0:E0, P * q:P * q + P], wts[:, TC * c + q, :], g.ident[:])
                            last.then_inc(wT, 1)
                            pe.wait_ge(wTc, c + 1)
                        if t:
                            pe.wait_ge(xup, t)
                        pe.matmul(g.b7[:, 0:D], wtsT[:, c % 2, P * (t % TC):P * (t % TC) + P], be[:],
                                  start=True, stop=True).then_inc(ymade, 1)

            @block.scalar
            def _(act):
                for c in range(NC):
                    ln.scalar(act, c)
                    act.wait_ge(shifted, c + 1)
                    act.activation(gate[:], gate[:], ACT.Exp).then_inc(gexp, 1)
                    act.wait_ge(wT, c + 1)
                    act.activation(wtsT[:, c % 2, :], g.b6[0:E0, :], ACT.Copy).then_inc(wTc, 1)

            @block.gpsimd
            def _(pool):
                ln.gpsimd(pool)

            @block.vector
            def _(v):
                count = [0]

                def step(ins):
                    count[0] += 1
                    ins.then_inc(chain, 1)
                    v.wait_ge(chain, count[0])

                ln.vector(v, lambda c: None)
                v.wait_ge(w_in, 48)
                for c in range(NC):
                    v.wait_ge(gmade, c + 1)
                    step(v.tensor_tensor(gate[:], g.b6[:, 0:TC * E0].rearrange("p (t e) -> p t e", e=E0),
                                         bg[:].unsqueeze(1).broadcast_to([P, TC, E0]), ALU.add))
                    step(v.tensor_reduce(top[:], gate[:], AX.X, ALU.max))
                    step(rank_select(v, step, gate[:], g.tie8[:], sel[:], cmp[:], eq[:], E0, TOP0))
                    v.tensor_tensor(gate[:], gate[:], top[:].unsqueeze(2).broadcast_to([P, TC, E0]),
                                    ALU.subtract).then_inc(shifted, 1)
                    v.wait_ge(gexp, c + 1)
                    step(v.tensor_tensor(gate[:], gate[:], sel[:], ALU.mult))
                    step(v.tensor_reduce(top[:], gate[:], AX.X, ALU.add))
                    step(v.reciprocal(top[:], top[:]))
                    v.tensor_tensor(wts[:, TC * c:TC * c + TC, :], gate[:],
                                    top[:].unsqueeze(2).broadcast_to([P, TC, E0]), ALU.mult).then_inc(wready, 1)
                    v.wait_ge(wready, c + 1)
                    for t in range(TC * c, TC * c + TC):
                        for e in range(E0):
                            j = e // 2
                            if e % 2 == 0:
                                v.wait_ge(ymade, (NE + 1) * t + j + 1)
                            ins = v.scalar_tensor_tensor(
                                out=g.x[:, t, :], in0=ybank[j][:, D * (e % 2):D * (e % 2) + D],
                                scalar=wts[:, t, e:e + 1], in1=g.x[:, t, :], op0=ALU.mult, op1=ALU.add)
                            if e % 2:
                                ins.then_inc(yused, 1)
                                v.wait_ge(yused, NE * t + j + 1)
                            else:
                                step(ins)
                        v.wait_ge(ymade, (NE + 1) * (t + 1))
                        v.tensor_tensor(g.x[:, t, :], g.b7[:, 0:D], g.x[:, t, :], ALU.add).then_inc(xup, 1)


U = 32


def recurrence(g, n, w):
    g.stage = f"r{n}_"
    nc = g.nc
    with ExitStack() as ctx:
        norm_buffers(g, ctx, pad=True)
        wi = g.sb("wi", [P, KD, D], ctx=ctx)
        wh = g.sb("wh", [P, KD, D], ctx=ctx)
        whr = g.sb("whr", [P, KD, D], ctx=ctx)
        whp = g.sb("whp", [P, 3, KD, D], BF16, ctx=ctx)
        bb = g.sb("bb", [1, 3, D], ctx=ctx)
        bbp = g.sb("bbp", [1, 3, D], BF16, ctx=ctx)
        one = g.sb("one", [1, B * U], BF16, ctx=ctx)
        hr = g.sb("hr", [P, 2, KD, B, U], ctx=ctx)
        rem = g.sb("rem", [P, 2, 2, KD, B], ctx=ctx)
        ln = Norm(g, n)
        w_in, wprep, pre, h_ready, r1_ready, r2_ready, summed, copied = (g.sem(f"r{n}_{k}") for k in (
            "w_in", "wprep", "pre", "h_ready", "r1_ready", "r2_ready", "summed", "copied"))
        hr_hi = hr[:].rearrange("p s k b t -> p (s k b t)").bitcast(BF16).rearrange(
            "p (s k b t two) -> p s k b t two", s=2, k=KD, b=B, two=2)
        rem_hi = rem[:].rearrange("p s r k b -> p (s r k b)").bitcast(BF16).rearrange(
            "p (s r k b two) -> p s r k b two", s=2, r=2, k=KD, two=2)
        bank = [g.big0[:, 0, 0:KD * B * U].rearrange("p (m b t) -> p m b t", m=KD, b=B),
                g.big1[:, 0, 0:KD * B * U].rearrange("p (m b t) -> p m b t", m=KD, b=B)]

        def prev(half, t):
            return (half, t - 1) if t else (1 - half, U - 1)

        with nc.Block() as block:
            @block.sync
            def _(sp):
                sp.dma_start(wh[:], w["WhT"].rearrange("(k p) n -> p k n", p=P)).then_inc(w_in, 16)
                sp.dma_start(bb[:, 0, :], w["bi"].rearrange("(a n) -> a n", a=1)).then_inc(w_in, 16)
                sp.dma_start(bb[:, 1, :], w["bh"].rearrange("(a n) -> a n", a=1)).then_inc(w_in, 16)
                sp.dma_start(wi[:], w["WiT"].rearrange("(k p) n -> p k n", p=P)).then_inc(w_in, 16)

            @block.tensor
            def _(pe):
                for c in range(NC):
                    ln.tensor(pe, c)
                pe.wait_ge(ln.xnT, NT)
                pe.wait_ge(wprep, 9)
                pe.wait_ge(pre, 2)

                def inputs(half, t0, piece):
                    if piece < 4:
                        m, k = piece // 2, piece % 2
                        x = g.xnT_flat[:, bass.ds(t0 + k * B * S, B * S)].rearrange(
                            "p (b t) -> p b t", b=B)[:, :, 0:U]
                        pe.matmul(bank[half][:, m], wi[:, k, m * P:(m + 1) * P], x, start=(piece == 0),
                                  stop=True, skip_group_check=True)
                    else:
                        m = piece - 4
                        for q in range(3):
                            pe.matmul(bank[half][:, m], bbp[:, q, m * P:(m + 1) * P],
                                      one[:].rearrange("p (b t) -> p b t", b=B), start=False, stop=True,
                                      skip_group_check=True)

                for piece in range(6):
                    inputs(0, 0, piece)
                with pe.Fori(0, S // (2 * U)) as it:
                    for half in range(2):
                        for t in range(U):
                            at = it * (2 * U) + (half * U + t + 1)
                            hp, tp = prev(half, t)
                            par = (t + 1) % 2
                            for q, ready in enumerate((h_ready, r1_ready, r2_ready)):
                                pe.wait_ge(ready, at)
                                for k in range(KD):
                                    h = hr_hi[:, hp, k, :, tp, 1] if q == 0 else rem_hi[:, par, q - 1, k, :, 1]
                                    for m in range(KD):
                                        for a in range(3 - q):
                                            last = pe.matmul(bank[half][:, m, :, t],
                                                             whp[:, a, k, m * P:(m + 1) * P], h,
                                                             start=False, stop=True, skip_group_check=True)
                            last.then_inc(summed, 1)
                            if 4 <= t < 28 and t % 4 == 0:
                                inputs(1 - half, it * (2 * U) + (half + 1) * U, t // 4 - 1)

            @block.scalar
            def _(act):
                for c in range(NC):
                    ln.scalar(act, c)
                act.wait_ge(w_in, 64)
                act.activation(whp[:, 0], wh[:], ACT.Copy).then_inc(wprep, 1)
                with act.Fori(0, S // (2 * U)) as it:
                    for half in range(2):
                        act.wait_ge(copied, it * 2 + (half + 1))
                        for t in range(U):
                            act.wait_ge(summed, it * (2 * U) + (half * U + t + 1))
                            act.activation(hr[:, half, :, :, t], bank[half][:, :, :, t], ACT.Tanh).then_inc(h_ready, 1)

            @block.vector
            def _(v):
                ln.vector(v, lambda c: None)
                v.wait_ge(w_in, 64)
                v.wait_ge(wprep, 1)
                steps = 1

                def step(ins):
                    nonlocal steps
                    steps += 1
                    ins.then_inc(wprep, 1)
                    v.wait_ge(wprep, steps)

                step(v.tensor_tensor(whr[:], wh[:], whp[:, 0], ALU.subtract))
                step(v.tensor_copy(whp[:, 1], whr[:]))
                step(v.tensor_tensor(whp[:, 2], whr[:], whp[:, 1], ALU.subtract))
                step(v.tensor_tensor(bb[:, 2, :], bb[:, 0, :], bb[:, 1, :], ALU.add))
                step(v.tensor_copy(bbp[:, 0, :], bb[:, 2, :]))
                step(v.tensor_tensor(bb[:, 0, :], bb[:, 2, :], bbp[:, 0, :], ALU.subtract))
                step(v.tensor_copy(bbp[:, 1, :], bb[:, 0, :]))
                step(v.tensor_tensor(bbp[:, 2, :], bb[:, 0, :], bbp[:, 1, :], ALU.subtract))
                with v.Fori(0, S // (2 * U)) as it:
                    for half in range(2):
                        for t in range(U):
                            at = it * (2 * U) + (half * U + t + 2)
                            par = t % 2
                            v.wait_ge(h_ready, at)
                            v.tensor_tensor(rem[:, par, 0], hr[:, half, :, :, t], hr_hi[:, half, :, :, t, 1],
                                            ALU.subtract).then_inc(r1_ready, 1)
                            v.wait_ge(r1_ready, at)
                            v.tensor_tensor(rem[:, par, 1], rem[:, par, 0], rem_hi[:, par, 0, :, :, 1],
                                            ALU.subtract).then_inc(r2_ready, 1)

            @block.gpsimd
            def _(pool):
                ln.gpsimd(pool)
                pool.memset(one[:], 1.0).then_inc(pre, 1)
                pool.memset(g.xnT_flat[:, KD * B * S:KD * B * S + S], 0.0).then_inc(pre, 1)
                pool.memset(hr[:], 0.0).then_inc(h_ready, 1)
                pool.memset(rem[:, :, 0], 0.0).then_inc(r1_ready, 1)
                pool.memset(rem[:, :, 1], 0.0).then_inc(r2_ready, 1)
                pool.memset(g.hist[:, 0, 0, 0:U], 0.0).then_inc(copied, 1)
                pool.memset(g.hist[:, 0, 0, U:2 * U], 0.0).then_inc(copied, 1)
                pool.wait_ge(copied, 2)
                with pool.Fori(0, S // (2 * U)) as it:
                    for half in range(2):
                        pool.wait_ge(h_ready, it * (2 * U) + ((half + 1) * U + 1))
                        t0 = it * (2 * U) + half * U
                        pool.tensor_copy(g.hist[:, :, :, bass.ds(t0, U)], hr[:, half]).then_inc(copied, 1)


def gated_experts(g, n, w, out):
    g.stage = f"e{n}_"
    nc = g.nc
    with ExitStack() as ctx:
        norm_buffers(g, ctx)
        wr = g.sb("wr", [P, KD, E1], ctx=ctx)
        wg = g.sb("wgate", [P, KD, HID], ctx=ctx)
        wu = g.sb("wup", [P, KD, HID], ctx=ctx)
        wd = g.sb("wdown", [P, MH, D], ctx=ctx)
        cb = g.sb("cb", [P, E1], ctx=ctx)
        sc = g.sb("sc", [P, TC, E1], ctx=ctx)
        sb = g.sb("sb", [P, TC, E1], ctx=ctx)
        prs = g.sb("prs", [P, TC, G1, 6], ctx=ctx)
        gs = g.sb("gs", [P, TC, G1], ctx=ctx)
        gm = g.sb("gm", [P, TC, G1], ctx=ctx)
        gmn = g.sb("gmn", [P, TC, G1], ctx=ctx)
        gc = g.sb("gc", [P, TC, G1, G1], ctx=ctx)
        ge = g.sb("ge", [P, TC, G1, G1], ctx=ctx)
        cmp = g.sb("cmp1", [P, TC, E1, E1], ctx=ctx)
        eq = g.sb("eq1", [P, TC, E1, E1], ctx=ctx)
        sel = g.sb("sel1", [P, TC, E1], ctx=ctx)
        tot = g.sb("tot", [P, TC], ctx=ctx)
        comb = g.sb("comb", [P, 2, TC, E1], ctx=ctx)
        cp1 = g.sb("cp1", [E1, CH], BF16, ctx=ctx)
        cr = g.sb("cr", [E1, CH], ctx=ctx)
        cp2 = g.sb("cp2", [E1, CH], BF16, ctx=ctx)
        cps = g.sb("cps", [P, 2, CH], BF16, ctx=ctx)
        sg = g.sb("sg", [P, 2, CH], ctx=ctx)
        hT = g.sb("hT", [P, 2, MH, CH], ctx=ctx)
        ln = Norm(g, n)
        (w_in, w_in2, logits, scored, chain, combed, cT, c1, parted, gmade, umade, bmade, sgd, hmul, hready, ymade,
         xup, stored, zero) = (g.sem(f"e{n}_{k}") for k in (
             "w_in", "w_in2", "logits", "scored", "chain", "combed", "cT", "c1", "parted", "gmade", "umade", "bmade",
             "sgd", "hmul", "hready", "ymade", "xup", "stored", "zero"))
        NR = MH - MS
        KR = 2 * QD + E1
        with nc.Block() as block:
            @block.sync
            def _(sp):
                sp.dma_start(wr[:], w["router"].rearrange("(k p) e -> p k e", p=P)).then_inc(w_in, 16)
                sp.dma_start(cb[:], w["cbias"].partition_broadcast(P)).then_inc(w_in, 16)
                sp.dma_start(wg[:], w["gate"].rearrange("(k p) n -> p k n", p=P)).then_inc(w_in, 16)
                sp.dma_start(wu[:], w["up"].rearrange("(k p) n -> p k n", p=P)).then_inc(w_in, 16)
                sp.dma_start(wd[:], w["down"].rearrange("(m p) n -> p m n", p=P)).then_inc(w_in2, 16)
                ov = out.rearrange("(t p) d -> p t d", p=P)
                for c in range(NC):
                    sp.wait_ge(xup, TC * (c + 1))
                    sp.dma_start(ov[:, TC * c:TC * c + TC, :], g.x[:, TC * c:TC * c + TC, :]).then_inc(stored, 16)
                sp.wait_ge(stored, 16 * NC)

            @block.tensor
            def _(pe):
                pe.wait_ge(w_in, 64)
                for c in range(NC):
                    ln.tensor(pe, c)
                pe.wait_ge(ln.xnT, NT)

                def route(c):
                    if c:
                        pe.wait_ge(parted, 2 * c)
                    for t in range(TC):
                        last = acc(pe, g.b7[:, E1 * t:E1 * t + E1],
                                   [(g.xnT[:, k, CH * c + P * t:CH * c + P * t + P], wr[:, k, :]) for k in range(KD)])
                    last.then_inc(logits, 1)

                def turn(c):
                    pe.wait_ge(combed, c + 1)
                    for t in range(TC):
                        last = pe.transpose(g.b7[0:E1, P * t:P * t + P], comb[:, c % 2, t, :], g.ident[:])
                    last.then_inc(cT, 1)

                def down(c):
                    pe.wait_ge(w_in2, 16)
                    pe.wait_ge(hready, MH * (c + 1))
                    for t in range(TC * c, TC * c + TC):
                        if t >= 2:
                            pe.wait_ge(xup, t - 1)
                        acc(pe, (g.b4, g.b5)[t % 2][:, 0:D],
                            [(hT[:, c % 2, m, P * (t % TC):P * (t % TC) + P], wd[:, m, :])
                             for m in range(MH)]).then_inc(ymade, 1)

                route(0)
                for c in range(NC):
                    for m in range(MH):
                        i = MH * c + m
                        if i >= 2:
                            pe.wait_ge(sgd, i - 1)
                        cols = slice(m * P, (m + 1) * P)
                        acc(pe, g.big0[:, i % 2, :], [(wg[:, k, cols], g.xnT[:, k, CH * c:CH * c + CH])
                                                      for k in range(KD)]).then_inc(gmade, 1)
                        if i >= 2:
                            pe.wait_ge(hmul, i - 1)
                        acc(pe, g.big1[:, i % 2, :], [(wu[:, k, cols], g.xnT[:, k, CH * c:CH * c + CH])
                                                      for k in range(KD)]).then_inc(umade, 1)
                        if m == MS - 1:
                            turn(c)
                        if m >= MS:
                            pe.wait_ge(parted, 2 * (c + 1))
                            j = NR * c + m - MS
                            if j:
                                pe.wait_ge(hready, MH * ((j - 1) // NR) + MS + (j - 1) % NR + 1)
                            pe.matmul(g.b6[:], g.sel_pair[0:KR, m - MS, :], cps[0:KR, c % 2, :],
                                      start=True, stop=True).then_inc(bmade, 1)
                    if c + 1 < NC:
                        route(c + 1)
                    if c:
                        down(c - 1)
                down(NC - 1)

            @block.scalar
            def _(act):
                for c in range(NC):
                    ln.scalar(act, c)

                def scores(c):
                    act.wait_ge(logits, c + 1)
                    if c:
                        act.wait_ge(combed, c)
                    act.activation(sc[:].rearrange("p t e -> p (t e)"), g.b7[:, 0:TC * E1],
                                   ACT.Sigmoid).then_inc(scored, 1)

                scores(0)
                for c in range(NC):
                    for m in range(MH):
                        i = MH * c + m
                        act.wait_ge(gmade, i + 1)
                        if i >= 2:
                            act.wait_ge(hmul, i - 1)
                        act.activation(sg[:, i % 2, :], g.big0[:, i % 2, :], ACT.Silu).then_inc(sgd, 1)
                        if m == MS - 1:
                            act.wait_ge(cT, c + 1)
                            act.activation(cp1[:], g.b7[0:E1, :], ACT.Copy).then_inc(c1, 1)
                    if c + 1 < NC:
                        scores(c + 1)

            @block.gpsimd
            def _(pool):
                pool.memset(cps[:].rearrange("p a n -> p (a n)"), 0.0).then_inc(zero, 1)
                ln.gpsimd(pool)

            @block.vector
            def _(v):
                ln.vector(v, lambda c: None)
                v.wait_ge(w_in, 64)
                v.wait_ge(zero, 1)
                count = [0]

                def step(ins):
                    count[0] += 1
                    ins.then_inc(chain, 1)
                    v.wait_ge(chain, count[0])

                def wide(ap, e):
                    return ap.unsqueeze(3).broadcast_to([P, TC, G1, e])

                def choose(c):
                    v.wait_ge(scored, c + 1)
                    step(v.tensor_tensor(sb[:], sc[:], cb[:].unsqueeze(1).broadcast_to([P, TC, E1]), ALU.add))
                    sg4 = sb[:].rearrange("p t (q e) -> p (t q) e", q=G1)
                    pv = prs[:].rearrange("p t q s -> p (t q) s")
                    step(v.tensor_tensor(pv[:, :, 0:3], sg4[:, :, 0:3], sg4[:, :, 1:4], ALU.add))
                    step(v.tensor_tensor(pv[:, :, 3:5], sg4[:, :, 0:2], sg4[:, :, 2:4], ALU.add))
                    step(v.tensor_tensor(pv[:, :, 5:6], sg4[:, :, 0:1], sg4[:, :, 3:4], ALU.add))
                    step(v.tensor_reduce(gs[:].rearrange("p t q -> p (t q)"), pv, AX.X, ALU.max))
                    step(rank_select(v, step, gs[:], g.tie16[:, 0:G1, 0:G1], gm[:], gc[:], ge[:], G1, 2))
                    step(v.tensor_scalar(gmn[:], gm[:], 1.0, BIG, ALU.subtract, ALU.mult))
                    s4 = sb[:].rearrange("p t (q e) -> p t q e", q=G1)
                    step(v.tensor_tensor(s4, s4, wide(gm[:], EPG), ALU.mult))
                    step(v.tensor_tensor(s4, s4, wide(gmn[:], EPG), ALU.add))
                    step(rank_select(v, step, sb[:], g.tie16[:], sel[:], cmp[:], eq[:], E1, TOP1))
                    step(v.tensor_tensor(sel[:], sel[:], sc[:], ALU.mult))
                    step(v.tensor_reduce(tot[:], sel[:], AX.X, ALU.add))
                    step(v.tensor_scalar(tot[:], tot[:], 1e-20, None, ALU.add))
                    step(v.reciprocal(tot[:], tot[:]))
                    v.tensor_tensor(comb[:, c % 2], sel[:], tot[:].unsqueeze(2).broadcast_to([P, TC, E1]),
                                    ALU.mult).then_inc(combed, 1)

                def parts(c):
                    v.wait_ge(c1, c + 1)
                    v.tensor_tensor(cr[:], g.b7[0:E1, :], cp1[:], ALU.subtract).then_inc(parted, 1)
                    v.wait_ge(parted, 2 * c + 1)
                    step(v.tensor_copy(cp2[:], cr[:]))
                    step(v.tensor_copy(cps[0:E1, c % 2, :], cp1[:]))
                    step(v.tensor_copy(cps[QD:QD + E1, c % 2, :], cp2[:]))
                    v.tensor_tensor(cps[2 * QD:2 * QD + E1, c % 2, :], cr[:], cp2[:], ALU.subtract).then_inc(parted, 1)

                def finish(c):
                    for t in range(TC * c, TC * c + TC):
                        v.wait_ge(ymade, t + 1)
                        v.tensor_tensor(g.x[:, t, :], (g.b4, g.b5)[t % 2][:, 0:D], g.x[:, t, :],
                                        ALU.add).then_inc(xup, 1)

                choose(0)
                for c in range(NC):
                    for m in range(MH):
                        i = MH * c + m
                        v.wait_ge(sgd, i + 1)
                        v.wait_ge(umade, i + 1)
                        if c >= 2 and m == 0:
                            v.wait_ge(ymade, TC * (c - 1))
                        h = hT[:, c % 2, m, :]
                        ins = v.tensor_tensor(h, sg[:, i % 2, :], g.big1[:, i % 2, :], ALU.mult)
                        ins.then_inc(hmul, 1)
                        v.wait_ge(hmul, i + 1)
                        if m < MS:
                            v.tensor_copy(h[:, 0:1], h[:, 0:1]).then_inc(hready, 1)
                        else:
                            v.wait_ge(bmade, NR * c + m - MS + 1)
                            v.tensor_tensor(h, h, g.b6[:], ALU.mult).then_inc(hready, 1)
                        if m == MS - 1:
                            parts(c)
                    if c + 1 < NC:
                        choose(c + 1)
                    if c:
                        finish(c - 1)
                finish(NC - 1)


def decoder(nc, a, out):
    with ExitStack() as ctx:
        g = Prog(nc, ctx)
        g.big0 = ctx.enter_context(nc.psum_tensor("big0", [P, 2, 512], F32))
        g.big1 = ctx.enter_context(nc.psum_tensor("big1", [P, 2, 512], F32))
        g.b4 = ctx.enter_context(nc.psum_tensor("b4", [P, 512], F32))
        g.b5 = ctx.enter_context(nc.psum_tensor("b5", [P, 512], F32))
        g.b6 = ctx.enter_context(nc.psum_tensor("b6", [P, 512], F32))
        g.b7 = ctx.enter_context(nc.psum_tensor("b7", [P, 512], F32))
        g.x = g.sb("x", [P, NT, D])
        g.q_scr = nc.dram_tensor("q_scr", (3, D, B * S), BF16)
        g.k_scr = nc.dram_tensor("k_scr", (3, D, B * S), BF16)
        g.kc_scr = nc.dram_tensor("kc_scr", (3, D, B * M2), BF16)
        g.wo_dram = {0: a["L0_attn_wo"], 1: a["L0_xattn_wo"], 4: a["L1_xattn_wo"]}
        constants(g)
        stage = DEBUG_STAGES
        with ExitStack() as inner:
            g.va = g.sb("va", [P, NT, H, QD], ctx=inner)
            project(g, 0, {"x": a["x"], "wqkv": a["L0_attn_wqkvT"]}, True)
            if stage > 0:
                attention(g, 0, True)
        g.stage = "ctx_"
        g.vc = g.sb("vc", [P, B, H, QD])
        if stage > 1:
            w = {"ctxT": a["ctxT"], "wq": a["L0_xattn_Wq"], "wk": a["L0_xattn_Wk"], "wv": a["L0_xattn_Wv"],
                 "bq": None, "bo": None, "mask": a["mask"]}
            project(g, 1, w, False)
            attention(g, 1, False, w)
        if stage > 2:
            linear_experts(g, 2, {"Wg": a["L0_ffn_Wg"], "bg": a["L0_ffn_bg"], "We": a["L0_ffn_We"], "be": a["L0_ffn_be"]})
        g.hist = g.sb("hist", [P, KD, B, S])
        if stage > 3:
            recurrence(g, 3, {"WiT": a["L1_attn_WiT"], "WhT": a["L1_attn_WhT"], "bi": a["L1_attn_bi"], "bh": a["L1_attn_bh"]})
        if stage > 4:
            g.recycle()
            w = {"ctxT": a["ctxT"], "wq": a["L1_xattn_wq"], "wk": a["L1_xattn_wk"], "wv": a["L1_xattn_wv"],
                 "bq": a["L1_xattn_bq"], "bk": a["L1_xattn_bk"], "bv": a["L1_xattn_bv"], "bo": a["L1_xattn_bo"],
                 "mask": None}
            project(g, 4, w, False)
            attention(g, 4, False, w)
        if stage > 5:
            gated_experts(g, 5, {"router": a["router"], "cbias": a["cbias"], "gate": a["gate"], "up": a["up"],
                                 "down": a["down"]}, out)
        else:
            s_out = g.sem("s_out")
            with nc.Block() as block:
                @block.sync
                def _(sp):
                    sp.dma_start(out.rearrange("(t p) d -> p t d", p=P), g.x[:]).then_inc(s_out, 16)
                    sp.wait_ge(s_out, 16)


DEBUG_STAGES = 6


def _layout(i):
    def padded(wo):
        rows = wo.reshape(H, DH, D)
        return np.concatenate([rows, np.zeros((H, QD - DH, D), rows.dtype)], axis=1).reshape(H * QD, D)

    def by_feature(w):
        return w.transpose(1, 0, 2).reshape(w.shape[1], -1)

    return {
        "x": i["x"].reshape(B * S, D),
        "ctxT": i["ctx_768"].reshape(B * M2, C2).T,
        "mask": i["mask_BxS2_bf1"].reshape(B * M2).view(np.uint8),
        "L0_attn_wqkvT": i["L0_attn_w_qkv"].T,
        "L0_attn_wo": padded(i["L0_attn_w_proj"].T),
        "L0_xattn_Wq": i["L0_xattn_Wq"], "L0_xattn_Wk": i["L0_xattn_Wk"], "L0_xattn_Wv": i["L0_xattn_Wv"],
        "L0_xattn_wo": padded(i["L0_xattn_Wo"]),
        "L0_ffn_Wg": i["L0_ffn_Wg"], "L0_ffn_bg": i["L0_ffn_bg"], "L0_ffn_We": i["L0_ffn_We"], "L0_ffn_be": i["L0_ffn_be"],
        "L1_attn_WiT": i["L1_attn_Wi"].T, "L1_attn_WhT": i["L1_attn_Wh"].T,
        "L1_attn_bi": i["L1_attn_bi"], "L1_attn_bh": i["L1_attn_bh"],
        "L1_xattn_wq": i["L1_xattn_wq"], "L1_xattn_wk": i["L1_xattn_wk"], "L1_xattn_wv": i["L1_xattn_wv"],
        "L1_xattn_bq": i["L1_xattn_bq"], "L1_xattn_bk": i["L1_xattn_bk"], "L1_xattn_bv": i["L1_xattn_bv"],
        "L1_xattn_wo": padded(i["L1_xattn_wo"]), "L1_xattn_bo": i["L1_xattn_bo"],
        "router": i["L1_ffn_router_w"].T, "cbias": i["L1_ffn_correction_bias"],
        "gate": np.concatenate([i["L1_ffn_shared_gate_w"].T, by_feature(i["L1_ffn_gate_w"])], axis=1),
        "up": np.concatenate([i["L1_ffn_shared_up_w"].T, by_feature(i["L1_ffn_up_w"])], axis=1),
        "down": np.concatenate([i["L1_ffn_shared_down_w"].T, i["L1_ffn_down_w"].reshape(E1 * 64, D)], axis=0),
    }


def kernel(**inputs):
    import concourse.bacc as bacc
    from concourse.bass_utils import run_bass_kernel_spmd

    nc = bacc.Bacc("TRN2", target_bir_lowering=False, num_devices=1)
    arrays, aps = {}, {}
    for name, value in _layout({k: np.asarray(v) for k, v in inputs.items()}).items():
        value = np.ascontiguousarray(value)
        arrays[f"in_{name}"] = value
        aps[name] = nc.dram_tensor(f"in_{name}", value.shape, mybir.dt.from_np(value.dtype), kind="ExternalInput").ap()
    out = nc.dram_tensor("out", (B * S, D), F32, kind="ExternalOutput").ap()
    decoder(nc, aps, out)
    r = run_bass_kernel_spmd(nc, [arrays], core_ids=[0])
    return r.results[0]["out"].reshape(B, S, D)
```

```python
from contextlib import ExitStack

import numpy as np

import concourse.bass as bass
from concourse import mybir

F32 = mybir.dt.float32
BF16 = mybir.dt.bfloat16
F16 = mybir.dt.float16
U8 = mybir.dt.uint8
ALU = mybir.AluOpType
ACT = mybir.ActivationFunctionType
AX = mybir.AxisListType

P = 128
B, S, D = 2, 1024, 256
KD = D // P
NT = B * S // P
TC = 4
NC = NT // TC
CH = TC * P
H, DH = 16, 16
HG = 4
NG = H // HG
QD = 32
M2, C2 = 77, 192
CK = C2 // 2
SCALE = float(DH) ** -0.5
BIG = float(2.0 ** 100)
EPS = 1e-5
COMBOS = [(0, 0), (0, 1), (1, 0), (0, 2), (1, 1), (2, 0)]
R_EXTRA = len(COMBOS) * DH
E0, TOP0 = 8, 2
E1, G1, TOP1 = 16, 4, 4
EPG = E1 // G1
HID = 512 + E1 * 64
MH = HID // P
MS = 512 // P


class Prog:

    def __init__(self, nc, ctx):
        self.nc, self.ctx, self.stage = nc, ctx, ""
        self.sems = []

    def sb(self, name, shape, dt=F32, ctx=None):
        return (ctx or self.ctx).enter_context(self.nc.sbuf_tensor(self.stage + name, shape, dt))

    def sem(self, name):
        self.sems.append(self.nc.alloc_semaphore(name=name))
        return self.sems[-1]

    def recycle(self):
        self.nc.clear_and_free_semaphores(self.sems)
        self.nc.all_engine_barrier()
        self.sems = []


def acc(pe, out, pairs):
    for n, (lhs, rhs) in enumerate(pairs):
        last = pe.matmul(out, lhs, rhs, start=(n == 0), stop=(n == len(pairs) - 1))
    return last


def constants(g):
    nc = g.nc
    g.ident = g.sb("ident", [P, P])
    g.identb = g.sb("identb", [P, P], BF16)
    g.mask_qk = g.sb("mask_qk", [P, P], BF16)
    g.mask_kq = g.sb("mask_kq", [P, P], BF16)
    g.neg_half = g.sb("neg_half", [P, NT])
    g.tie8 = g.sb("tie8", [P, E0, E0])
    g.tie16 = g.sb("tie16", [P, E1, E1])
    g.sel_pair = g.sb("sel_pair", [P, MH - MS, P], BF16)
    zeroed, filled = g.sem("zeroed"), g.sem("filled")
    with nc.Block() as block:
        @block.gpsimd
        def _(pool):
            for t, value in ((g.ident, 0.0), (g.identb, 0.0), (g.mask_qk, 0.0), (g.mask_kq, 0.0),
                             (g.neg_half, -0.5), (g.tie8, 1.0), (g.tie16, 1.0), (g.sel_pair, 1.0)):
                pool.memset(t[:], value).then_inc(zeroed, 1)
            pool.wait_ge(zeroed, 8)
            for t in (g.ident, g.identb):
                pool.affine_select(out=t[:], in_=t[:], compare_op=ALU.not_equal, fill=1.0, base=0,
                                   pattern=[[-1, P]], channel_multiplier=1).then_inc(filled, 1)
            pool.affine_select(out=g.mask_qk[:], in_=g.mask_qk[:], compare_op=ALU.is_ge, fill=-BIG, base=0,
                               pattern=[[-1, P]], channel_multiplier=1).then_inc(filled, 1)
            pool.affine_select(out=g.mask_kq[:], in_=g.mask_kq[:], compare_op=ALU.is_ge, fill=-BIG, base=0,
                               pattern=[[1, P]], channel_multiplier=-1).then_inc(filled, 1)
            for t, e in ((g.tie8, E0), (g.tie16, E1)):
                pool.affine_select(out=t[:], in_=t[:], compare_op=ALU.is_ge, fill=0.0, base=-1,
                                   pattern=[[1, e], [-1, e]], channel_multiplier=0).then_inc(filled, 1)
            pool.memset(g.sel_pair[:], 0.0).then_inc(zeroed, 1)
            pool.wait_ge(zeroed, 9)
            for n in range(3):
                v = g.sel_pair[:].rearrange("p m (a i) -> p m a i", a=2)
                pool.affine_select(out=v, in_=v, compare_op=ALU.not_equal, fill=1.0, base=-QD * n,
                                   pattern=[[-2, MH - MS], [-1, 2], [0, 64]], channel_multiplier=1).then_inc(filled, 1)
                pool.wait_ge(filled, 7 + n)


class Norm:

    def __init__(self, g, n):
        self.g = g
        self.stats, self.meanvar = g.sem(f"n{n}_stats"), g.sem(f"n{n}_meanvar")
        self.var_eps, self.rstd = g.sem(f"n{n}_var_eps"), g.sem(f"n{n}_rstd")
        self.xn, self.turned, self.xnT = g.sem(f"n{n}_xn"), g.sem(f"n{n}_turned"), g.sem(f"n{n}_xnT")

    def vector(self, v, chunk_ready):
        g = self.g
        for c in range(NC + 1):
            if c < NC:
                chunk_ready(c)
                for t in range(TC * c, TC * c + TC):
                    v.bn_stats(g.bn[:, t, :], g.x[:, t, :]).then_inc(self.stats, 1)
                for t in range(TC * c, TC * c + TC):
                    v.wait_ge(self.stats, t + 1)
                    v.bn_aggr(g.mv[:, t, :], g.bn[:, t, :]).then_inc(self.meanvar, 1)
                v.wait_ge(self.meanvar, TC * (c + 1))
                v.tensor_scalar(g.ve[:, TC * c:TC * c + TC], g.mv[:, TC * c:TC * c + TC, 1], EPS, None,
                                ALU.add).then_inc(self.var_eps, 1)
            if c:
                v.wait_ge(self.rstd, c)
                for t in range(TC * (c - 1), TC * c):
                    v.tensor_scalar(g.xn[:, t, :], g.x[:, t, :], g.mv[:, t, 0:1], g.rs[:, t:t + 1],
                                    ALU.subtract, ALU.mult).then_inc(self.xn, 1)

    def gpsimd(self, pool):
        g = self.g
        for c in range(NC):
            pool.wait_ge(self.var_eps, c + 1)
            pool.tensor_tensor(g.rs[:, TC * c:TC * c + TC], g.ve[:, TC * c:TC * c + TC],
                               g.neg_half[:, 0:TC], ALU.pow).then_inc(self.rstd, 1)

    def tensor(self, pe, c):
        g = self.g
        for t in range(TC * c, TC * c + TC):
            pe.wait_ge(self.xn, t + 1)
            if t >= 2:
                pe.wait_ge(self.xnT, t - 1)
            bank = (g.b4, g.b5)[t % 2]
            for k in range(KD):
                last = pe.transpose(bank[:, k * P:(k + 1) * P], g.xn[:, t, k * P:(k + 1) * P], g.ident[:])
            last.then_inc(self.turned, 1)

    def scalar(self, act, c):
        g = self.g
        for t in range(TC * c, TC * c + TC):
            act.wait_ge(self.turned, t + 1)
            bank = (g.b4, g.b5)[t % 2]
            act.activation(g.xnT[:, :, t * P:(t + 1) * P], bank[:, 0:KD * P].rearrange("p (k n) -> p k n", k=KD),
                           ACT.Copy).then_inc(self.xnT, 1)


def norm_buffers(g, ctx, pad=False):
    g.bn = g.sb("bn", [P, NT, 6], ctx=ctx)
    g.mv = g.sb("mv", [P, NT, 2], ctx=ctx)
    g.ve = g.sb("ve", [P, NT], ctx=ctx)
    g.rs = g.sb("rs", [P, NT], ctx=ctx)
    g.xn = g.sb("xn", [P, NT, D], ctx=ctx)
    g.xnT_flat = g.sb("xnT", [P, KD * B * S + (S if pad else 0)], ctx=ctx)
    g.xnT = g.xnT_flat[:, 0:KD * B * S].rearrange("p (k n) -> p k n", k=KD)


def project(g, n, w, causal, st):
    g.stage = f"p{n}_"
    nc = g.nc
    with ExitStack() as ctx:
        norm_buffers(g, ctx)
        NM = 4 if causal else 2
        if causal:
            wqkv = g.sb("wqkv", [P, KD, 3 * D], ctx=ctx)
        else:
            wq = g.sb("wq", [P, KD, D], ctx=ctx)
            wk = g.sb("wk", [CK, 2, D], ctx=ctx)
            wv = g.sb("wv", [CK, 2, D], ctx=ctx)
            cT = g.sb("cT", [CK, 2, B * M2], ctx=ctx)
            bq = g.sb("bq", [P, KD], ctx=ctx)
            bk = g.sb("bk", [P, KD], ctx=ctx)
            bv = g.sb("bv", [P, D], ctx=ctx)
        parts = g.sb("parts", [P, 3, 3, CH], BF16, ctx=ctx)
        rest = g.sb("rest", [P, 3, CH], ctx=ctx)
        ln = Norm(g, n)
        w_in, made, part1, left, part2, part3, vmade, vcopied, ones = (g.sem(f"p{n}_{s}") for s in (
            "w_in", "made", "part1", "left", "part2", "part3", "vmade", "vcopied", "ones"))
        x_in = [g.sem(f"p{n}_x_in{c}") for c in range(NC)] if causal else None
        stored = [g.sem(f"p{n}_stored{r}") for r in range(3)]
        banks = [g.b0[:], g.b1[:], g.b2[:], g.b3[:]]
        jobs = [("x", c, m) for c in range(NC) for m in range(NM)]
        if not causal:
            jobs = [("c", 0, m) for m in range(KD)] + jobs
        if causal:
            loads = [(NM * 1, st.load_q, 0), (NM * 2, st.load_q, 1), (NM * 2, st.load_k, 0), (NM * 4, st.load_k, 1)]
        else:
            loads = [(KD + 1, st.load_k, 0), (KD + 1, st.load_k, 1)]
            loads += [(KD + NM * (c + 1), st.load_q, c) for c in range(NC)]
        bias = not causal and w["bq"] is not None
        after_rnn = bias
        back, xup = g.sem(f"p{n}_back"), g.sem(f"p{n}_xup")

        def width(job):
            return CH if job[0] == "x" else B * M2

        with nc.Block() as block:
            @block.sync
            def _(sp):
                if causal:
                    xv = w["x"].rearrange("(t p) d -> p t d", p=P)
                    sp.dma_start(g.x[:, 0:TC, :], xv[:, 0:TC, :]).then_inc(x_in[0], 16)
                    sp.dma_start(wqkv[:], w["wqkv"].rearrange("(k p) n -> p k n", p=P)).then_inc(w_in, 16)
                    for c in range(1, NC):
                        sp.dma_start(g.x[:, TC * c:TC * c + TC, :], xv[:, TC * c:TC * c + TC, :]).then_inc(x_in[c], 16)
                else:
                    sp.dma_start(cT[:], w["ctxT"].rearrange("(k p) n -> p k n", p=CK)).then_inc(w_in, 16)
                    sp.dma_start(wk[:], w["wk"].rearrange("(k p) n -> p k n", p=CK)).then_inc(w_in, 16)
                    sp.dma_start(wv[:], w["wv"].rearrange("(k p) n -> p k n", p=CK)).then_inc(w_in, 16)
                    sp.dma_start(wq[:], w["wq"].rearrange("(k p) n -> p k n", p=P)).then_inc(w_in, 16)
                    if bias:
                        with nc.allow_non_contiguous_dma("256 biases"):
                            sp.dma_start(bq[:], w["bq"].rearrange("(k p) -> p k", p=P)).then_inc(w_in, 16)
                            sp.dma_start(bk[:], w["bk"].rearrange("(k p) -> p k", p=P)).then_inc(w_in, 16)
                        sp.dma_start(bv[:], w["bv"].partition_broadcast(P)).then_inc(w_in, 16)
                for i, job in enumerate(jobs):
                    sp.wait_ge(part3, i + 1)
                    N = width(job)
                    if job[0] == "x":
                        row, scr = (job[2] % KD) * P, (g.q_scr if job[2] < KD else g.k_scr)
                        dst = scr[:, row:row + P, CH * job[1]:CH * job[1] + N]
                    else:
                        dst = g.kc_scr[:, job[2] * P:(job[2] + 1) * P, :]
                    sp.dma_start(dst.rearrange("a p n -> p a n"), parts[:, i % 3, :, 0:N]).then_inc(stored[i % 3], 16)
                    for at, load, x in loads:
                        if at == i:
                            for r in range(3):
                                sp.wait_ge(stored[r], 16 * ((i - 1 - r) // 3 + 1))
                            load(g, sp, x)
                for r in range(3):
                    sp.wait_ge(stored[r], 16 * ((len(jobs) - r + 2) // 3))
                for at, load, x in loads:
                    if at == len(jobs):
                        load(g, sp, x)

            n_w = 1 if causal else (7 if bias else 4)

            @block.tensor
            def _(pe):
                pe.wait_ge(w_in, 16 * n_w)
                if after_rnn:
                    for t in range(NT):
                        if t >= 2:
                            pe.wait_ge(xup, t - 1)
                        for k in range(KD):
                            last = pe.transpose((g.b6, g.b7)[t % 2][:, k * P:(k + 1) * P],
                                                g.hist[:, k, t // (NT // B), P * (t % (NT // B)):P * (t % (NT // B)) + P],
                                                g.ident[:])
                        last.then_inc(back, 1)
                    pe.wait_ge(xup, NT)
                for i, job in enumerate(jobs):
                    if job[0] == "x" and job[2] == 0:
                        ln.tensor(pe, job[1])
                        pe.wait_ge(ln.xnT, TC * (job[1] + 1))
                    if i >= 4:
                        pe.wait_ge(left, i - 3)
                    out = banks[i % 4][:, 0:width(job)]
                    if job[0] == "x":
                        c, m = job[1], job[2]
                        wt = wqkv if causal else wq
                        acc(pe, out, [(wt[:, k, m * P:(m + 1) * P], g.xnT[:, k, CH * c:CH * c + CH])
                                      for k in range(KD)]).then_inc(made, 1)
                    else:
                        m = job[2]
                        acc(pe, out, [(wk[:, k, m * P:(m + 1) * P], cT[:, k, :]) for k in range(2)]).then_inc(made, 1)
                    if causal and job[2] == NM - 1:
                        for t in range(TC * job[1], TC * job[1] + TC):
                            if t >= 2:
                                pe.wait_ge(vcopied, t - 1)
                            acc(pe, (g.b6, g.b7)[t % 2][:, 0:D],
                                [(g.xnT[:, k, t * P:(t + 1) * P], wqkv[:, k, 2 * D:3 * D])
                                 for k in range(KD)]).then_inc(vmade, 1)
                    if not causal and i < B:
                        acc(pe, (g.b6, g.b7)[i][0:M2, 0:D], [(cT[:, k, M2 * i:M2 * i + M2], wv[:, k, :])
                                                            for k in range(2)]).then_inc(vmade, 1)

            @block.scalar
            def _(act):
                nv = 0
                for i, job in enumerate(jobs):
                    if job[0] == "x" and job[2] == 0:
                        ln.scalar(act, job[1])
                    N = width(job)
                    act.wait_ge(made, i + 1)
                    if i >= 3:
                        act.wait_ge(stored[i % 3], 16 * (i // 3))
                    out, src = parts[:, i % 3, 0, 0:N], banks[i % 4][:, 0:N]
                    if bias:
                        if i == 0:
                            act.wait_ge(w_in, 16 * n_w)
                        col = job[2]
                        act.activation(out, src, ACT.Identity,
                                       bias=(bq if job[0] == "x" else bk)[:, col:col + 1]).then_inc(part1, 1)
                    else:
                        act.activation(out, src, ACT.Copy).then_inc(part1, 1)
                    if causal and job[2] == NM - 1:
                        for t in range(TC * job[1], TC * job[1] + TC):
                            act.wait_ge(vmade, t + 1)
                            if t == 0:
                                act.wait_ge(ones, 1)
                            act.activation(g.va[:, t, :, 0:DH],
                                           (g.b6, g.b7)[t % 2][:, 0:D].rearrange("p (h d) -> p h d", d=DH),
                                           ACT.Copy).then_inc(vcopied, 1)
                    if not causal and i < B:
                        act.wait_ge(vmade, i + 1)
                        act.wait_ge(ones, 1)
                        act.activation(g.vc[0:M2, i, :, 0:DH],
                                       (g.b6, g.b7)[i][0:M2, 0:D].rearrange("p (h d) -> p h d", d=DH),
                                       ACT.Copy).then_inc(vcopied, 1)

            @block.vector
            def _(v):
                def chunk_ready(c):
                    if causal:
                        v.wait_ge(x_in[c], 16)
                    if after_rnn:
                        for t in range(TC * c, TC * c + TC):
                            v.wait_ge(xup, t + 1)

                def jobs_of(c):
                    for i, job in enumerate(jobs):
                        if (job[1] if job[0] == "x" else -1) != c:
                            continue
                        N = width(job)
                        v.wait_ge(part1, i + 1)
                        if i >= 3:
                            v.wait_ge(part3, i - 2)
                        src, p1, r = banks[i % 4][:, 0:N], parts[:, i % 3, 0, 0:N], rest[:, i % 3, 0:N]
                        if bias:
                            b = (bq if job[0] == "x" else bk)[:, job[2]:job[2] + 1]
                            v.scalar_tensor_tensor(out=r, in0=src, scalar=b, in1=p1, op0=ALU.add,
                                                   op1=ALU.subtract).then_inc(left, 1)
                        else:
                            v.tensor_tensor(r, src, p1, ALU.subtract).then_inc(left, 1)
                        v.wait_ge(left, i + 1)
                        v.tensor_copy(parts[:, i % 3, 1, 0:N], r).then_inc(part2, 1)

                if after_rnn:
                    for t in range(NT):
                        v.wait_ge(back, t + 1)
                        v.tensor_tensor(g.x[:, t, :], (g.b6, g.b7)[t % 2][:, 0:D], g.x[:, t, :],
                                        ALU.add).then_inc(xup, 1)
                if bias:
                    v.wait_ge(w_in, 16 * n_w)
                jobs_of(-1)
                if bias:
                    for b in range(B):
                        v.wait_ge(vcopied, B)
                        vb = g.vc[0:M2, b, :, 0:DH]
                        v.tensor_tensor(vb, vb, bv[0:M2, :].rearrange("p (h d) -> p h d", d=DH), ALU.add)
                ln.vector(v, chunk_ready)
                for c in range(NC):
                    jobs_of(c)

            @block.gpsimd
            def _(pool):
                va = g.va[:, :, :, DH:QD] if causal else g.vc[:, :, :, DH:QD]
                pool.memset(va, 1.0).then_inc(ones, 1)
                order = [("n", None)] + [("j", i) for i in range(len(jobs))]
                if not causal:
                    order = [("j", 0), ("j", 1), ("n", None)] + [("j", i) for i in range(2, len(jobs))]
                for what, i in order:
                    if what == "n":
                        ln.gpsimd(pool)
                        continue
                    N = width(jobs[i])
                    r, p2, p3 = rest[:, i % 3, 0:N], parts[:, i % 3, 1, 0:N], parts[:, i % 3, 2, 0:N]
                    pool.wait_ge(part2, i + 1)
                    pool.tensor_tensor(p3, r, p2, ALU.subtract).then_inc(part3, 1)


class Stacks:

    def __init__(self, g, n, causal, masked, ctx):
        self.causal = causal
        self.r_mask = R_EXTRA
        self.r_max = R_EXTRA + 1 if masked else R_EXTRA
        self.rows = self.r_max + 3
        self.first_rows = self.r_max
        self.ks = g.sb("ks", [P, B, H, S if causal else M2], BF16, ctx=ctx)
        self.ring = 2 if causal else NC
        self.qs = g.sb("qs", [P, self.ring, H, CH], BF16, ctx=ctx)
        self.k_in = [g.sem(f"k{n}_in{b}") for b in range(B)]
        self.q_in = [g.sem(f"q{n}_in{r}") for r in range(self.ring)]

    def load_q(self, g, sp, c, slot=None):
        slot = c if slot is None else slot
        for r, (qp, _) in enumerate(COMBOS):
            sp.dma_start(self.qs[DH * r:DH * r + DH, slot, :, :],
                         g.q_scr[qp, :, CH * c:CH * c + CH].rearrange("(h d) t -> d h t", d=DH)
                         ).then_inc(self.q_in[slot], 16)

    def load_k(self, g, sp, b):
        scr, N = (g.k_scr, S) if self.causal else (g.kc_scr, M2)
        for r, (_, kp) in enumerate(COMBOS):
            sp.dma_start(self.ks[DH * r:DH * r + DH, b, :, :],
                         scr[kp, :, N * b:N * b + N].rearrange("(h d) t -> d h t", d=DH)).then_inc(self.k_in[b], 16)


def attention_order(causal, first, first_of, steps, steps_of):
    order, later = [], []
    for p in range(-1, NC):
        a = first_of[p + 1] if p + 1 < NC else []
        b = steps_of[p] if p >= 0 else []
        slots = 5 * max(1, len(b))
        begin, end = (15 if p >= 1 else 0, slots - 15) if causal and b else (0, max(1, slots - 12))
        todo = list(a)
        total = sum(first[i][4] + 64 for i in a)
        done = 0
        for j in range(slots):
            while todo and j >= begin and done < total * (j + 1 - begin) / (end - begin):
                order.append(("first", todo[0]))
                done += first[todo.pop(0)][4] + 64
            if a and j == end - 1:
                order += [("first", i) for i in todo] + [("max", p + 1)]
                todo = []
            if a and j == min(end + 1, slots - 1):
                order.append(("turn", p + 1))
            if not b:
                continue
            i, part = b[j // 5], j % 5
            if part != 2:
                order.append(("scores", i, part - (part > 2)))
            elif i:
                order.append(("values", i - 1))
                u = steps[i - 1][0]
                if steps[i][0] != u:
                    later.append(("norm", u))
                    if u % NG == NG - 1:
                        for t in range(TC * (u // NG), TC * (u // NG) + TC):
                            later += [("turned", t), ("out", t)]
            if part in ((0, 4) if causal else (0, 1, 3, 4)):
                order += later[:1]
                later = later[1:]
    u = NG * NC - 1
    order += later + [("values", len(steps) - 1), ("norm", u)]
    for t in range(NT - TC, NT):
        order += [("turned", t), ("out", t)]
    return order


def attention(g, n, causal, st, w=None):
    g.stage = f"a{n}_"
    nc = g.nc
    KP = P if causal else M2
    chunks = [0, 1, 3, 2] if causal else list(range(NC))
    units = [(c, hg) for c in chunks for hg in range(NG)]

    def blocks(c):
        return TC * (c % 2) + TC if causal else 1

    first, items_end = [], []
    for p, c in enumerate(chunks):
        for qt in range(TC):
            if causal:
                keys = P * (TC * (c % 2) + qt + 1)
                for h in range(H):
                    for half in range((keys + CH - 1) // CH):
                        first.append((p, qt, h, half, min(CH, keys - CH * half)))
            else:
                first += [(p, qt, hg, 0, HG * M2) for hg in range(NG)]
        items_end.append(len(first))
    steps = [(u, kb) for u in range(len(units)) for kb in range(blocks(units[u][0]))]
    first_of = [[i for i, it in enumerate(first) if it[0] == p] for p in range(NC)]
    steps_of = [[i for i, step in enumerate(steps) if step[0] // NG == p] for p in range(NC)]
    order = attention_order(causal, first, first_of, steps, steps_of)
    b7 = [(e[0], e[1]) for e in order if e[0] in ("turn", "norm", "turned", "out")]

    def ends_unit(i):
        return i + 1 == len(steps) or steps[i + 1][0] != steps[i][0]

    with ExitStack() as ctx:
        ks, qs = st.ks, st.qs
        mxp = g.sb("mxp", [P, 2, TC, H, 2], ctx=ctx)
        nm = g.sb("nm", [P, 2, TC, H], ctx=ctx)
        mp = g.sb("mp", [H, 2, 3, CH], BF16, ctx=ctx)
        mr = g.sb("mr", [H, 2, CH], ctx=ctx)
        pr = g.sb("pr", [P, 2, HG, CH], ctx=ctx)
        osb = g.sb("osb", [P, 2, CH], ctx=ctx)
        rec = g.sb("rec", [P, 2, TC, HG], ctx=ctx)
        on = g.sb("on", [P, 2, TC, D], ctx=ctx)
        onT = g.sb("onT", [P, 2, KD, P], ctx=ctx)
        wo = g.sb("wo", [P, KD, D], ctx=ctx)
        va = g.va if causal else g.vc
        names = ("s1", "max", "nm", "nmT", "n1", "nr", "n2", "n3", "s2", "exp", "pv", "oev", "oT", "rec", "on",
                 "back", "onT", "wo_in", "y", "xup", "ones", "rows", "kmul", "bo_in", "xbo", "mneg", "mask_rows")
        s = {k: g.sem(f"a{n}_{k}") for k in names}
        m_in = [g.sem(f"a{n}_m_in{r}") for r in range(2)]
        masked = not causal and w["mask"] is not None
        bias_o = not causal and w["bo"] is not None
        rowsrc = g.sb("rowsrc", [P, CH], BF16, ctx=ctx)
        if masked:
            mrow8 = g.sb("mrow8", [P, B * M2], U8, ctx=ctx)
            mrow = g.sb("mrow", [P, B * M2], ctx=ctx)
            mneg = g.sb("mneg", [P, B * M2], BF16, ctx=ctx)
        if bias_o:
            bo = g.sb("bo", [P, D], ctx=ctx)
        n_q = len(COMBOS) * 16
        first_banks, score_banks = (g.b3, g.b4, g.b5), (g.b0, g.b1, g.b2)
        freed_by = {"turn": "nr", "norm": "on", "turned": "onT", "out": "xup"}

        def wait_b7(pe, user):
            at = b7.index(user)
            if at:
                kind, u = b7[at - 1]
                pe.wait_ge(s[freed_by[kind]], u + 1)

        with nc.Block() as block:
            @block.sync
            def _(sp):
                if masked:
                    sp.dma_start(mrow8[:], w["mask"].partition_broadcast(P)).then_inc(s["bo_in"], 16)
                if bias_o:
                    sp.dma_start(bo[:], w["bo"].partition_broadcast(P)).then_inc(s["bo_in"], 16)
                sp.wait_ge(s["ones"], 1)
                if masked:
                    sp.dma_start(qs[st.r_mask:st.r_mask + 1].rearrange("p a h t -> p (a h) t"),
                                 rowsrc[0:1, :].unsqueeze(1).broadcast_to([1, st.ring * H, CH])).then_inc(s["mask_rows"], 16)
                    sp.wait_ge(s["mneg"], 2)
                    for b in range(B):
                        sp.dma_start(ks[st.r_mask:st.r_mask + 1, b], mneg[0:1, M2 * b:M2 * b + M2].unsqueeze(1)
                                     .broadcast_to([1, H, M2])).then_inc(s["mask_rows"], 16)
                for b in range(B):
                    src = rowsrc[st.r_max:st.rows, 0:CH if causal else M2]
                    if causal:
                        for half in range(S // CH):
                            sp.dma_start(ks[st.r_max:st.rows, b, :, CH * half:CH * half + CH],
                                         src.unsqueeze(1).broadcast_to([3, H, CH])).then_inc(s["rows"], 16)
                    else:
                        sp.dma_start(ks[st.r_max:st.rows, b], src.unsqueeze(1).broadcast_to([3, H, M2])
                                     ).then_inc(s["rows"], 16)
                sp.dma_start(wo[:], g.wo_dram[n].rearrange("(k p) n -> p k n", p=P)).then_inc(s["wo_in"], 16)
                for what, i, *h in order:
                    if what == "turn":
                        sp.wait_ge(s["n3"], i + 1)
                        sp.wait_ge(s["n2"], i + 1)
                        for k in range(3):
                            sp.dma_start(qs[st.r_max + k:st.r_max + k + 1, i % st.ring, :, :],
                                         mp[:, i % 2, k, :]).then_inc(m_in[i % 2], 16)
                    if what == "scores" and h[0] == HG - 1 and ends_unit(i) and steps[i][0] % NG == NG - 1:
                        p = steps[i][0] // NG
                        if p + st.ring < NC:
                            sp.wait_ge(s["s2"], HG * (i + 1))
                            st.load_q(g, sp, chunks[p + st.ring], p)

            n_rows = 16 * B * (S // CH if causal else 1)

            @block.gpsimd
            def _(pool):
                if masked:
                    pool.wait_ge(s["bo_in"], 16)
                    pool.tensor_copy(mrow[:], mrow8[:]).then_inc(s["mneg"], 1)
                    pool.wait_ge(s["mneg"], 1)
                    pool.tensor_scalar(mneg[:], mrow[:], 1.0, BIG, ALU.subtract, ALU.mult).then_inc(s["mneg"], 1)
                if bias_o:
                    pool.wait_ge(s["bo_in"], 16 * (1 + masked))
                    for t in range(NT):
                        pool.tensor_tensor(g.x[:, t, :], g.x[:, t, :], bo[:], ALU.add).then_inc(s["xbo"], 1)
                for what, u, *_ in order:
                    if what == "turn":
                        pool.wait_ge(s["n2"], u + 1)
                        pool.tensor_tensor(mp[:, u % 2, 2, :], mr[:, u % 2, :], mp[:, u % 2, 1, :],
                                           ALU.subtract).then_inc(s["n3"], 1)

            @block.tensor
            def _(pe):
                def first_pass(i):
                    p, qt, h, half, N = first[i]
                    c, slot = chunks[p], p % st.ring
                    bank = first_banks[i % 3]
                    if qt == 0 and h == 0 and half == 0:
                        pe.wait_ge(st.q_in[slot], n_q * (p // st.ring + 1))
                        pe.wait_ge(st.k_in[c // 2], n_q)
                        if masked:
                            pe.wait_ge(s["kmul"], B)
                            pe.wait_ge(s["mask_rows"], 16 * (1 + B))
                    if i >= 3:
                        pe.wait_ge(s["max"], i - 2)
                    if causal:
                        diag = CH * half + N == P * (TC * (c % 2) + qt + 1)
                        last = pe.matmul(bank[:, 0:N], qs[0:st.first_rows, slot, h, P * qt:P * qt + P],
                                         ks[0:st.first_rows, c // 2, h, CH * half:CH * half + N],
                                         start=True, stop=not diag)
                        if diag:
                            last = pe.matmul(bank[:, N - P:N], g.identb[:], g.mask_qk[:], start=False, stop=True)
                    else:
                        for j in range(HG):
                            last = pe.matmul(bank[:, M2 * j:M2 * j + M2],
                                             qs[0:st.first_rows, slot, HG * h + j, P * qt:P * qt + P],
                                             ks[0:st.first_rows, c // 2, HG * h + j, :], start=True, stop=True)
                    last.then_inc(s["s1"], 1)

                def turn_max(p):
                    if causal:
                        pe.wait_ge(s["nm"], p + 1)
                    else:
                        pe.wait_ge(s["max"], items_end[p])
                    wait_b7(pe, ("turn", p))
                    for qt in range(TC):
                        last = pe.transpose(g.b7[0:H, P * qt:P * qt + P], nm[:, p % 2, qt, :], g.ident[:])
                    last.then_inc(s["nmT"], 1)

                def scores(i, h):
                    u, kb = steps[i]
                    c, hg = units[u]
                    p = u // NG
                    if u % NG == 0 and kb == 0 and h == 0:
                        pe.wait_ge(m_in[p % 2], 48 * (p // 2 + 1))
                        if u == 0:
                            pe.wait_ge(s["rows"], n_rows)
                    d = kb - TC * (c % 2) if causal else -1
                    off = P * max(d, 0)
                    k = HG * i + h
                    if k >= 3:
                        pe.wait_ge(s["exp"], k - 2)
                    bank = score_banks[k % 3]
                    hh = HG * hg + h
                    last = pe.matmul(bank[0:KP, off:CH], ks[0:st.rows, c // 2, hh, P * kb:P * kb + KP],
                                     qs[0:st.rows, p % st.ring, hh, off:CH], start=True, stop=d < 0)
                    if d >= 0:
                        last = pe.matmul(bank[:, off:off + P], g.identb[:], g.mask_kq[:], start=False, stop=True)
                    last.then_inc(s["s2"], 1)

                def values(i):
                    u, kb = steps[i]
                    c, hg = units[u]
                    off = P * max(kb - TC * (c % 2), 0) if causal else 0
                    tile = TC * 2 * (c // 2) + kb if causal else c // 2
                    if kb == 0 and u:
                        pe.wait_ge(s["oev"], u)
                    pe.wait_ge(s["exp"], HG * (i + 1))
                    for h in range(HG):
                        last = pe.matmul(g.b6[QD * h:QD * h + QD, off:CH], va[0:KP, tile, HG * hg + h, :],
                                         pr[0:KP, i % 2, h, off:CH], start=(kb == 0), stop=ends_unit(i),
                                         tile_position=(0, QD * h))
                    last.then_inc(s["pv"], 1)

                def norm(u):
                    pe.wait_ge(s["oev"], u + 1)
                    wait_b7(pe, ("norm", u))
                    for qt in range(TC):
                        last = pe.transpose(g.b7[:, P * qt:P * qt + P], osb[:, u % 2, P * qt:P * qt + P], g.ident[:])
                    last.then_inc(s["oT"], 1)

                def turned(t):
                    pe.wait_ge(s["on"], NG * (t // TC + 1))
                    wait_b7(pe, ("turned", t))
                    for k in range(KD):
                        last = pe.transpose(g.b7[:, k * P:(k + 1) * P],
                                            on[:, t // TC % 2, t % TC, k * P:(k + 1) * P], g.ident[:])
                    last.then_inc(s["back"], 1)

                def output(t):
                    if t == 0:
                        pe.wait_ge(s["wo_in"], 16)
                    wait_b7(pe, ("out", t))
                    pe.wait_ge(s["onT"], t + 1)
                    acc(pe, g.b7[:, 0:D], [(onT[:, t % 2, k, :], wo[:, k, :]) for k in range(KD)]).then_inc(s["y"], 1)

                for what, i, *h in order:
                    if what == "first":
                        first_pass(i)
                    if what == "turn":
                        turn_max(i)
                    if what == "scores":
                        scores(i, h[0])
                    if what == "values":
                        values(i)
                    if what == "norm":
                        norm(i)
                    if what == "turned":
                        turned(i)
                    if what == "out":
                        output(i)

            @block.scalar
            def _(act):
                for what, i, *h in order:
                    if what == "scores":
                        u, kb = steps[i]
                        off = P * max(kb - TC * (units[u][0] % 2), 0) if causal else 0
                        k = HG * i + h[0]
                        act.wait_ge(s["s2"], k + 1)
                        if i >= 2:
                            act.wait_ge(s["pv"], i - 1)
                        act.activation(pr[0:KP, i % 2, h[0], off:CH], score_banks[k % 3][0:KP, off:CH],
                                       ACT.Exp, scale=SCALE).then_inc(s["exp"], 1)
                    if what == "values" and ends_unit(i):
                        u = steps[i][0]
                        act.wait_ge(s["pv"], i + 1)
                        if u >= 2:
                            act.wait_ge(s["oT"], u - 1)
                        act.activation(osb[:, u % 2, :], g.b6[:], ACT.Copy).then_inc(s["oev"], 1)
                    if what == "turned":
                        act.wait_ge(s["back"], i + 1)
                        if i >= 2:
                            act.wait_ge(s["y"], i - 1)
                        act.activation(onT[:, i % 2].rearrange("p k n -> p (k n)"), g.b7[:, 0:D],
                                       ACT.Copy).then_inc(s["onT"], 1)

            @block.vector
            def _(v):
                v.memset(rowsrc[:], 1.0).then_inc(s["ones"], 1)
                if masked:
                    for b in range(B):
                        v.wait_ge(st.k_in[b], n_q)
                        v.wait_ge(s["mneg"], 1)
                        kk = ks[0:R_EXTRA, b]
                        v.tensor_tensor(kk, kk, mrow[0:R_EXTRA, M2 * b:M2 * b + M2].unsqueeze(1)
                                        .broadcast_to([R_EXTRA, H, M2]), ALU.mult).then_inc(s["kmul"], 1)
                for what, i, *_ in order:
                    if what == "first":
                        p, qt, h, half, N = first[i]
                        bank = first_banks[i % 3]
                        v.wait_ge(s["s1"], i + 1)
                        if causal:
                            v.tensor_reduce(mxp[:, p % 2, qt, h, half:half + 1], bank[:, 0:N], AX.X,
                                            ALU.max).then_inc(s["max"], 1)
                        else:
                            if qt == 0 and h == 0 and p >= 2:
                                v.wait_ge(s["nmT"], p - 1)
                            v.tensor_reduce(nm[:, p % 2, qt, HG * h:HG * h + HG],
                                            bank[:, 0:N].rearrange("p (h t) -> p h t", h=HG),
                                            AX.X, ALU.max, negate=True).then_inc(s["max"], 1)
                    if what == "max" and causal:
                        v.wait_ge(s["max"], items_end[i])
                        if i >= 2:
                            v.wait_ge(s["nmT"], i - 1)
                        c = chunks[i]
                        for qt in range(TC):
                            last = v.tensor_reduce(nm[:, i % 2, qt, :], mxp[:, i % 2, qt, :, 0:1 + c % 2],
                                                   AX.X, ALU.max, negate=True)
                        last.then_inc(s["nm"], 1)
                    if what == "turn":
                        v.wait_ge(s["nmT"], i + 1)
                        if i >= 2:
                            v.wait_ge(m_in[i % 2], 48 * (i // 2))
                        v.tensor_copy(mp[:, i % 2, 0, :], g.b7[0:H, :]).then_inc(s["n1"], 1)
                        v.wait_ge(s["n1"], i + 1)
                        if i >= 2:
                            v.wait_ge(s["n3"], i - 1)
                        v.tensor_tensor(mr[:, i % 2, :], g.b7[0:H, :], mp[:, i % 2, 0, :],
                                        ALU.subtract).then_inc(s["nr"], 1)
                        v.wait_ge(s["nr"], i + 1)
                        v.tensor_copy(mp[:, i % 2, 1, :], mr[:, i % 2, :]).then_inc(s["n2"], 1)
                    if what == "norm":
                        p, hg = i // NG, i % NG
                        o = g.b7[:].rearrange("p (t h d) -> p t h d", t=TC, h=HG)
                        v.wait_ge(s["oT"], i + 1)
                        v.reciprocal(rec[:, i % 2], o[:, :, :, DH]).then_inc(s["rec"], 1)
                        v.wait_ge(s["rec"], i + 1)
                        if p >= 2:
                            v.wait_ge(s["back"], TC * (p - 1))
                        v.tensor_tensor(
                            on[:, p % 2, :, HG * DH * hg:HG * DH * hg + HG * DH].rearrange("p t (h d) -> p t h d", h=HG),
                            o[:, :, :, 0:DH], rec[:, i % 2].unsqueeze(3).broadcast_to([P, TC, HG, DH]),
                            ALU.mult).then_inc(s["on"], 1)
                    if what == "out":
                        if bias_o and i == 0:
                            v.wait_ge(s["xbo"], NT)
                        v.wait_ge(s["y"], i + 1)
                        t = TC * chunks[i // TC] + i % TC
                        v.tensor_tensor(g.x[:, t, :], g.b7[:, 0:D], g.x[:, t, :], ALU.add).then_inc(s["xup"], 1)


def rank_select(v, step, gates, tie, sel, cmp, eq, e, top):
    n = gates.shape[1]
    gj = gates.unsqueeze(2).broadcast_to([P, n, e, e])
    ge = gates.unsqueeze(3).broadcast_to([P, n, e, e])
    step(v.tensor_tensor(cmp, gj, ge, ALU.is_gt))
    step(v.tensor_tensor(eq, gj, ge, ALU.is_equal))
    step(v.tensor_tensor(eq, eq, tie.unsqueeze(1).broadcast_to([P, n, e, e]), ALU.mult))
    step(v.tensor_tensor(cmp, cmp, eq, ALU.add))
    step(v.tensor_reduce(sel, cmp, AX.X, ALU.add))
    return v.tensor_scalar(sel, sel, float(top), None, ALU.is_lt)


def linear_experts(g, n, w):
    g.stage = f"f{n}_"
    nc = g.nc
    with ExitStack() as ctx:
        norm_buffers(g, ctx)
        wg = g.sb("wg", [P, KD, E0], ctx=ctx)
        we = g.sb("we", [P, KD, E0 * D], ctx=ctx)
        be = g.sb("be", [E0, D], ctx=ctx)
        bg = g.sb("bg", [P, E0], ctx=ctx)
        gate = g.sb("gate", [P, TC, E0], ctx=ctx)
        sel = g.sb("sel", [P, TC, E0], ctx=ctx)
        top = g.sb("top", [P, TC], ctx=ctx)
        cmp = g.sb("cmp", [P, TC, E0, E0], ctx=ctx)
        eq = g.sb("eq", [P, TC, E0, E0], ctx=ctx)
        wts = g.sb("wts", [P, NT, E0], ctx=ctx)
        wtsT = g.sb("wtsT", [E0, 2, CH], ctx=ctx)
        ln = Norm(g, n)
        w_in, w_in2, gmade, chain, gexp, shifted, wready, wT, wTc, ymade, yused, xup = (g.sem(f"f{n}_{k}") for k in (
            "w_in", "w_in2", "gmade", "chain", "gexp", "shifted", "wready", "wT", "wTc", "ymade", "yused", "xup"))
        ybank = [g.b0[:], g.b1[:], g.b2[:], g.b3[:]]
        NE = E0 // 2
        with nc.Block() as block:
            @block.sync
            def _(sp):
                sp.dma_start(wg[:], w["Wg"].rearrange("(k p) e -> p k e", p=P)).then_inc(w_in, 16)
                sp.dma_start(bg[:], w["bg"].partition_broadcast(P)).then_inc(w_in, 16)
                sp.dma_start(be[:], w["be"]).then_inc(w_in, 16)
                for k in range(KD):
                    sp.dma_start(we[:, k, :].rearrange("p (e o) -> p e o", e=E0),
                                 w["We"][:, k * P:(k + 1) * P, :].rearrange("e p o -> p e o")).then_inc(w_in2, 16)

            @block.tensor
            def _(pe):
                pe.wait_ge(w_in, 48)
                for c in range(NC):
                    ln.tensor(pe, c)
                    pe.wait_ge(ln.xnT, TC * (c + 1))
                    if c:
                        pe.wait_ge(wTc, c)
                    for t in range(TC * c, TC * c + TC):
                        last = acc(pe, g.b6[:, E0 * (t % TC):E0 * (t % TC) + E0],
                                   [(g.xnT[:, k, t * P:(t + 1) * P], wg[:, k, :]) for k in range(KD)])
                    last.then_inc(gmade, 1)
                    if c == 0:
                        pe.wait_ge(w_in2, 32)
                    for t in range(TC * c, TC * c + TC):
                        for j in range(NE):
                            i = NE * t + j
                            if i >= NE:
                                pe.wait_ge(yused, i - NE + 1)
                            acc(pe, ybank[j], [(g.xnT[:, k, t * P:(t + 1) * P], we[:, k, 512 * j:512 * j + 512])
                                               for k in range(KD)]).then_inc(ymade, 1)
                        if t % TC == 0:
                            pe.wait_ge(wready, c + 1)
                            for q in range(TC):
                                last = pe.transpose(g.b6[0:E0, P * q:P * q + P], wts[:, TC * c + q, :], g.ident[:])
                            last.then_inc(wT, 1)
                            pe.wait_ge(wTc, c + 1)
                        if t:
                            pe.wait_ge(xup, t)
                        pe.matmul(g.b7[:, 0:D], wtsT[:, c % 2, P * (t % TC):P * (t % TC) + P], be[:],
                                  start=True, stop=True).then_inc(ymade, 1)

            @block.scalar
            def _(act):
                for c in range(NC):
                    ln.scalar(act, c)
                    act.wait_ge(shifted, c + 1)
                    act.activation(gate[:], gate[:], ACT.Exp).then_inc(gexp, 1)
                    act.wait_ge(wT, c + 1)
                    act.activation(wtsT[:, c % 2, :], g.b6[0:E0, :], ACT.Copy).then_inc(wTc, 1)

            @block.gpsimd
            def _(pool):
                ln.gpsimd(pool)

            @block.vector
            def _(v):
                count = [0]

                def step(ins):
                    count[0] += 1
                    ins.then_inc(chain, 1)
                    v.wait_ge(chain, count[0])

                ln.vector(v, lambda c: None)
                v.wait_ge(w_in, 48)
                for c in range(NC):
                    v.wait_ge(gmade, c + 1)
                    step(v.tensor_tensor(gate[:], g.b6[:, 0:TC * E0].rearrange("p (t e) -> p t e", e=E0),
                                         bg[:].unsqueeze(1).broadcast_to([P, TC, E0]), ALU.add))
                    step(v.tensor_reduce(top[:], gate[:], AX.X, ALU.max))
                    step(rank_select(v, step, gate[:], g.tie8[:], sel[:], cmp[:], eq[:], E0, TOP0))
                    v.tensor_tensor(gate[:], gate[:], top[:].unsqueeze(2).broadcast_to([P, TC, E0]),
                                    ALU.subtract).then_inc(shifted, 1)
                    v.wait_ge(gexp, c + 1)
                    step(v.tensor_tensor(gate[:], gate[:], sel[:], ALU.mult))
                    step(v.tensor_reduce(top[:], gate[:], AX.X, ALU.add))
                    step(v.reciprocal(top[:], top[:]))
                    v.tensor_tensor(wts[:, TC * c:TC * c + TC, :], gate[:],
                                    top[:].unsqueeze(2).broadcast_to([P, TC, E0]), ALU.mult).then_inc(wready, 1)
                    v.wait_ge(wready, c + 1)
                    for t in range(TC * c, TC * c + TC):
                        for e in range(E0):
                            j = e // 2
                            if e % 2 == 0:
                                v.wait_ge(ymade, (NE + 1) * t + j + 1)
                            ins = v.scalar_tensor_tensor(
                                out=g.x[:, t, :], in0=ybank[j][:, D * (e % 2):D * (e % 2) + D],
                                scalar=wts[:, t, e:e + 1], in1=g.x[:, t, :], op0=ALU.mult, op1=ALU.add)
                            if e % 2:
                                ins.then_inc(yused, 1)
                                v.wait_ge(yused, NE * t + j + 1)
                            else:
                                step(ins)
                        v.wait_ge(ymade, (NE + 1) * (t + 1))
                        v.tensor_tensor(g.x[:, t, :], g.b7[:, 0:D], g.x[:, t, :], ALU.add).then_inc(xup, 1)


U = 32


def recurrence(g, n, w):
    g.stage = f"r{n}_"
    nc = g.nc
    with ExitStack() as ctx:
        norm_buffers(g, ctx)
        wi = g.sb("wi", [P, KD, D], ctx=ctx)
        wh = g.sb("wh", [P, KD, D], ctx=ctx)
        whr = g.sb("whr", [P, KD, D], ctx=ctx)
        whp = g.sb("whp", [P, 3, KD, D], BF16, ctx=ctx)
        bb = g.sb("bb", [P, 3, KD], ctx=ctx)
        xi = g.sb("xi", [P, 2, CH], ctx=ctx)
        xip = g.sb("xip", [P, 3, KD, B, S + U], BF16, ctx=ctx)
        hr = g.sb("hr", [P, 2, KD, B, U], ctx=ctx)
        hp16 = g.sb("hp16", [P, 2, 2, KD, B], F16, ctx=ctx)
        ln = Norm(g, n)
        w_in, wprep, pre, made, left, part1, part2, part3, copied = (g.sem(f"r{n}_{k}") for k in (
            "w_in", "wprep", "pre", "made", "left", "part1", "part2", "part3", "copied"))
        h_ready, hi_ready, lo_ready, summed = ([g.sem(f"r{n}_{k}{m}") for m in range(KD)] for k in (
            "h_ready", "hi_ready", "lo_ready", "summed"))
        in_banks = (g.b6, g.b7)
        jobs = [(c, m) for c in range(NC) for m in range(KD)]

        def bank(m, half, parity):
            return (g.b0, g.b1, g.b2, g.b3, g.b4, g.b5, g.b6, g.b7)[4 * m + 2 * half + parity][
                :, 0:B * U // 2].rearrange("p (b t) -> p b t", b=B)

        def xi_part(q, job):
            c, m = job
            return xip[:, q, m, c // 2, CH * (c % 2):CH * (c % 2) + CH]

        with nc.Block() as block:
            @block.sync
            def _(sp):
                sp.dma_start(wi[:], w["WiT"].rearrange("(k p) n -> p k n", p=P)).then_inc(w_in, 16)
                with nc.allow_non_contiguous_dma("256 biases"):
                    sp.dma_start(bb[:, 0, :], w["bi"].rearrange("(k p) -> p k", p=P)).then_inc(w_in, 16)
                    sp.dma_start(bb[:, 1, :], w["bh"].rearrange("(k p) -> p k", p=P)).then_inc(w_in, 16)
                sp.dma_start(wh[:], w["WhT"].rearrange("(k p) n -> p k n", p=P)).then_inc(w_in, 16)

            @block.tensor
            def _(pe):
                pe.wait_ge(w_in, 64)
                for i, (c, m) in enumerate(jobs):
                    if m == 0:
                        ln.tensor(pe, c)
                        pe.wait_ge(ln.xnT, TC * (c + 1))
                    if i >= 2:
                        pe.wait_ge(left, i - 1)
                    acc(pe, in_banks[i % 2][:], [(wi[:, k, m * P:(m + 1) * P], g.xnT[:, k, CH * c:CH * c + CH])
                                                 for k in range(KD)]).then_inc(made, 1)
                pe.wait_ge(part3, len(jobs))
                pe.wait_ge(wprep, 5)
                pe.wait_ge(pre, 1)

                def inputs(half, it, m, parity):
                    for q in range(3):
                        x = xip[:, q, m].rearrange("p b (s two) -> p b s two", two=2)
                        pe.matmul(bank(m, half, parity), g.identb[:],
                                  x[:, :, bass.ds(it * U + half * (U // 2), U // 2), parity],
                                  start=(q == 0), stop=True, skip_group_check=True)

                groups = [(0, 0, 0, (0, 1, 2)), (0, 0, 1, (0, 1, 2)), (1, 0, 0, (0, 1, 2)), (1, 0, 1, (2,)),
                          (0, 1, 0, (0, 1)), (0, 1, 1, (0, 1)), (1, 1, 0, (0, 1)),
                          (1, 0, 1, (1, 0)), (1, 1, 1, (0, 1))]
                ready = (hi_ready, lo_ready)
                for m in range(KD):
                    for parity in range(2):
                        inputs(0, 0, m, parity)
                with pe.Fori(0, S // (2 * U)) as it:
                    for half in range(2):
                        for t in range(U):
                            at = it * (2 * U) + (half * U + t + 1)
                            waited = set()
                            for k, q, m, parts in groups:
                                if (k, q) not in waited:
                                    pe.wait_ge(ready[q][k], at)
                                    waited.add((k, q))
                                for a in parts:
                                    last = pe.matmul(bank(m, half, t % 2)[:, :, t // 2],
                                                     whp[:, a, k, m * P:(m + 1) * P], hp16[:, (t + 1) % 2, q, k, :],
                                                     start=False, stop=True, skip_group_check=True)
                                if (k, q) == (1, 1):
                                    last.then_inc(summed[m], 1)
                            if t in (4, 8, 12, 16):
                                piece = t // 4 - 1
                                inputs(1 - half, it + half, piece // 2, piece % 2)

            @block.scalar
            def _(act):
                act.wait_ge(w_in, 64)
                act.activation(whp[:, 0], wh[:], ACT.Copy).then_inc(wprep, 1)
                act.wait_ge(wprep, 2)
                for i, (c, m) in enumerate(jobs):
                    if m == 0:
                        ln.scalar(act, c)
                    act.wait_ge(made, i + 1)
                    if i >= 2:
                        act.wait_ge(part3, i - 1)
                    act.activation(xi[:, i % 2, :], in_banks[i % 2][:], ACT.Identity,
                                   bias=bb[:, 2, m:m + 1]).then_inc(left, 1)
                with act.Fori(0, S // (2 * U)) as it:
                    for half in range(2):
                        act.wait_ge(copied, it * 2 + (half + 1))
                        for t in range(U):
                            for m in range(KD):
                                act.wait_ge(summed[m], it * (2 * U) + (half * U + t + 1))
                                x = bank(m, half, t % 2)[:, :, t // 2]
                                act.activation(hp16[:, t % 2, 0, m, :], x, ACT.Tanh).then_inc(hi_ready[m], 1)
                                act.activation(hr[:, half, m, :, t], x, ACT.Tanh).then_inc(h_ready[m], 1)

            @block.vector
            def _(v):
                v.wait_ge(w_in, 64)
                v.wait_ge(wprep, 1)
                v.tensor_tensor(bb[:, 2, :], bb[:, 0, :], bb[:, 1, :], ALU.add).then_inc(wprep, 1)
                v.tensor_tensor(whr[:], wh[:], whp[:, 0], ALU.subtract).then_inc(wprep, 1)
                v.wait_ge(wprep, 3)
                v.tensor_copy(whp[:, 1], whr[:]).then_inc(wprep, 1)
                v.wait_ge(wprep, 4)
                v.tensor_tensor(whp[:, 2], whr[:], whp[:, 1], ALU.subtract).then_inc(wprep, 1)
                ln.vector(v, lambda c: None)
                for i, job in enumerate(jobs):
                    v.wait_ge(left, i + 1)
                    x = xi[:, i % 2, :]
                    v.tensor_copy(xi_part(0, job), x).then_inc(part1, 1)
                    v.wait_ge(part1, i + 1)
                    v.tensor_tensor(x, x, xi_part(0, job), ALU.subtract).then_inc(part2, 1)
                    v.wait_ge(part2, 2 * i + 1)
                    v.tensor_copy(xi_part(1, job), x).then_inc(part2, 1)
                with v.Fori(0, S // (2 * U)) as it:
                    for half in range(2):
                        for t in range(U):
                            for k in range(KD):
                                v.wait_ge(h_ready[k], it * (2 * U) + (half * U + t + 1))
                                v.tensor_tensor(hp16[:, t % 2, 1, k, :], hr[:, half, k, :, t], hp16[:, t % 2, 0, k, :],
                                                ALU.subtract).then_inc(lo_ready[k], 1)

            @block.gpsimd
            def _(pool):
                ln.gpsimd(pool)
                pool.memset(xip[:, :, :, :, S:S + U].rearrange("p q m b t -> p (q m b) t"), 0.0).then_inc(pre, 1)
                for k in range(KD):
                    pool.memset(hp16[:, 1, 0, k], 0.0).then_inc(hi_ready[k], 1)
                    pool.memset(hp16[:, 1, 1, k], 0.0).then_inc(lo_ready[k], 1)
                pool.memset(g.hist[:, 0, 0, 0:U], 0.0).then_inc(copied, 1)
                pool.memset(g.hist[:, 0, 0, U:2 * U], 0.0).then_inc(copied, 1)
                for i, job in enumerate(jobs):
                    pool.wait_ge(part2, 2 * (i + 1))
                    pool.tensor_tensor(xi_part(2, job), xi[:, i % 2, :], xi_part(1, job),
                                       ALU.subtract).then_inc(part3, 1)
                pool.wait_ge(copied, 2)
                with pool.Fori(0, S // (2 * U)) as it:
                    for half in range(2):
                        for k in range(KD):
                            pool.wait_ge(h_ready[k], it * (2 * U) + (half + 1) * U)
                        t0 = it * (2 * U) + half * U
                        pool.tensor_copy(g.hist[:, :, :, bass.ds(t0, U)], hr[:, half]).then_inc(copied, 1)


def gated_experts(g, n, w, out):
    g.stage = f"e{n}_"
    nc = g.nc
    with ExitStack() as ctx:
        norm_buffers(g, ctx)
        wr = g.sb("wr", [P, KD, E1], ctx=ctx)
        wg = g.sb("wgate", [P, KD, HID], ctx=ctx)
        wu = g.sb("wup", [P, KD, HID], ctx=ctx)
        wd = g.sb("wdown", [P, MH, D], ctx=ctx)
        cb = g.sb("cb", [P, E1], ctx=ctx)
        sc = g.sb("sc", [P, TC, E1], ctx=ctx)
        sb = g.sb("sb", [P, TC, E1], ctx=ctx)
        prs = g.sb("prs", [P, TC, G1, 6], ctx=ctx)
        gs = g.sb("gs", [P, TC, G1], ctx=ctx)
        gm = g.sb("gm", [P, TC, G1], ctx=ctx)
        gmn = g.sb("gmn", [P, TC, G1], ctx=ctx)
        gc = g.sb("gc", [P, TC, G1, G1], ctx=ctx)
        ge = g.sb("ge", [P, TC, G1, G1], ctx=ctx)
        cmp = g.sb("cmp1", [P, TC, E1, E1], ctx=ctx)
        eq = g.sb("eq1", [P, TC, E1, E1], ctx=ctx)
        sel = g.sb("sel1", [P, TC, E1], ctx=ctx)
        tot = g.sb("tot", [P, TC], ctx=ctx)
        comb = g.sb("comb", [P, 2, TC, E1], ctx=ctx)
        cp1 = g.sb("cp1", [E1, CH], BF16, ctx=ctx)
        cr = g.sb("cr", [E1, CH], ctx=ctx)
        cp2 = g.sb("cp2", [E1, CH], BF16, ctx=ctx)
        cps = g.sb("cps", [P, 2, CH], BF16, ctx=ctx)
        sg = g.sb("sg", [P, 2, CH], ctx=ctx)
        hT = g.sb("hT", [P, 2, MH, CH], ctx=ctx)
        ln = Norm(g, n)
        (w_in, w_in2, logits, scored, chain, combed, cT, c1, parted, gmade, umade, bmade, sgd, hmul, hready, ymade,
         xup, stored, zero) = (g.sem(f"e{n}_{k}") for k in (
             "w_in", "w_in2", "logits", "scored", "chain", "combed", "cT", "c1", "parted", "gmade", "umade", "bmade",
             "sgd", "hmul", "hready", "ymade", "xup", "stored", "zero"))
        NR = MH - MS
        KR = 2 * QD + E1
        with nc.Block() as block:
            @block.sync
            def _(sp):
                sp.dma_start(wr[:], w["router"].rearrange("(k p) e -> p k e", p=P)).then_inc(w_in, 16)
                sp.dma_start(cb[:], w["cbias"].partition_broadcast(P)).then_inc(w_in, 16)
                sp.dma_start(wg[:], w["gate"].rearrange("(k p) n -> p k n", p=P)).then_inc(w_in, 16)
                sp.dma_start(wu[:], w["up"].rearrange("(k p) n -> p k n", p=P)).then_inc(w_in, 16)
                sp.dma_start(wd[:], w["down"].rearrange("(m p) n -> p m n", p=P)).then_inc(w_in2, 16)
                ov = out.rearrange("(t p) d -> p t d", p=P)
                for c in range(NC):
                    sp.wait_ge(xup, TC * (c + 1))
                    sp.dma_start(ov[:, TC * c:TC * c + TC, :], g.x[:, TC * c:TC * c + TC, :]).then_inc(stored, 16)
                sp.wait_ge(stored, 16 * NC)

            @block.tensor
            def _(pe):
                pe.wait_ge(w_in, 64)
                for c in range(NC):
                    ln.tensor(pe, c)
                pe.wait_ge(ln.xnT, NT)

                def route(c):
                    if c:
                        pe.wait_ge(parted, 2 * c)
                    for t in range(TC):
                        last = acc(pe, g.b7[:, E1 * t:E1 * t + E1],
                                   [(g.xnT[:, k, CH * c + P * t:CH * c + P * t + P], wr[:, k, :]) for k in range(KD)])
                    last.then_inc(logits, 1)

                def turn(c):
                    pe.wait_ge(combed, c + 1)
                    for t in range(TC):
                        last = pe.transpose(g.b7[0:E1, P * t:P * t + P], comb[:, c % 2, t, :], g.ident[:])
                    last.then_inc(cT, 1)

                def down(c):
                    pe.wait_ge(w_in2, 16)
                    pe.wait_ge(hready, MH * (c + 1))
                    for t in range(TC * c, TC * c + TC):
                        if t >= 2:
                            pe.wait_ge(xup, t - 1)
                        acc(pe, (g.b4, g.b5)[t % 2][:, 0:D],
                            [(hT[:, c % 2, m, P * (t % TC):P * (t % TC) + P], wd[:, m, :])
                             for m in range(MH)]).then_inc(ymade, 1)

                route(0)
                for c in range(NC):
                    for m in range(MH):
                        i = MH * c + m
                        if i >= 2:
                            pe.wait_ge(sgd, i - 1)
                        cols = slice(m * P, (m + 1) * P)
                        acc(pe, (g.b0, g.b1)[i % 2][:], [(wg[:, k, cols], g.xnT[:, k, CH * c:CH * c + CH])
                                                      for k in range(KD)]).then_inc(gmade, 1)
                        if i >= 2:
                            pe.wait_ge(hmul, i - 1)
                        acc(pe, (g.b2, g.b3)[i % 2][:], [(wu[:, k, cols], g.xnT[:, k, CH * c:CH * c + CH])
                                                      for k in range(KD)]).then_inc(umade, 1)
                        if m == MS - 1:
                            turn(c)
                        if m >= MS:
                            pe.wait_ge(parted, 2 * (c + 1))
                            j = NR * c + m - MS
                            if j:
                                pe.wait_ge(hready, MH * ((j - 1) // NR) + MS + (j - 1) % NR + 1)
                            pe.matmul(g.b6[:], g.sel_pair[0:KR, m - MS, :], cps[0:KR, c % 2, :],
                                      start=True, stop=True).then_inc(bmade, 1)
                    if c + 1 < NC:
                        route(c + 1)
                    if c:
                        down(c - 1)
                down(NC - 1)

            @block.scalar
            def _(act):
                for c in range(NC):
                    ln.scalar(act, c)

                def scores(c):
                    act.wait_ge(logits, c + 1)
                    if c:
                        act.wait_ge(combed, c)
                    act.activation(sc[:].rearrange("p t e -> p (t e)"), g.b7[:, 0:TC * E1],
                                   ACT.Sigmoid).then_inc(scored, 1)

                scores(0)
                for c in range(NC):
                    for m in range(MH):
                        i = MH * c + m
                        act.wait_ge(gmade, i + 1)
                        if i >= 2:
                            act.wait_ge(hmul, i - 1)
                        act.activation(sg[:, i % 2, :], (g.b0, g.b1)[i % 2][:], ACT.Silu).then_inc(sgd, 1)
                        if m == MS - 1:
                            act.wait_ge(cT, c + 1)
                            act.activation(cp1[:], g.b7[0:E1, :], ACT.Copy).then_inc(c1, 1)
                    if c + 1 < NC:
                        scores(c + 1)

            @block.gpsimd
            def _(pool):
                pool.memset(cps[:].rearrange("p a n -> p (a n)"), 0.0).then_inc(zero, 1)
                ln.gpsimd(pool)

            @block.vector
            def _(v):
                ln.vector(v, lambda c: None)
                v.wait_ge(w_in, 64)
                v.wait_ge(zero, 1)
                count = [0]

                def step(ins):
                    count[0] += 1
                    ins.then_inc(chain, 1)
                    v.wait_ge(chain, count[0])

                def wide(ap, e):
                    return ap.unsqueeze(3).broadcast_to([P, TC, G1, e])

                def choose(c):
                    v.wait_ge(scored, c + 1)
                    step(v.tensor_tensor(sb[:], sc[:], cb[:].unsqueeze(1).broadcast_to([P, TC, E1]), ALU.add))
                    sg4 = sb[:].rearrange("p t (q e) -> p (t q) e", q=G1)
                    pv = prs[:].rearrange("p t q s -> p (t q) s")
                    step(v.tensor_tensor(pv[:, :, 0:3], sg4[:, :, 0:3], sg4[:, :, 1:4], ALU.add))
                    step(v.tensor_tensor(pv[:, :, 3:5], sg4[:, :, 0:2], sg4[:, :, 2:4], ALU.add))
                    step(v.tensor_tensor(pv[:, :, 5:6], sg4[:, :, 0:1], sg4[:, :, 3:4], ALU.add))
                    step(v.tensor_reduce(gs[:].rearrange("p t q -> p (t q)"), pv, AX.X, ALU.max))
                    step(rank_select(v, step, gs[:], g.tie16[:, 0:G1, 0:G1], gm[:], gc[:], ge[:], G1, 2))
                    step(v.tensor_scalar(gmn[:], gm[:], 1.0, BIG, ALU.subtract, ALU.mult))
                    s4 = sb[:].rearrange("p t (q e) -> p t q e", q=G1)
                    step(v.tensor_tensor(s4, s4, wide(gm[:], EPG), ALU.mult))
                    step(v.tensor_tensor(s4, s4, wide(gmn[:], EPG), ALU.add))
                    step(rank_select(v, step, sb[:], g.tie16[:], sel[:], cmp[:], eq[:], E1, TOP1))
                    step(v.tensor_tensor(sel[:], sel[:], sc[:], ALU.mult))
                    step(v.tensor_reduce(tot[:], sel[:], AX.X, ALU.add))
                    step(v.tensor_scalar(tot[:], tot[:], 1e-20, None, ALU.add))
                    step(v.reciprocal(tot[:], tot[:]))
                    v.tensor_tensor(comb[:, c % 2], sel[:], tot[:].unsqueeze(2).broadcast_to([P, TC, E1]),
                                    ALU.mult).then_inc(combed, 1)

                def parts(c):
                    v.wait_ge(c1, c + 1)
                    v.tensor_tensor(cr[:], g.b7[0:E1, :], cp1[:], ALU.subtract).then_inc(parted, 1)
                    v.wait_ge(parted, 2 * c + 1)
                    step(v.tensor_copy(cp2[:], cr[:]))
                    step(v.tensor_copy(cps[0:E1, c % 2, :], cp1[:]))
                    step(v.tensor_copy(cps[QD:QD + E1, c % 2, :], cp2[:]))
                    v.tensor_tensor(cps[2 * QD:2 * QD + E1, c % 2, :], cr[:], cp2[:], ALU.subtract).then_inc(parted, 1)

                def finish(c):
                    for t in range(TC * c, TC * c + TC):
                        v.wait_ge(ymade, t + 1)
                        v.tensor_tensor(g.x[:, t, :], (g.b4, g.b5)[t % 2][:, 0:D], g.x[:, t, :],
                                        ALU.add).then_inc(xup, 1)

                choose(0)
                for c in range(NC):
                    for m in range(MH):
                        i = MH * c + m
                        v.wait_ge(sgd, i + 1)
                        v.wait_ge(umade, i + 1)
                        if c >= 2 and m == 0:
                            v.wait_ge(ymade, TC * (c - 1))
                        h = hT[:, c % 2, m, :]
                        ins = v.tensor_tensor(h, sg[:, i % 2, :], (g.b2, g.b3)[i % 2][:], ALU.mult)
                        ins.then_inc(hmul, 1)
                        v.wait_ge(hmul, i + 1)
                        if m < MS:
                            v.tensor_copy(h[:, 0:1], h[:, 0:1]).then_inc(hready, 1)
                        else:
                            v.wait_ge(bmade, NR * c + m - MS + 1)
                            v.tensor_tensor(h, h, g.b6[:], ALU.mult).then_inc(hready, 1)
                        if m == MS - 1:
                            parts(c)
                    if c + 1 < NC:
                        choose(c + 1)
                    if c:
                        finish(c - 1)
                finish(NC - 1)


def decoder(nc, a, out):
    with ExitStack() as ctx:
        g = Prog(nc, ctx)
        g.b0, g.b1, g.b2, g.b3, g.b4, g.b5, g.b6, g.b7 = (
            ctx.enter_context(nc.psum_tensor(f"b{i}", [P, 512], F32)) for i in range(8))
        g.x = g.sb("x", [P, NT, D])
        g.q_scr = nc.dram_tensor("q_scr", (3, D, B * S), BF16)
        g.k_scr = nc.dram_tensor("k_scr", (3, D, B * S), BF16)
        g.kc_scr = nc.dram_tensor("kc_scr", (3, D, B * M2), BF16)
        g.wo_dram = {0: a["L0_attn_wo"], 1: a["L0_xattn_wo"], 4: a["L1_xattn_wo"]}
        constants(g)
        stage = DEBUG_STAGES
        with ExitStack() as inner:
            g.stage = "self_"
            g.va = g.sb("va", [P, NT, H, QD], ctx=inner)
            st = Stacks(g, 0, True, False, inner)
            project(g, 0, {"x": a["x"], "wqkv": a["L0_attn_wqkvT"]}, True, st)
            if stage > 0:
                attention(g, 0, True, st)
        g.stage = "ctx_"
        g.vc = g.sb("vc", [P, B, H, QD])
        if stage > 1:
            w = {"ctxT": a["ctxT"], "wq": a["L0_xattn_Wq"], "wk": a["L0_xattn_Wk"], "wv": a["L0_xattn_Wv"],
                 "bq": None, "bo": None, "mask": a["mask"]}
            with ExitStack() as inner:
                g.stage = "ctx0_"
                st = Stacks(g, 1, False, True, inner)
                project(g, 1, w, False, st)
                attention(g, 1, False, st, w)
        if stage > 2:
            linear_experts(g, 2, {"Wg": a["L0_ffn_Wg"], "bg": a["L0_ffn_bg"], "We": a["L0_ffn_We"], "be": a["L0_ffn_be"]})
        g.hist = g.sb("hist", [P, KD, B, S])
        g.recycle()
        if stage > 3:
            recurrence(g, 3, {"WiT": a["L1_attn_WiT"], "WhT": a["L1_attn_WhT"], "bi": a["L1_attn_bi"], "bh": a["L1_attn_bh"]})
        if stage > 4:
            g.recycle()
            w = {"ctxT": a["ctxT"], "wq": a["L1_xattn_wq"], "wk": a["L1_xattn_wk"], "wv": a["L1_xattn_wv"],
                 "bq": a["L1_xattn_bq"], "bk": a["L1_xattn_bk"], "bv": a["L1_xattn_bv"], "bo": a["L1_xattn_bo"],
                 "mask": None}
            with ExitStack() as inner:
                g.stage = "ctx1_"
                st = Stacks(g, 4, False, False, inner)
                project(g, 4, w, False, st)
                attention(g, 4, False, st, w)
        if stage > 5:
            gated_experts(g, 5, {"router": a["router"], "cbias": a["cbias"], "gate": a["gate"], "up": a["up"],
                                 "down": a["down"]}, out)
        else:
            s_out = g.sem("s_out")
            with nc.Block() as block:
                @block.sync
                def _(sp):
                    sp.dma_start(out.rearrange("(t p) d -> p t d", p=P), g.x[:]).then_inc(s_out, 16)
                    sp.wait_ge(s_out, 16)


DEBUG_STAGES = 6


def _layout(i):
    def by_feature(w):
        return w.transpose(1, 0, 2).reshape(w.shape[1], -1)

    return {
        "x": i["x"].reshape(B * S, D),
        "ctxT": i["ctx_768"].reshape(B * M2, C2).T,
        "mask": i["mask_BxS2_bf1"].reshape(B * M2).view(np.uint8),
        "L0_attn_wqkvT": i["L0_attn_w_qkv"].T,
        "L0_attn_wo": i["L0_attn_w_proj"].T,
        "L0_xattn_Wq": i["L0_xattn_Wq"], "L0_xattn_Wk": i["L0_xattn_Wk"], "L0_xattn_Wv": i["L0_xattn_Wv"],
        "L0_xattn_wo": i["L0_xattn_Wo"],
        "L0_ffn_Wg": i["L0_ffn_Wg"], "L0_ffn_bg": i["L0_ffn_bg"], "L0_ffn_We": i["L0_ffn_We"], "L0_ffn_be": i["L0_ffn_be"],
        "L1_attn_WiT": i["L1_attn_Wi"].T, "L1_attn_WhT": i["L1_attn_Wh"].T,
        "L1_attn_bi": i["L1_attn_bi"], "L1_attn_bh": i["L1_attn_bh"],
        "L1_xattn_wq": i["L1_xattn_wq"], "L1_xattn_wk": i["L1_xattn_wk"], "L1_xattn_wv": i["L1_xattn_wv"],
        "L1_xattn_bq": i["L1_xattn_bq"], "L1_xattn_bk": i["L1_xattn_bk"], "L1_xattn_bv": i["L1_xattn_bv"],
        "L1_xattn_wo": i["L1_xattn_wo"], "L1_xattn_bo": i["L1_xattn_bo"],
        "router": i["L1_ffn_router_w"].T, "cbias": i["L1_ffn_correction_bias"],
        "gate": np.concatenate([i["L1_ffn_shared_gate_w"].T, by_feature(i["L1_ffn_gate_w"])], axis=1),
        "up": np.concatenate([i["L1_ffn_shared_up_w"].T, by_feature(i["L1_ffn_up_w"])], axis=1),
        "down": np.concatenate([i["L1_ffn_shared_down_w"].T, i["L1_ffn_down_w"].reshape(E1 * 64, D)], axis=0),
    }


def kernel(**inputs):
    import concourse.bacc as bacc
    from concourse.bass_utils import run_bass_kernel_spmd

    nc = bacc.Bacc("TRN2", target_bir_lowering=False, num_devices=1)
    arrays, aps = {}, {}
    for name, value in _layout({k: np.asarray(v) for k, v in inputs.items()}).items():
        value = np.ascontiguousarray(value)
        arrays[f"in_{name}"] = value
        aps[name] = nc.dram_tensor(f"in_{name}", value.shape, mybir.dt.from_np(value.dtype), kind="ExternalInput").ap()
    out = nc.dram_tensor("out", (B * S, D), F32, kind="ExternalOutput").ap()
    decoder(nc, aps, out)
    r = run_bass_kernel_spmd(nc, [arrays], core_ids=[0])
    return r.results[0]["out"].reshape(B, S, D)
```

```python
from contextlib import ExitStack

import numpy as np

import concourse.bass as bass
from concourse import mybir

F32 = mybir.dt.float32
BF16 = mybir.dt.bfloat16
F16 = mybir.dt.float16
F32R = mybir.dt.float32r
U8 = mybir.dt.uint8
ALU = mybir.AluOpType
ACT = mybir.ActivationFunctionType
AX = mybir.AxisListType

P = 128
B, S, D = 2, 1024, 256
KD = D // P
NT = B * S // P
TC = 4
NC = NT // TC
CH = TC * P
H, DH = 16, 16
HG = 4
NG = H // HG
QD = 32
M2, C2 = 77, 192
CK = C2 // 2
SCALE = float(DH) ** -0.5
BIG = float(2.0 ** 100)
EPS = 1e-5
COMBOS = [(0, 0), (0, 1), (1, 0), (0, 2), (1, 1), (2, 0)]
R_EXTRA = len(COMBOS) * DH
E0, TOP0 = 8, 2
E1, G1, TOP1 = 16, 4, 4
EPG = E1 // G1
HID = 512 + E1 * 64
MH = HID // P
MS = 512 // P


class Prog:

    def __init__(self, nc, ctx):
        self.nc, self.ctx, self.stage = nc, ctx, ""
        self.sems = []

    def sb(self, name, shape, dt=F32, ctx=None):
        return (ctx or self.ctx).enter_context(self.nc.sbuf_tensor(self.stage + name, shape, dt))

    def sem(self, name):
        self.sems.append(self.nc.alloc_semaphore(name=name))
        return self.sems[-1]

    def recycle(self):
        self.nc.clear_and_free_semaphores(self.sems)
        self.nc.all_engine_barrier()
        self.sems = []


def acc(pe, out, pairs):
    for n, (lhs, rhs) in enumerate(pairs):
        last = pe.matmul(out, lhs, rhs, start=(n == 0), stop=(n == len(pairs) - 1))
    return last


def constants(g, x):
    nc = g.nc
    g.ident = g.sb("ident", [P, P])
    g.identb = g.sb("identb", [P, P], BF16)
    g.mask_qk = g.sb("mask_qk", [P, P], BF16)
    g.mask_kq = g.sb("mask_kq", [P, P], BF16)
    g.neg_half = g.sb("neg_half", [P, NT])
    g.tie8 = g.sb("tie8", [P, E0, E0])
    g.tie16 = g.sb("tie16", [P, E1, E1])
    g.sel_pair = g.sb("sel_pair", [P, MH - MS, P], BF16)
    g.x_in = [g.sem(f"x_in{c}") for c in range(NC)]
    zeroed, filled = g.sem("zeroed"), g.sem("filled")
    with nc.Block() as block:
        @block.sync
        def _(sp):
            xv = x.rearrange("(t p) d -> p t d", p=P)
            for c in range(NC):
                sp.dma_start(g.x[:, TC * c:TC * c + TC, :], xv[:, TC * c:TC * c + TC, :]).then_inc(g.x_in[c], 16)

        @block.vector
        def _(v):
            for t, value in ((g.ident, 0.0), (g.identb, 0.0), (g.mask_qk, 0.0), (g.mask_kq, 0.0), (g.neg_half, -0.5)):
                v.memset(t[:], value).then_inc(zeroed, 1)

        @block.gpsimd
        def _(pool):
            pool.wait_ge(zeroed, 5)
            for t in (g.ident, g.identb):
                pool.affine_select(out=t[:], in_=t[:], compare_op=ALU.not_equal, fill=1.0, base=0,
                                   pattern=[[-1, P]], channel_multiplier=1).then_inc(filled, 1)
            pool.affine_select(out=g.mask_qk[:], in_=g.mask_qk[:], compare_op=ALU.is_ge, fill=-BIG, base=0,
                               pattern=[[-1, P]], channel_multiplier=1).then_inc(filled, 1)
            pool.affine_select(out=g.mask_kq[:], in_=g.mask_kq[:], compare_op=ALU.is_ge, fill=-BIG, base=0,
                               pattern=[[1, P]], channel_multiplier=-1).then_inc(filled, 1)


def routing_constants(g, pool, zeroed, filled):
    for t, value in ((g.tie8, 1.0), (g.tie16, 1.0), (g.sel_pair, 0.0)):
        pool.memset(t[:], value).then_inc(zeroed, 1)
    pool.wait_ge(zeroed, 3)
    for t, e in ((g.tie8, E0), (g.tie16, E1)):
        pool.affine_select(out=t[:], in_=t[:], compare_op=ALU.is_ge, fill=0.0, base=-1,
                           pattern=[[1, e], [-1, e]], channel_multiplier=0).then_inc(filled, 1)
    for n in range(3):
        v = g.sel_pair[:].rearrange("p m (a i) -> p m a i", a=2)
        pool.affine_select(out=v, in_=v, compare_op=ALU.not_equal, fill=1.0, base=-QD * n,
                           pattern=[[-2, MH - MS], [-1, 2], [0, 64]], channel_multiplier=1).then_inc(filled, 1)
        pool.wait_ge(filled, 3 + n)


class ExpertWeights0:

    def __init__(self, g, ctx, a):
        self.wg = g.sb("wg", [P, KD, E0], ctx=ctx)
        self.we = g.sb("we", [P, KD, E0 * D], ctx=ctx)
        self.be = g.sb("be", [E0, D], ctx=ctx)
        self.bg = g.sb("bg", [P, E0], ctx=ctx)
        self.we_hi = g.sb("we_hi", [P, KD, E0 * D], F32R, ctx=ctx)
        self.we_lo = g.sb("we_lo", [P, KD, E0 * D], F32R, ctx=ctx)
        self.a, self.came, self.count = a, g.sem("experts0_came"), 16 * (3 + KD)
        self.split = g.sem("experts0_split")

    def load(self, sp):
        sp.dma_start(self.wg[:], self.a["L0_ffn_Wg"].rearrange("(k p) e -> p k e", p=P)).then_inc(self.came, 16)
        sp.dma_start(self.bg[:], self.a["L0_ffn_bg"].partition_broadcast(P)).then_inc(self.came, 16)
        sp.dma_start(self.be[:], self.a["L0_ffn_be"]).then_inc(self.came, 16)
        for k in range(KD):
            sp.dma_start(self.we[:, k, :].rearrange("p (e o) -> p e o", e=E0),
                         self.a["L0_ffn_We"][:, k * P:(k + 1) * P, :].rearrange("e p o -> p e o")
                         ).then_inc(self.came, 16)

    def prepare(self, pool):
        pool.wait_ge(self.came, self.count)
        for i in range(4):
            cols = slice(i * E0 * D // 4, (i + 1) * E0 * D // 4)
            pool.tensor_copy(self.we_hi[:, :, cols], self.we[:, :, cols]).then_inc(self.split, 1)
            pool.wait_ge(self.split, 2 * i + 1)
            pool.tensor_tensor(self.we_lo[:, :, cols], self.we[:, :, cols], self.we_hi[:, :, cols], ALU.subtract
                               ).then_inc(self.split, 1)


class RecurrenceWeights:
    def __init__(self, g, ctx, a):
        self.wi = g.sb("wi", [P, KD, D], ctx=ctx)
        self.wh = g.sb("wh", [P, KD, D], ctx=ctx)
        self.bb = g.sb("bb", [P, 3, KD], ctx=ctx)
        self.nc, self.a, self.came, self.count = g.nc, a, g.sem("recurrence_came"), 16 * 4

    def load(self, sp):
        sp.dma_start(self.wi[:], self.a["L1_attn_WiT"].rearrange("(k p) n -> p k n", p=P)).then_inc(self.came, 16)
        with self.nc.allow_non_contiguous_dma("256 biases"):
            sp.dma_start(self.bb[:, 0, :], self.a["L1_attn_bi"].rearrange("(k p) -> p k", p=P)).then_inc(self.came, 16)
            sp.dma_start(self.bb[:, 1, :], self.a["L1_attn_bh"].rearrange("(k p) -> p k", p=P)).then_inc(self.came, 16)
        sp.dma_start(self.wh[:], self.a["L1_attn_WhT"].rearrange("(k p) n -> p k n", p=P)).then_inc(self.came, 16)


class ExpertWeights1:

    def __init__(self, g, ctx):
        self.wr = g.sb("wr", [P, KD, E1], ctx=ctx)
        self.cb = g.sb("cb", [P, E1], ctx=ctx)
        self.hi = [g.sb(f"hi{i}", [P, KD, HID], F32R, ctx=ctx) for i in range(2)]
        self.lo = [g.sb(f"lo{i}", [P, KD, HID], F32R, ctx=ctx) for i in range(2)]

    def stage_in(self, g, ctx, a):
        self.whole = [g.sb(f"whole{i}", [P, KD, HID], ctx=ctx) for i in range(2)]
        self.a, self.came, self.split = a, g.sem("experts1_came"), g.sem("experts1_split")
        self.count = 16 * 4

    def load(self, sp):
        for w, name in zip(self.whole, ("gate", "up")):
            sp.dma_start(w[:], self.a[name].rearrange("(k p) n -> p k n", p=P)).then_inc(self.came, 16)
        sp.dma_start(self.wr[:], self.a["router"].rearrange("(k p) e -> p k e", p=P)).then_inc(self.came, 16)
        sp.dma_start(self.cb[:], self.a["cbias"].partition_broadcast(P)).then_inc(self.came, 16)

    def prepare(self, pool):
        pool.wait_ge(self.came, self.count)
        for i, (w, hi, lo) in enumerate(zip(self.whole, self.hi, self.lo)):
            pool.tensor_copy(hi[:], w[:]).then_inc(self.split, 1)
            pool.wait_ge(self.split, 2 * i + 1)
            pool.tensor_tensor(lo[:], w[:], hi[:], ALU.subtract).then_inc(self.split, 1)


class NextStats:

    def __init__(self, g, n, updated, tile_of):
        self.g, self.updated, self.tile_of = g, updated, tile_of
        self.stats, self.meanvar, self.var_eps, self.rstd = (
            g.sem(f"s{n}_{x}") for x in ("stats", "meanvar", "var_eps", "rstd"))

    def sums(self, v, i):
        v.wait_ge(self.updated, i + 1)
        t = self.tile_of(i)
        v.bn_stats(self.g.bn[:, t, :], self.g.x[:, t, :]).then_inc(self.stats, 1)

    def mean_var(self, v, i):
        v.wait_ge(self.stats, i + 1)
        t = self.tile_of(i)
        v.bn_aggr(self.g.mv[:, t, :], self.g.bn[:, t, :]).then_inc(self.meanvar, 1)

    def vector(self, v, i):
        if i >= 1:
            self.sums(v, i - 1)
        if i >= 2:
            self.mean_var(v, i - 2)
        if i == NT - 1:
            self.sums(v, i)
            self.mean_var(v, i - 1)
            self.mean_var(v, i)
            self.add_eps(v, NC - 1)
        elif i % TC == 2 and i > TC:
            self.add_eps(v, i // TC - 1)

    def add_eps(self, v, j):
        v.wait_ge(self.meanvar, TC * (j + 1))
        t = self.tile_of(TC * j)
        v.tensor_scalar(self.g.ve[:, t:t + TC], self.g.mv[:, t:t + TC, 1], EPS, None, ALU.add).then_inc(self.var_eps, 1)

    def gpsimd(self, pool):
        for j in range(NC):
            pool.wait_ge(self.var_eps, j + 1)
            t = self.tile_of(TC * j)
            pool.tensor_tensor(self.g.rs[:, t:t + TC], self.g.ve[:, t:t + TC], self.g.neg_half[:, 0:TC],
                               ALU.pow).then_inc(self.rstd, 1)


class Norm:

    def __init__(self, g, n, with_stats=False):
        self.g, self.with_stats = g, with_stats
        if with_stats:
            self.stats, self.meanvar, self.var_eps, self.rstd = (
                g.sem(f"n{n}_{x}") for x in ("stats", "meanvar", "var_eps", "rstd"))
        self.xn, self.turned, self.xnT = g.sem(f"n{n}_xn"), g.sem(f"n{n}_turned"), g.sem(f"n{n}_xnT")

    def normalise(self, v, t):
        g = self.g
        v.tensor_scalar(g.xn[:, t, :], g.x[:, t, :], g.mv[:, t, 0:1], g.rs[:, t:t + 1],
                        ALU.subtract, ALU.mult).then_inc(self.xn, 1)

    def vector(self, v, chunk_ready=None):
        g = self.g
        if not self.with_stats:
            for t in range(NT):
                self.normalise(v, t)
            return
        for c in range(NC + 1):
            if c < NC:
                chunk_ready(c)
                for t in range(TC * c, TC * c + TC):
                    v.bn_stats(g.bn[:, t, :], g.x[:, t, :]).then_inc(self.stats, 1)
                for t in range(TC * c, TC * c + TC):
                    v.wait_ge(self.stats, t + 1)
                    v.bn_aggr(g.mv[:, t, :], g.bn[:, t, :]).then_inc(self.meanvar, 1)
                v.wait_ge(self.meanvar, TC * (c + 1))
                v.tensor_scalar(g.ve[:, TC * c:TC * c + TC], g.mv[:, TC * c:TC * c + TC, 1], EPS, None,
                                ALU.add).then_inc(self.var_eps, 1)
            if c:
                v.wait_ge(self.rstd, c)
                for t in range(TC * (c - 1), TC * c):
                    self.normalise(v, t)

    def gpsimd(self, pool):
        g = self.g
        for c in range(NC if self.with_stats else 0):
            pool.wait_ge(self.var_eps, c + 1)
            pool.tensor_tensor(g.rs[:, TC * c:TC * c + TC], g.ve[:, TC * c:TC * c + TC],
                               g.neg_half[:, 0:TC], ALU.pow).then_inc(self.rstd, 1)

    def tensor(self, pe, c):
        g = self.g
        for t in range(TC * c, TC * c + TC):
            pe.wait_ge(self.xn, t + 1)
            if t >= 2:
                pe.wait_ge(self.xnT, t - 1)
            bank = (g.b4, g.b5)[t % 2]
            for k in range(KD):
                last = pe.transpose(bank[:, k * P:(k + 1) * P], g.xn[:, t, k * P:(k + 1) * P], g.ident[:])
            last.then_inc(self.turned, 1)

    def scalar(self, act, c):
        g = self.g
        for t in range(TC * c, TC * c + TC):
            act.wait_ge(self.turned, t + 1)
            bank = (g.b4, g.b5)[t % 2]
            act.activation(g.xnT[:, :, t * P:(t + 1) * P], bank[:, 0:KD * P].rearrange("p (k n) -> p k n", k=KD),
                           ACT.Copy).then_inc(self.xnT, 1)


def norm_buffers(g, ctx, over=None):
    g.xn = g.sb("xn", [P, NT, D], ctx=ctx) if over is None else over.rearrange("p (t d) -> p t d", d=D)
    g.xnT = g.sb("xnT", [P, KD, B * S], ctx=ctx)


def project(g, n, w, causal, st):
    g.stage = f"p{n}_"
    nc = g.nc
    with ExitStack() as ctx:
        after_rnn = n == 4
        norm_buffers(g, ctx, over=g.hist[:].rearrange("p k b t -> p (k b t)") if after_rnn else None)
        NM = 4 if causal else 2
        if causal:
            wqkv = g.sb("wqkv", [P, KD, 3 * D], ctx=ctx)
        else:
            wq = g.sb("wq", [P, KD, D], ctx=ctx)
            wk = g.sb("wk", [CK, 2, D], ctx=ctx)
            wv = g.sb("wv", [CK, 2, D], ctx=ctx)
            cT = g.sb("cT", [CK, 2, B * M2], ctx=ctx)
            bq = g.sb("bq", [P, KD], ctx=ctx)
            bk = g.sb("bk", [P, KD], ctx=ctx)
            bv = g.sb("bv", [P, D], ctx=ctx)
        parts = g.sb("parts", [P, 3, 3, CH], BF16, ctx=ctx)
        rest = g.sb("rest", [P, 3, CH], ctx=ctx)
        ln = Norm(g, n, with_stats=causal or after_rnn)
        w_in, made, part1, left, part2, part3, vmade, vcopied, ones = (g.sem(f"p{n}_{s}") for s in (
            "w_in", "made", "part1", "left", "part2", "part3", "vmade", "vcopied", "ones"))
        stored = [g.sem(f"p{n}_stored{r}") for r in range(3)]
        banks = [g.b0[:], g.b1[:], g.b2[:], g.b3[:]]
        jobs = [("x", c, m) for c in range(NC) for m in range(NM)]
        if not causal:
            jobs = [("c", 0, m) for m in range(KD)] + jobs
        if causal:
            loads = [(NM * 1, st.load_q, 0), (NM * 2, st.load_q, 1), (NM * 2, st.load_k, 0)]
        else:
            loads = [(KD + 1, st.load_k, 0), (KD + 1, st.load_k, 1)]
            loads += [(KD + NM * (c + 1), st.load_q, c) for c in range(2)]
        bias = not causal and w["bq"] is not None
        back, xup = g.sem(f"p{n}_back"), g.sem(f"p{n}_xup")

        def width(job):
            return CH if job[0] == "x" else B * M2

        with nc.Block() as block:
            @block.sync
            def _(sp):
                if causal:
                    sp.dma_start(wqkv[:], w["wqkv"].rearrange("(k p) n -> p k n", p=P)).then_inc(w_in, 16)
                else:
                    sp.dma_start(cT[:], w["ctxT"].rearrange("(k p) n -> p k n", p=CK)).then_inc(w_in, 16)
                    sp.dma_start(wk[:], w["wk"].rearrange("(k p) n -> p k n", p=CK)).then_inc(w_in, 16)
                    sp.dma_start(wv[:], w["wv"].rearrange("(k p) n -> p k n", p=CK)).then_inc(w_in, 16)
                    sp.dma_start(wq[:], w["wq"].rearrange("(k p) n -> p k n", p=P)).then_inc(w_in, 16)
                    if bias:
                        with nc.allow_non_contiguous_dma("256 biases"):
                            sp.dma_start(bq[:], w["bq"].rearrange("(k p) -> p k", p=P)).then_inc(w_in, 16)
                            sp.dma_start(bk[:], w["bk"].rearrange("(k p) -> p k", p=P)).then_inc(w_in, 16)
                        sp.dma_start(bv[:], w["bv"].partition_broadcast(P)).then_inc(w_in, 16)
                st.load_rows(g, sp)
                for i, job in enumerate(jobs):
                    sp.wait_ge(part3, i + 1)
                    N = width(job)
                    if job[0] == "x":
                        row, scr = (job[2] % KD) * P, (g.q_scr if job[2] < KD else g.k_scr)
                        dst = scr[:, row:row + P, CH * job[1]:CH * job[1] + N]
                    else:
                        dst = g.kc_scr[:, job[2] * P:(job[2] + 1) * P, :]
                    sp.dma_start(dst.rearrange("a p n -> p a n"), parts[:, i % 3, :, 0:N]).then_inc(stored[i % 3], 16)
                    for at, load, x in loads:
                        if at == i:
                            for r in range(3):
                                sp.wait_ge(stored[r], 16 * ((i - 1 - r) // 3 + 1))
                            load(g, sp, x)
                for r in range(3):
                    sp.wait_ge(stored[r], 16 * ((len(jobs) - r + 2) // 3))

            n_w = 1 if causal else (7 if bias else 4)

            @block.tensor
            def _(pe):
                pe.wait_ge(w_in, 16 * n_w)
                if after_rnn:
                    for t in range(NT):
                        if t >= 2:
                            pe.wait_ge(xup, t - 1)
                        for k in range(KD):
                            last = pe.transpose((g.b6, g.b7)[t % 2][:, k * P:(k + 1) * P],
                                                g.hist[:, k, t // (NT // B), P * (t % (NT // B)):P * (t % (NT // B)) + P],
                                                g.ident[:])
                        last.then_inc(back, 1)
                    pe.wait_ge(xup, NT)
                for i, job in enumerate(jobs):
                    if job[0] == "x" and job[2] == 0:
                        ln.tensor(pe, job[1])
                        pe.wait_ge(ln.xnT, TC * (job[1] + 1))
                    if i >= 4:
                        pe.wait_ge(left, i - 3)
                    out = banks[i % 4][:, 0:width(job)]
                    if job[0] == "x":
                        c, m = job[1], job[2]
                        wt = wqkv if causal else wq
                        acc(pe, out, [(wt[:, k, m * P:(m + 1) * P], g.xnT[:, k, CH * c:CH * c + CH])
                                      for k in range(KD)]).then_inc(made, 1)
                    else:
                        m = job[2]
                        acc(pe, out, [(wk[:, k, m * P:(m + 1) * P], cT[:, k, :]) for k in range(2)]).then_inc(made, 1)
                    if causal and job[2] == NM - 1:
                        for t in range(TC * job[1], TC * job[1] + TC):
                            if t >= 2:
                                pe.wait_ge(vcopied, t - 1)
                            acc(pe, (g.b6, g.b7)[t % 2][:, 0:D],
                                [(g.xnT[:, k, t * P:(t + 1) * P], wqkv[:, k, 2 * D:3 * D])
                                 for k in range(KD)]).then_inc(vmade, 1)
                    if not causal and i < B:
                        acc(pe, (g.b6, g.b7)[i][0:M2, 0:D], [(cT[:, k, M2 * i:M2 * i + M2], wv[:, k, :])
                                                            for k in range(2)]).then_inc(vmade, 1)

            @block.scalar
            def _(act):
                nv = 0
                for i, job in enumerate(jobs):
                    if job[0] == "x" and job[2] == 0:
                        ln.scalar(act, job[1])
                    N = width(job)
                    act.wait_ge(made, i + 1)
                    if i >= 3:
                        act.wait_ge(stored[i % 3], 16 * (i // 3))
                    out, src = parts[:, i % 3, 0, 0:N], banks[i % 4][:, 0:N]
                    if bias:
                        if i == 0:
                            act.wait_ge(w_in, 16 * n_w)
                        col = job[2]
                        act.activation(out, src, ACT.Identity,
                                       bias=(bq if job[0] == "x" else bk)[:, col:col + 1]).then_inc(part1, 1)
                    else:
                        act.activation(out, src, ACT.Copy).then_inc(part1, 1)
                    if causal and job[2] == NM - 1:
                        for t in range(TC * job[1], TC * job[1] + TC):
                            act.wait_ge(vmade, t + 1)
                            if t == 0:
                                act.wait_ge(ones, 1)
                            act.activation(g.va[:, t, :, 0:DH],
                                           (g.b6, g.b7)[t % 2][:, 0:D].rearrange("p (h d) -> p h d", d=DH),
                                           ACT.Copy).then_inc(vcopied, 1)
                    if not causal and i < B:
                        act.wait_ge(vmade, i + 1)
                        act.wait_ge(ones, 1)
                        act.activation(g.vc[0:M2, i, :, 0:DH],
                                       (g.b6, g.b7)[i][0:M2, 0:D].rearrange("p (h d) -> p h d", d=DH),
                                       ACT.Copy).then_inc(vcopied, 1)

            @block.vector
            def _(v):
                def chunk_ready(c):
                    if causal:
                        v.wait_ge(g.x_in[c], 16)
                    if after_rnn:
                        for t in range(TC * c, TC * c + TC):
                            v.wait_ge(xup, t + 1)

                def jobs_of(c):
                    for i, job in enumerate(jobs):
                        if (job[1] if job[0] == "x" else -1) != c:
                            continue
                        N = width(job)
                        v.wait_ge(part1, i + 1)
                        if i >= 3:
                            v.wait_ge(part3, i - 2)
                        src, p1, r = banks[i % 4][:, 0:N], parts[:, i % 3, 0, 0:N], rest[:, i % 3, 0:N]
                        if bias:
                            b = (bq if job[0] == "x" else bk)[:, job[2]:job[2] + 1]
                            v.scalar_tensor_tensor(out=r, in0=src, scalar=b, in1=p1, op0=ALU.add,
                                                   op1=ALU.subtract).then_inc(left, 1)
                        else:
                            v.tensor_tensor(r, src, p1, ALU.subtract).then_inc(left, 1)
                        v.wait_ge(left, i + 1)
                        v.tensor_copy(parts[:, i % 3, 1, 0:N], r).then_inc(part2, 1)

                if after_rnn:
                    for t in range(NT):
                        v.wait_ge(back, t + 1)
                        v.tensor_tensor(g.x[:, t, :], (g.b6, g.b7)[t % 2][:, 0:D], g.x[:, t, :],
                                        ALU.add).then_inc(xup, 1)
                if bias:
                    v.wait_ge(w_in, 16 * n_w)
                if not ln.with_stats:
                    ln.vector(v)
                jobs_of(-1)
                if bias:
                    for b in range(B):
                        v.wait_ge(vcopied, B)
                        vb = g.vc[0:M2, b, :, 0:DH]
                        v.tensor_tensor(vb, vb, bv[0:M2, :].rearrange("p (h d) -> p h d", d=DH), ALU.add)
                if ln.with_stats:
                    ln.vector(v, chunk_ready)
                for c in range(NC):
                    jobs_of(c)
                    if c == 1 and st.mask is not None:
                        st.mask_keys(v)

            @block.gpsimd
            def _(pool):
                order = [("n", None), ("s", None)] + [("j", i) for i in range(len(jobs))]
                if not causal:
                    order = [("s", None), ("j", 0), ("j", 1), ("n", None)] + [("j", i) for i in range(2, len(jobs))]
                for what, i in order:
                    if what == "n":
                        ln.gpsimd(pool)
                        continue
                    if what == "s":
                        st.set_rows(pool)
                        pool.memset(g.va[:, :, :, DH:QD] if causal else g.vc[:, :, :, DH:QD], 1.0).then_inc(ones, 1)
                        continue
                    N = width(jobs[i])
                    r, p2, p3 = rest[:, i % 3, 0:N], parts[:, i % 3, 1, 0:N], parts[:, i % 3, 2, 0:N]
                    pool.wait_ge(part2, i + 1)
                    pool.tensor_tensor(p3, r, p2, ALU.subtract).then_inc(part3, 1)


class Stacks:

    def __init__(self, g, n, causal, mask, ctx):
        self.causal, self.mask = causal, mask
        self.first_rows = self.r_max = R_EXTRA
        self.rows = self.r_max + 3
        self.ks = g.sb("ks", [P, B, H, S if causal else M2], BF16, ctx=ctx)
        self.ring = 2 if causal else NC
        self.qs = g.sb("qs", [P, self.ring, H, CH], BF16, ctx=ctx)
        self.ones = g.sb("ones", [P, CH], BF16, ctx=ctx)
        self.k_in = [g.sem(f"k{n}_in{b}") for b in range(B)]
        self.q_in = [g.sem(f"q{n}_in{r}") for r in range(self.ring)]
        self.ones_set, self.rows_in = g.sem(f"k{n}_ones_set"), g.sem(f"k{n}_rows_in")
        self.n_rows = 16 * B * (S // CH if causal else 1)
        if mask is not None:
            self.row8 = g.sb("row8", [P, B * M2], U8, ctx=ctx)
            self.row = g.sb("row", [P, B * M2], ctx=ctx)
            self.row_neg = g.sb("row_neg", [1, B, HG, M2], BF16, ctx=ctx)
            self.col8 = g.sb("col8", [M2, B], U8, ctx=ctx)
            self.col_neg = g.sb("col_neg", [M2, B], ctx=ctx)
            self.mask_in, self.mask_set, self.k_masked = (
                g.sem(f"k{n}_{x}") for x in ("mask_in", "mask_set", "k_masked"))

    def load_rows(self, g, sp):
        if self.mask is not None:
            sp.dma_start(self.row8[:], self.mask.partition_broadcast(P)).then_inc(self.mask_in, 16)
            with g.nc.allow_non_contiguous_dma("77 flags"):
                sp.dma_start(self.col8[:], self.mask.rearrange("(b m) -> m b", b=B)).then_inc(self.mask_in, 16)
        N = CH if self.causal else M2
        sp.wait_ge(self.ones_set, 1)
        src = self.ones[self.r_max:self.rows, 0:N].unsqueeze(1).broadcast_to([3, H, N])
        for b in range(B):
            for half in range(S // CH if self.causal else 1):
                sp.dma_start(self.ks[self.r_max:self.rows, b, :, N * half:N * half + N], src
                             ).then_inc(self.rows_in, 16)

    def set_rows(self, pool):
        pool.memset(self.ones[:], 1.0).then_inc(self.ones_set, 1)
        if self.mask is not None:
            pool.wait_ge(self.mask_in, 32)
            pool.tensor_copy(self.row[:], self.row8[:]).then_inc(self.mask_set, 1)
            pool.tensor_copy(self.col_neg[:], self.col8[:]).then_inc(self.mask_set, 1)
            pool.wait_ge(self.mask_set, 2)
            pool.tensor_scalar(self.row_neg[:], self.row[0:1, :].rearrange("p (b t) -> p b t", b=B).unsqueeze(2)
                               .broadcast_to([1, B, HG, M2]), 1.0, BIG, ALU.subtract, ALU.mult
                               ).then_inc(self.mask_set, 1)
            pool.tensor_scalar(self.col_neg[:], self.col_neg[:], 1.0, BIG * SCALE, ALU.subtract, ALU.mult
                               ).then_inc(self.mask_set, 1)

    def mask_keys(self, v):
        v.wait_ge(self.mask_set, 1)
        for b in range(B):
            v.wait_ge(self.k_in[b], 16 * len(COMBOS))
            kk = self.ks[0:R_EXTRA, b]
            v.tensor_tensor(kk, kk, self.row[0:R_EXTRA, M2 * b:M2 * b + M2].unsqueeze(1)
                            .broadcast_to([R_EXTRA, H, M2]), ALU.mult).then_inc(self.k_masked, 1)

    def load_q(self, g, sp, c, slot=None):
        slot = c if slot is None else slot
        for r, (qp, _) in enumerate(COMBOS):
            sp.dma_start(self.qs[DH * r:DH * r + DH, slot, :, :],
                         g.q_scr[qp, :, CH * c:CH * c + CH].rearrange("(h d) t -> d h t", d=DH)
                         ).then_inc(self.q_in[slot], 16)

    def load_k(self, g, sp, b):
        scr, N = (g.k_scr, S) if self.causal else (g.kc_scr, M2)
        for r, (_, kp) in enumerate(COMBOS):
            sp.dma_start(self.ks[DH * r:DH * r + DH, b, :, :],
                         scr[kp, :, N * b:N * b + N].rearrange("(h d) t -> d h t", d=DH)).then_inc(self.k_in[b], 16)


BEGIN, END = 12, 20
AHEAD = 0.5


def attention_order(causal, first, first_of, steps, steps_of):
    order, later = [], []
    ahead = len(first_of[1]) * AHEAD if causal else 0
    lead = 1 if causal else 2
    if not causal:
        order += [("first", i) for i in first_of[0]] + [("max", 0), ("turn", 0)]
    for p in range(-1, NC):
        a = first_of[p + lead] if p + lead < NC else []
        b = steps_of[p] if p >= 0 else []
        slots = 5 * max(1, len(b))
        begin, end = (BEGIN if p >= 1 else 0, slots - END) if causal and b else (0, max(1, slots - 10))
        todo = [i for i in a if ("first", i) not in order]
        total = sum(first[i][4] + 64 for i in todo)
        done = 0
        for j in range(slots):
            while todo and j >= begin and done < total * (j + 1 - begin) / (end - begin):
                order.append(("first", todo[0]))
                done += first[todo.pop(0)][4] + 64
            if a and j == end - 1:
                order += [("first", i) for i in todo] + [("max", p + lead)]
                todo = []
            if a and j == min(end + 1, slots - 1):
                order.append(("turn", p + lead))
                if p < 0 and causal:
                    order += [("first", i) for i in first_of[1][:int(ahead)]]
            if not b:
                continue
            i, part = b[j // 5], j % 5
            if part != 2:
                order.append(("scores", i, part - (part > 2)))
            elif i:
                order.append(("values", i - 1))
                u = steps[i - 1][0]
                if steps[i][0] != u:
                    later.append(("norm", u))
                    if u % NG == NG - 1:
                        for t in range(TC * (u // NG), TC * (u // NG) + TC):
                            later += [("turned", t), ("out", t)]
            if part in ((0, 4) if causal else (0, 1, 3, 4)):
                order += later[:1]
                later = later[1:]
    u = NG * NC - 1
    order += later + [("values", len(steps) - 1), ("norm", u)]
    for t in range(NT - TC, NT):
        order += [("turned", t)] + [("out", t - 1)] * (t > NT - TC)
    return order + [("out", NT - 1)]


def attention(g, n, causal, st, w=None, following=None):
    g.stage = f"a{n}_"
    nc = g.nc
    KP = P if causal else M2
    chunks = [0, 1, 3, 2] if causal else list(range(NC))
    units = [(c, hg) for c in chunks for hg in range(NG)]

    def blocks(c):
        return TC * (c % 2) + TC if causal else 1

    first, items_end = [], []
    for p, c in enumerate(chunks):
        for qt in range(TC):
            if causal:
                keys = P * (TC * (c % 2) + qt + 1)
                for h in range(H):
                    for half in range((keys + CH - 1) // CH):
                        first.append((p, qt, h, half, min(CH, keys - CH * half)))
            else:
                first += [(p, qt, hg, 0, HG * M2) for hg in range(NG)]
        items_end.append(len(first))
    steps = [(u, kb) for u in range(len(units)) for kb in range(blocks(units[u][0]))]
    first_of = [[i for i, it in enumerate(first) if it[0] == p] for p in range(NC)]
    steps_of = [[i for i, step in enumerate(steps) if step[0] // NG == p] for p in range(NC)]
    order = attention_order(causal, first, first_of, steps, steps_of)
    def shares_b7(t):
        return causal and t < NT - TC

    b7 = [(e[0], e[1]) for e in order if e[0] in ("turn", "norm", "turned") or e[0] == "out" and shares_b7(e[1])]

    def ends_unit(i):
        return i + 1 == len(steps) or steps[i + 1][0] != steps[i][0]

    with ExitStack() as ctx:
        ks, qs = st.ks, st.qs
        mxp = g.sb("mxp", [P, 2, TC, H, 2], ctx=ctx)
        nm = g.sb("nm", [P, 2, TC, H], ctx=ctx)
        mp = g.sb("mp", [H, 2, 3, CH], BF16, ctx=ctx)
        mr = g.sb("mr", [H, 2, CH], ctx=ctx)
        pr = g.sb("pr", [P, 2, HG, CH], ctx=ctx)
        osb = g.sb("osb", [P, 2, CH], ctx=ctx)
        rec = g.sb("rec", [P, 2, TC, HG], ctx=ctx)
        on = g.sb("on", [P, 2, TC, D], ctx=ctx)
        onT = g.sb("onT", [P, 2, KD, P], ctx=ctx)
        wo = g.sb("wo", [P, KD, D], ctx=ctx)
        va = g.va if causal else g.vc
        names = ("s1", "max", "nm", "nmT", "n1", "nr", "n2", "n3", "s2", "exp", "pv", "oev", "oT", "rec", "on",
                 "back", "onT", "wo_in", "y", "xup", "bo_in", "xbo", "zeroed", "filled")
        s = {k: g.sem(f"a{n}_{k}") for k in names}
        stats = NextStats(g, n, s["xup"], lambda i: TC * chunks[i // TC] + i % TC)
        m_in = [g.sem(f"a{n}_m_in{r}") for r in range(2)]
        masked = st.mask is not None
        bias_o = not causal and w["bo"] is not None
        if bias_o:
            bo = g.sb("bo", [P, D], ctx=ctx)
        n_q = len(COMBOS) * 16
        first_banks = (g.b3, g.b4, g.b5) if causal else (g.b2, g.b3, g.b4)
        score_banks = (g.b0, g.b1, g.b2) if causal else (g.b0, g.b1)
        n_first, n_score = len(first_banks), len(score_banks)
        freed_by = {"turn": "nr", "norm": "on", "turned": "onT", "out": "xup"}

        def out_bank(t):
            return g.b7 if shares_b7(t) else g.b5


        def wait_b7(pe, user):
            at = b7.index(user)
            if at:
                kind, u = b7[at - 1]
                pe.wait_ge(s[freed_by[kind]], u + 1)

        with nc.Block() as block:
            @block.sync
            def _(sp):
                if causal:
                    st.load_k(g, sp, 1)
                else:
                    st.load_q(g, sp, 2)
                    st.load_q(g, sp, 3)
                if bias_o:
                    sp.dma_start(bo[:], w["bo"].partition_broadcast(P)).then_inc(s["bo_in"], 16)
                if following is not None:
                    following.load(sp)
                sp.dma_start(wo[:], g.wo_dram[n].rearrange("(k p) n -> p k n", p=P)).then_inc(s["wo_in"], 16)
                for what, i, *h in order:
                    if what == "turn":
                        sp.wait_ge(s["n3"], i + 1)
                        sp.wait_ge(s["n2"], i + 1)
                        for k in range(3):
                            sp.dma_start(qs[st.r_max + k:st.r_max + k + 1, i % st.ring, :, :],
                                         mp[:, i % 2, k, :]).then_inc(m_in[i % 2], 16)
                    if what == "scores" and h[0] == HG - 1 and ends_unit(i) and steps[i][0] % NG == NG - 1:
                        p = steps[i][0] // NG
                        if p + st.ring < NC:
                            sp.wait_ge(s["s2"], HG * (i + 1))
                            st.load_q(g, sp, chunks[p + st.ring], p)
                if following is not None:
                    sp.wait_ge(following.came, following.count)

            @block.gpsimd
            def _(pool):
                if causal:
                    routing_constants(g, pool, s["zeroed"], s["filled"])
                for what, u, *_ in order:
                    if what == "turn":
                        pool.wait_ge(s["n2"], u + 1)
                        pool.tensor_tensor(mp[:, u % 2, 2, :], mr[:, u % 2, :], mp[:, u % 2, 1, :],
                                           ALU.subtract).then_inc(s["n3"], 1)
                    if what == "turn" and u == 1 and bias_o:
                        pool.wait_ge(s["bo_in"], 16)
                        for t in range(NT):
                            pool.tensor_tensor(g.x[:, t, :], g.x[:, t, :], bo[:], ALU.add).then_inc(s["xbo"], 1)
                    if what == "turn" and u == 2 and n == 1:
                        following.prepare(pool)
                stats.gpsimd(pool)

            @block.tensor
            def _(pe):
                def first_pass(i):
                    p, qt, h, half, N = first[i]
                    c, slot = chunks[p], p % st.ring
                    bank = first_banks[i % n_first]
                    if qt == 0 and h == 0 and half == 0:
                        pe.wait_ge(st.q_in[slot], n_q * (p // st.ring + 1))
                        pe.wait_ge(st.k_in[c // 2], n_q)
                        if masked:
                            pe.wait_ge(st.k_masked, B)
                            pe.wait_ge(st.mask_set, 4)
                    if i >= n_first:
                        pe.wait_ge(s["max"], i - n_first + 1)
                    if causal:
                        diag = CH * half + N == P * (TC * (c % 2) + qt + 1)
                        last = pe.matmul(bank[:, 0:N], qs[0:st.first_rows, slot, h, P * qt:P * qt + P],
                                         ks[0:st.first_rows, c // 2, h, CH * half:CH * half + N],
                                         start=True, stop=not diag)
                        if diag:
                            last = pe.matmul(bank[:, N - P:N], g.identb[:], g.mask_qk[:], start=False, stop=True)
                    else:
                        if masked:
                            pe.matmul(bank[:, 0:HG * M2], st.ones[0:1, 0:P],
                                      st.row_neg[:, c // 2].rearrange("p h t -> p (h t)"), start=True, stop=False)
                        for j in range(HG):
                            last = pe.matmul(bank[:, M2 * j:M2 * j + M2],
                                             qs[0:st.first_rows, slot, HG * h + j, P * qt:P * qt + P],
                                             ks[0:st.first_rows, c // 2, HG * h + j, :], start=not masked,
                                             stop=not masked or j == HG - 1)
                    last.then_inc(s["s1"], 1)

                def turn_max(p):
                    if causal:
                        pe.wait_ge(s["nm"], p + 1)
                    else:
                        pe.wait_ge(s["max"], items_end[p])
                    wait_b7(pe, ("turn", p))
                    for qt in range(TC):
                        last = pe.transpose(g.b7[0:H, P * qt:P * qt + P], nm[:, p % 2, qt, :], g.ident[:])
                    last.then_inc(s["nmT"], 1)

                def scores(i, h):
                    u, kb = steps[i]
                    c, hg = units[u]
                    p = u // NG
                    if u % NG == 0 and kb == 0 and h == 0:
                        pe.wait_ge(m_in[p % 2], 48 * (p // 2 + 1))
                        if u == 0:
                            pe.wait_ge(st.rows_in, st.n_rows)
                    d = kb - TC * (c % 2) if causal else -1
                    off = P * max(d, 0)
                    k = HG * i + h
                    if k >= n_score:
                        pe.wait_ge(s["exp"], k - n_score + 1)
                    bank = score_banks[k % n_score]
                    hh = HG * hg + h
                    last = pe.matmul(bank[0:KP, off:CH], ks[0:st.rows, c // 2, hh, P * kb:P * kb + KP],
                                     qs[0:st.rows, p % st.ring, hh, off:CH], start=True, stop=d < 0)
                    if d >= 0:
                        last = pe.matmul(bank[:, off:off + P], g.identb[:], g.mask_kq[:], start=False, stop=True)
                    last.then_inc(s["s2"], 1)

                def values(i):
                    u, kb = steps[i]
                    c, hg = units[u]
                    off = P * max(kb - TC * (c % 2), 0) if causal else 0
                    tile = TC * 2 * (c // 2) + kb if causal else c // 2
                    if kb == 0 and u:
                        pe.wait_ge(s["oev"], u)
                    pe.wait_ge(s["exp"], HG * (i + 1))
                    for h in range(HG):
                        last = pe.matmul(g.b6[QD * h:QD * h + QD, off:CH], va[0:KP, tile, HG * hg + h, :],
                                         pr[0:KP, i % 2, h, off:CH], start=(kb == 0), stop=ends_unit(i),
                                         tile_position=(0, QD * h))
                    last.then_inc(s["pv"], 1)

                def norm(u):
                    pe.wait_ge(s["oev"], u + 1)
                    wait_b7(pe, ("norm", u))
                    for qt in range(TC):
                        last = pe.transpose(g.b7[:, P * qt:P * qt + P], osb[:, u % 2, P * qt:P * qt + P], g.ident[:])
                    last.then_inc(s["oT"], 1)

                def turned(t):
                    pe.wait_ge(s["on"], NG * (t // TC + 1))
                    wait_b7(pe, ("turned", t))
                    for k in range(KD):
                        last = pe.transpose(g.b7[:, k * P:(k + 1) * P],
                                            on[:, t // TC % 2, t % TC, k * P:(k + 1) * P], g.ident[:])
                    last.then_inc(s["back"], 1)

                def output(t):
                    if t == 0:
                        pe.wait_ge(s["wo_in"], 16)
                    if shares_b7(t):
                        wait_b7(pe, ("out", t))
                    elif t:
                        pe.wait_ge(s["xup"], t)
                        if causal:
                            pe.wait_ge(s["max"], len(first))
                    pe.wait_ge(s["onT"], t + 1)
                    acc(pe, out_bank(t)[:, 0:D], [(onT[:, t % 2, k, :], wo[:, k, :]) for k in range(KD)]).then_inc(s["y"], 1)

                for what, i, *h in order:
                    if what == "first":
                        first_pass(i)
                    if what == "turn":
                        turn_max(i)
                    if what == "scores":
                        scores(i, h[0])
                    if what == "values":
                        values(i)
                    if what == "norm":
                        norm(i)
                    if what == "turned":
                        turned(i)
                    if what == "out":
                        output(i)

            @block.scalar
            def _(act):
                for what, i, *h in order:
                    if what == "scores":
                        u, kb = steps[i]
                        off = P * max(kb - TC * (units[u][0] % 2), 0) if causal else 0
                        k = HG * i + h[0]
                        act.wait_ge(s["s2"], k + 1)
                        if i >= 2:
                            act.wait_ge(s["pv"], i - 1)
                        out, x = pr[0:KP, i % 2, h[0], off:CH], score_banks[k % n_score][0:KP, off:CH]
                        if masked:
                            b = units[u][0] // 2
                            act.activation(out, x, ACT.Exp, bias=st.col_neg[:, b:b + 1], scale=SCALE
                                           ).then_inc(s["exp"], 1)
                        else:
                            act.activation(out, x, ACT.Exp, scale=SCALE).then_inc(s["exp"], 1)
                    if what == "values" and ends_unit(i):
                        u = steps[i][0]
                        act.wait_ge(s["pv"], i + 1)
                        if u >= 2:
                            act.wait_ge(s["oT"], u - 1)
                        act.activation(osb[:, u % 2, :], g.b6[:], ACT.Copy).then_inc(s["oev"], 1)
                    if what == "turned":
                        act.wait_ge(s["back"], i + 1)
                        if i >= 2:
                            act.wait_ge(s["y"], i - 1)
                        act.activation(onT[:, i % 2].rearrange("p k n -> p (k n)"), g.b7[:, 0:D],
                                       ACT.Copy).then_inc(s["onT"], 1)

            @block.vector
            def _(v):
                for what, i, *_ in order:
                    if what == "first":
                        p, qt, h, half, N = first[i]
                        bank = first_banks[i % n_first]
                        v.wait_ge(s["s1"], i + 1)
                        if causal:
                            v.tensor_reduce(mxp[:, p % 2, qt, h, half:half + 1], bank[:, 0:N], AX.X,
                                            ALU.max).then_inc(s["max"], 1)
                        else:
                            if qt == 0 and h == 0 and p >= 2:
                                v.wait_ge(s["nmT"], p - 1)
                            v.tensor_reduce(nm[:, p % 2, qt, HG * h:HG * h + HG],
                                            bank[:, 0:N].rearrange("p (h t) -> p h t", h=HG),
                                            AX.X, ALU.max, negate=True).then_inc(s["max"], 1)
                    if what == "max" and causal:
                        v.wait_ge(s["max"], items_end[i])
                        if i >= 2:
                            v.wait_ge(s["nmT"], i - 1)
                        c = chunks[i]
                        for qt in range(TC):
                            last = v.tensor_reduce(nm[:, i % 2, qt, :], mxp[:, i % 2, qt, :, 0:1 + c % 2],
                                                   AX.X, ALU.max, negate=True)
                        last.then_inc(s["nm"], 1)
                    if what == "turn":
                        v.wait_ge(s["nmT"], i + 1)
                        if i >= 2:
                            v.wait_ge(m_in[i % 2], 48 * (i // 2))
                        v.tensor_copy(mp[:, i % 2, 0, :], g.b7[0:H, :]).then_inc(s["n1"], 1)
                        v.wait_ge(s["n1"], i + 1)
                        if i >= 2:
                            v.wait_ge(s["n3"], i - 1)
                        v.tensor_tensor(mr[:, i % 2, :], g.b7[0:H, :], mp[:, i % 2, 0, :],
                                        ALU.subtract).then_inc(s["nr"], 1)
                        v.wait_ge(s["nr"], i + 1)
                        v.tensor_copy(mp[:, i % 2, 1, :], mr[:, i % 2, :]).then_inc(s["n2"], 1)
                    if what == "norm":
                        p, hg = i // NG, i % NG
                        o = g.b7[:].rearrange("p (t h d) -> p t h d", t=TC, h=HG)
                        v.wait_ge(s["oT"], i + 1)
                        v.reciprocal(rec[:, i % 2], o[:, :, :, DH]).then_inc(s["rec"], 1)
                        v.wait_ge(s["rec"], i + 1)
                        if p >= 2:
                            v.wait_ge(s["back"], TC * (p - 1))
                        v.tensor_tensor(
                            on[:, p % 2, :, HG * DH * hg:HG * DH * hg + HG * DH].rearrange("p t (h d) -> p t h d", h=HG),
                            o[:, :, :, 0:DH], rec[:, i % 2].unsqueeze(3).broadcast_to([P, TC, HG, DH]),
                            ALU.mult).then_inc(s["on"], 1)
                    if what == "out":
                        if bias_o and i == 0:
                            v.wait_ge(s["xbo"], NT)
                        v.wait_ge(s["y"], i + 1)
                        t = TC * chunks[i // TC] + i % TC
                        v.tensor_tensor(g.x[:, t, :], out_bank(i)[:, 0:D], g.x[:, t, :], ALU.add).then_inc(s["xup"], 1)
                        stats.vector(v, i)


def rank_select(v, step, gates, tie, sel, cmp, eq, e, top):
    n = gates.shape[1]
    gj = gates.unsqueeze(2).broadcast_to([P, n, e, e])
    ge = gates.unsqueeze(3).broadcast_to([P, n, e, e])
    step(v.tensor_tensor(cmp, gj, ge, ALU.is_gt))
    step(v.tensor_tensor(eq, gj, ge, ALU.is_equal))
    step(v.tensor_tensor(eq, eq, tie.unsqueeze(1).broadcast_to([P, n, e, e]), ALU.mult))
    step(v.tensor_tensor(cmp, cmp, eq, ALU.add))
    step(v.tensor_reduce(sel, cmp, AX.X, ALU.add))
    return v.tensor_scalar(sel, sel, float(top), None, ALU.is_lt)


def linear_experts(g, n, w, following):
    g.stage = f"f{n}_"
    nc = g.nc
    with ExitStack() as ctx:
        norm_buffers(g, ctx)
        wg, we_hi, we_lo, be, bg = w.wg, w.we_hi, w.we_lo, w.be, w.bg
        xh = g.sb("xh", [P, KD, B * S], F32R, ctx=ctx)
        xl = g.sb("xl", [P, KD, B * S], F32R, ctx=ctx)
        x_hi, x_lo = g.sem(f"f{n}_x_hi"), g.sem(f"f{n}_x_lo")
        gate = g.sb("gate", [P, TC, E0], ctx=ctx)
        sel = g.sb("sel", [P, TC, E0], ctx=ctx)
        top = g.sb("top", [P, TC], ctx=ctx)
        cmp = g.sb("cmp", [P, TC, E0, E0], ctx=ctx)
        eq = g.sb("eq", [P, TC, E0, E0], ctx=ctx)
        wts = g.sb("wts", [P, NT, E0], ctx=ctx)
        wtsT = g.sb("wtsT", [E0, 2, CH], ctx=ctx)
        ln = Norm(g, n)
        gmade, chain, gexp, shifted, wready, wT, wTc, ymade, yused, xup = (g.sem(f"f{n}_{k}") for k in (
            "gmade", "chain", "gexp", "shifted", "wready", "wT", "wTc", "ymade", "yused", "xup"))
        stats = NextStats(g, n, xup, lambda i: i)
        ybank = [g.b0[:], g.b1[:], g.b2[:], g.b3[:]]
        NE = E0 // 2
        with nc.Block() as block:
            @block.sync
            def _(sp):
                following.load(sp)
                sp.wait_ge(following.came, following.count)

            @block.tensor
            def _(pe):
                def gates(c):
                    pe.wait_ge(ln.xnT, TC * (c + 1))
                    if c:
                        pe.wait_ge(wTc, c)
                    for t in range(TC * c, TC * c + TC):
                        last = acc(pe, g.b6[:, E0 * (t % TC):E0 * (t % TC) + E0],
                                   [(g.xnT[:, k, t * P:(t + 1) * P], wg[:, k, :]) for k in range(KD)])
                    last.then_inc(gmade, 1)

                ln.tensor(pe, 0)
                gates(0)
                for c in range(NC):
                    pe.wait_ge(x_lo, c + 1)
                    for t in range(TC * c, TC * c + TC):
                        for j in range(NE):
                            i = NE * t + j
                            if i >= NE:
                                pe.wait_ge(yused, i - NE + 1)
                            tok, cols = slice(t * P, (t + 1) * P), slice(512 * j, 512 * j + 512)
                            acc(pe, ybank[j], [(x[:, k, tok], we[:, k, cols])
                                               for x, we in ((xh, we_hi), (xh, we_lo), (xl, we_hi))
                                               for k in range(KD)]).then_inc(ymade, 1)
                        if t % TC == 0:
                            pe.wait_ge(wready, c + 1)
                            for q in range(TC):
                                last = pe.transpose(g.b6[0:E0, P * q:P * q + P], wts[:, TC * c + q, :], g.ident[:])
                            last.then_inc(wT, 1)
                            pe.wait_ge(wTc, c + 1)
                        if t:
                            pe.wait_ge(xup, t)
                        pe.matmul(g.b7[:, 0:D], wtsT[:, c % 2, P * (t % TC):P * (t % TC) + P], be[:],
                                  start=True, stop=True).then_inc(ymade, 1)
                        if t % TC == 1 and c + 1 < NC:
                            ln.tensor(pe, c + 1)
                        if t % TC == 2 and c + 1 < NC:
                            gates(c + 1)

            @block.scalar
            def _(act):
                for c in range(NC):
                    ln.scalar(act, c)
                    act.wait_ge(ln.xnT, TC * (c + 1))
                    cols = slice(CH * c, CH * c + CH)
                    act.activation(xh[:, :, cols], g.xnT[:, :, cols], ACT.Copy).then_inc(x_hi, 1)
                    act.wait_ge(shifted, c + 1)
                    act.activation(gate[:], gate[:], ACT.Exp).then_inc(gexp, 1)
                    act.wait_ge(wT, c + 1)
                    act.activation(wtsT[:, c % 2, :], g.b6[0:E0, :], ACT.Copy).then_inc(wTc, 1)

            @block.gpsimd
            def _(pool):
                for c in range(NC):
                    pool.wait_ge(x_hi, c + 1)
                    cols = slice(CH * c, CH * c + CH)
                    pool.tensor_tensor(xl[:, :, cols], g.xnT[:, :, cols], xh[:, :, cols], ALU.subtract).then_inc(x_lo, 1)
                stats.gpsimd(pool)

            @block.vector
            def _(v):
                count = [0]

                def step(ins):
                    count[0] += 1
                    ins.then_inc(chain, 1)
                    v.wait_ge(chain, count[0])

                ln.vector(v)
                for c in range(NC):
                    v.wait_ge(gmade, c + 1)
                    step(v.tensor_tensor(gate[:], g.b6[:, 0:TC * E0].rearrange("p (t e) -> p t e", e=E0),
                                         bg[:].unsqueeze(1).broadcast_to([P, TC, E0]), ALU.add))
                    step(v.tensor_reduce(top[:], gate[:], AX.X, ALU.max))
                    step(rank_select(v, step, gate[:], g.tie8[:], sel[:], cmp[:], eq[:], E0, TOP0))
                    v.tensor_tensor(gate[:], gate[:], top[:].unsqueeze(2).broadcast_to([P, TC, E0]),
                                    ALU.subtract).then_inc(shifted, 1)
                    v.wait_ge(gexp, c + 1)
                    step(v.tensor_tensor(gate[:], gate[:], sel[:], ALU.mult))
                    step(v.tensor_reduce(top[:], gate[:], AX.X, ALU.add))
                    step(v.reciprocal(top[:], top[:]))
                    v.tensor_tensor(wts[:, TC * c:TC * c + TC, :], gate[:],
                                    top[:].unsqueeze(2).broadcast_to([P, TC, E0]), ALU.mult).then_inc(wready, 1)
                    v.wait_ge(wready, c + 1)
                    for t in range(TC * c, TC * c + TC):
                        for e in range(E0):
                            j = e // 2
                            if e % 2 == 0:
                                v.wait_ge(ymade, (NE + 1) * t + j + 1)
                            ins = v.scalar_tensor_tensor(
                                out=g.x[:, t, :], in0=ybank[j][:, D * (e % 2):D * (e % 2) + D],
                                scalar=wts[:, t, e:e + 1], in1=g.x[:, t, :], op0=ALU.mult, op1=ALU.add)
                            if e % 2:
                                ins.then_inc(yused, 1)
                                v.wait_ge(yused, NE * t + j + 1)
                            else:
                                step(ins)
                        v.wait_ge(ymade, (NE + 1) * (t + 1))
                        v.tensor_tensor(g.x[:, t, :], g.b7[:, 0:D], g.x[:, t, :], ALU.add).then_inc(xup, 1)
                        stats.vector(v, t)


U = 32


def recurrence(g, n, w, following):
    g.stage = f"r{n}_"
    nc = g.nc
    with ExitStack() as ctx:
        norm_buffers(g, ctx)
        wi, wh, bb = w.wi, w.wh, w.bb
        following.stage_in(g, ctx, g.inputs)
        whr = g.sb("whr", [P, KD, D], ctx=ctx)
        whp = g.sb("whp", [P, 3, KD, D], BF16, ctx=ctx)
        R = 4
        xi = g.sb("xi", [P, R, CH], ctx=ctx)
        xip = g.sb("xip", [P, 3, KD, B, S + U], BF16, ctx=ctx)
        hr = g.sb("hr", [P, 2, KD, B, U], ctx=ctx)
        hp16 = g.sb("hp16", [P, 2, 2, KD, B], F16, ctx=ctx)
        ln = Norm(g, n)
        wprep, pre, made, left, part1, part2, part3, copied = (g.sem(f"r{n}_{k}") for k in (
            "wprep", "pre", "made", "left", "part1", "part2", "part3", "copied"))
        h_ready, hi_ready, lo_ready, summed = ([g.sem(f"r{n}_{k}{m}") for m in range(KD)] for k in (
            "h_ready", "hi_ready", "lo_ready", "summed"))
        in_banks = (g.b0, g.b1, g.b2, g.b3)
        jobs = [(c, m) for c in range(NC) for m in range(KD)]

        def bank(m, half, parity):
            return (g.b0, g.b1, g.b2, g.b3, g.b4, g.b5, g.b6, g.b7)[4 * m + 2 * half + parity][
                :, 0:B * U // 2].rearrange("p (b t) -> p b t", b=B)

        def xi_part(q, job):
            c, m = job
            return xip[:, q, m, c // 2, CH * (c % 2):CH * (c % 2) + CH]

        with nc.Block() as block:
            @block.sync
            def _(sp):
                following.load(sp)
                sp.wait_ge(following.came, following.count)

            @block.tensor
            def _(pe):
                ln.tensor(pe, 0)
                for i, (c, m) in enumerate(jobs):
                    if m == 0:
                        if c + 1 < NC:
                            ln.tensor(pe, c + 1)
                        pe.wait_ge(ln.xnT, TC * (c + 1))
                    if i >= R:
                        pe.wait_ge(left, i - R + 1)
                    acc(pe, in_banks[i % R][:], [(wi[:, k, m * P:(m + 1) * P], g.xnT[:, k, CH * c:CH * c + CH])
                                                 for k in range(KD)]).then_inc(made, 1)
                pe.wait_ge(part3, len(jobs))
                pe.wait_ge(wprep, 5)
                pe.wait_ge(pre, 1)

                def inputs(half, it, m, parity):
                    for q in range(3):
                        x = xip[:, q, m].rearrange("p b (s two) -> p b s two", two=2)
                        pe.matmul(bank(m, half, parity), g.identb[:],
                                  x[:, :, bass.ds(it * U + half * (U // 2), U // 2), parity],
                                  start=(q == 0), stop=True, skip_group_check=True)

                groups = [(0, 0, 0, (0, 1, 2)), (0, 0, 1, (0, 1, 2)), (1, 0, 0, (0, 1, 2)), (1, 0, 1, (2,)),
                          (0, 1, 0, (0, 1)), (0, 1, 1, (0, 1)), (1, 1, 0, (0, 1)),
                          (1, 0, 1, (1, 0)), (1, 1, 1, (0, 1))]
                ready = (hi_ready, lo_ready)
                for m in range(KD):
                    for parity in range(2):
                        inputs(0, 0, m, parity)
                with pe.Fori(0, S // (2 * U)) as it:
                    for half in range(2):
                        for t in range(U):
                            at = it * (2 * U) + (half * U + t + 1)
                            waited = set()
                            for k, q, m, parts in groups:
                                if (k, q) not in waited:
                                    pe.wait_ge(ready[q][k], at)
                                    waited.add((k, q))
                                for a in parts:
                                    last = pe.matmul(bank(m, half, t % 2)[:, :, t // 2],
                                                     whp[:, a, k, m * P:(m + 1) * P], hp16[:, (t + 1) % 2, q, k, :],
                                                     start=False, stop=True, skip_group_check=True)
                                if (k, q) == (1, 1):
                                    last.then_inc(summed[m], 1)
                            if t in (4, 8, 12, 16):
                                piece = t // 4 - 1
                                inputs(1 - half, it + half, piece // 2, piece % 2)

            @block.scalar
            def _(act):
                act.activation(whp[:, 0], wh[:], ACT.Copy).then_inc(wprep, 1)
                act.wait_ge(wprep, 2)
                ln.scalar(act, 0)
                for i, (c, m) in enumerate(jobs):
                    if m == 0 and c + 1 < NC:
                        ln.scalar(act, c + 1)
                    act.wait_ge(made, i + 1)
                    if i >= R:
                        act.wait_ge(part3, i - R + 1)
                    act.activation(xi[:, i % R, :], in_banks[i % R][:], ACT.Identity,
                                   bias=bb[:, 2, m:m + 1]).then_inc(left, 1)
                with act.Fori(0, S // (2 * U)) as it:
                    for half in range(2):
                        act.wait_ge(copied, it * 2 + (half + 1))
                        for t in range(U):
                            for m in range(KD):
                                act.wait_ge(summed[m], it * (2 * U) + (half * U + t + 1))
                                x = bank(m, half, t % 2)[:, :, t // 2]
                                act.activation(hp16[:, t % 2, 0, m, :], x, ACT.Tanh).then_inc(hi_ready[m], 1)
                                act.activation(hr[:, half, m, :, t], x, ACT.Tanh).then_inc(h_ready[m], 1)

            @block.vector
            def _(v):
                v.wait_ge(wprep, 1)
                v.tensor_tensor(bb[:, 2, :], bb[:, 0, :], bb[:, 1, :], ALU.add).then_inc(wprep, 1)
                v.tensor_tensor(whr[:], wh[:], whp[:, 0], ALU.subtract).then_inc(wprep, 1)
                v.wait_ge(wprep, 3)
                v.tensor_copy(whp[:, 1], whr[:]).then_inc(wprep, 1)
                v.wait_ge(wprep, 4)
                v.tensor_tensor(whp[:, 2], whr[:], whp[:, 1], ALU.subtract).then_inc(wprep, 1)
                ln.vector(v)
                for i, job in enumerate(jobs):
                    v.wait_ge(left, i + 1)
                    x = xi[:, i % R, :]
                    v.tensor_copy(xi_part(0, job), x).then_inc(part1, 1)
                    v.wait_ge(part1, i + 1)
                    v.tensor_tensor(x, x, xi_part(0, job), ALU.subtract).then_inc(part2, 1)
                    v.wait_ge(part2, 2 * i + 1)
                    v.tensor_copy(xi_part(1, job), x).then_inc(part2, 1)
                with v.Fori(0, S // (2 * U)) as it:
                    for half in range(2):
                        for t in range(U):
                            for k in range(KD):
                                v.wait_ge(h_ready[k], it * (2 * U) + (half * U + t + 1))
                                v.tensor_tensor(hp16[:, t % 2, 1, k, :], hr[:, half, k, :, t], hp16[:, t % 2, 0, k, :],
                                                ALU.subtract).then_inc(lo_ready[k], 1)

            @block.gpsimd
            def _(pool):
                pool.memset(xip[:, :, :, :, S:S + U].rearrange("p q m b t -> p (q m b) t"), 0.0).then_inc(pre, 1)
                for k in range(KD):
                    pool.memset(hp16[:, 1, 0, k], 0.0).then_inc(hi_ready[k], 1)
                    pool.memset(hp16[:, 1, 1, k], 0.0).then_inc(lo_ready[k], 1)
                pool.memset(g.hist[:, 0, 0, 0:U], 0.0).then_inc(copied, 1)
                pool.memset(g.hist[:, 0, 0, U:2 * U], 0.0).then_inc(copied, 1)
                for i, job in enumerate(jobs):
                    pool.wait_ge(part2, 2 * (i + 1))
                    pool.tensor_tensor(xi_part(2, job), xi[:, i % R, :], xi_part(1, job),
                                       ALU.subtract).then_inc(part3, 1)
                following.prepare(pool)
                pool.wait_ge(copied, 2)
                with pool.Fori(0, S // (2 * U)) as it:
                    for half in range(2):
                        for k in range(KD):
                            pool.wait_ge(h_ready[k], it * (2 * U) + (half + 1) * U)
                        t0 = it * (2 * U) + half * U
                        pool.tensor_copy(g.hist[:, :, :, bass.ds(t0, U)], hr[:, half]).then_inc(copied, 1)


def gated_experts(g, n, w, out):
    g.stage = f"e{n}_"
    nc = g.nc
    with ExitStack() as ctx:
        hT = g.sb("hT", [P, 2, MH, CH], ctx=ctx)
        norm_buffers(g, ctx, over=hT[:, 1].rearrange("p m n -> p (m n)")[:, 0:NT * D])
        wr, cb = w.wr, w.cb
        wd, wd_in = g.sb("wd", [P, MH, D], ctx=ctx), g.sem(f"e{n}_wd_in")
        xh = g.sb("xh", [P, KD, B * S], F32R, ctx=ctx)
        xl = g.sb("xl", [P, KD, B * S], F32R, ctx=ctx)
        x_hi, x_lo = g.sem(f"e{n}_x_hi"), g.sem(f"e{n}_x_lo")
        sc = g.sb("sc", [P, TC, E1], ctx=ctx)
        sb = g.sb("sb", [P, TC, E1], ctx=ctx)
        prs = g.sb("prs", [P, TC, G1, 6], ctx=ctx)
        gs = g.sb("gs", [P, TC, G1], ctx=ctx)
        gm = g.sb("gm", [P, TC, G1], ctx=ctx)
        gmn = g.sb("gmn", [P, TC, G1], ctx=ctx)
        gc = g.sb("gc", [P, TC, G1, G1], ctx=ctx)
        ge = g.sb("ge", [P, TC, G1, G1], ctx=ctx)
        cmp = g.sb("cmp1", [P, TC, E1, E1], ctx=ctx)
        eq = g.sb("eq1", [P, TC, E1, E1], ctx=ctx)
        sel = g.sb("sel1", [P, TC, E1], ctx=ctx)
        tot = g.sb("tot", [P, TC], ctx=ctx)
        comb = g.sb("comb", [P, 2, TC, E1], ctx=ctx)
        cp1 = g.sb("cp1", [E1, CH], BF16, ctx=ctx)
        cr = g.sb("cr", [E1, CH], ctx=ctx)
        cp2 = g.sb("cp2", [E1, CH], BF16, ctx=ctx)
        cps = g.sb("cps", [P, 2, CH], BF16, ctx=ctx)
        sg = g.sb("sg", [P, 2, CH], ctx=ctx)
        ln = Norm(g, n)
        (logits, scored, chain, combed, cT, c1, parted, gmade, umade, bmade, sgd, hmul, hready, ymade,
         xup, stored, zero) = (g.sem(f"e{n}_{k}") for k in (
             "logits", "scored", "chain", "combed", "cT", "c1", "parted", "gmade", "umade", "bmade",
             "sgd", "hmul", "hready", "ymade", "xup", "stored", "zero"))
        NR = MH - MS
        ROUTE_AT = MH - 3
        KR = 2 * QD + E1
        with nc.Block() as block:
            @block.sync
            def _(sp):
                sp.dma_start(wd[:], g.inputs["down"].rearrange("(m p) n -> p m n", p=P)).then_inc(wd_in, 16)
                ov = out.rearrange("(t p) d -> p t d", p=P)
                for c in range(NC):
                    sp.wait_ge(xup, TC * (c + 1))
                    sp.dma_start(ov[:, TC * c:TC * c + TC, :], g.x[:, TC * c:TC * c + TC, :]).then_inc(stored, 16)
                sp.wait_ge(stored, 16 * NC)

            @block.tensor
            def _(pe):
                ln.tensor(pe, 0)
                pe.wait_ge(ln.xnT, TC)

                def route(c):
                    if c:
                        pe.wait_ge(parted, 2 * c)
                    for t in range(TC):
                        last = acc(pe, g.b7[:, E1 * t:E1 * t + E1],
                                   [(g.xnT[:, k, CH * c + P * t:CH * c + P * t + P], wr[:, k, :]) for k in range(KD)])
                    last.then_inc(logits, 1)

                def turn(c):
                    pe.wait_ge(combed, c + 1)
                    for t in range(TC):
                        last = pe.transpose(g.b7[0:E1, P * t:P * t + P], comb[:, c % 2, t, :], g.ident[:])
                    last.then_inc(cT, 1)

                def down(c):
                    pe.wait_ge(wd_in, 16)
                    pe.wait_ge(ln.xnT, NT)
                    pe.wait_ge(hmul, MH * (c + 1))
                    pe.wait_ge(hready, NR * (c + 1))
                    for t in range(TC * c, TC * c + TC):
                        if t >= 2:
                            pe.wait_ge(xup, t - 1)
                        acc(pe, (g.b4, g.b5)[t % 2][:, 0:D],
                            [(hT[:, c % 2, m, P * (t % TC):P * (t % TC) + P], wd[:, m, :])
                             for m in range(MH)]).then_inc(ymade, 1)

                route(0)
                for c in range(NC):
                    for m in range(MH):
                        i = MH * c + m
                        if i >= 2:
                            pe.wait_ge(sgd, i - 1)
                        cols, tok = slice(m * P, (m + 1) * P), slice(CH * c, CH * c + CH)
                        if m == 0:
                            pe.wait_ge(x_lo, c + 1)

                        def products(j):
                            return [(wt[:, k, cols], x[:, k, tok])
                                    for wt, x in ((w.hi[j], xh), (w.lo[j], xh), (w.hi[j], xl)) for k in range(KD)]

                        acc(pe, (g.b0, g.b1)[i % 2][:], products(0)).then_inc(gmade, 1)
                        if i >= 2:
                            pe.wait_ge(hmul, i - 1)
                        acc(pe, (g.b2, g.b3)[i % 2][:], products(1)).then_inc(umade, 1)
                        if c == 0 and m + 1 < NC:
                            ln.tensor(pe, m + 1)
                        if m == MS - 1:
                            turn(c)
                        if m >= MS:
                            pe.wait_ge(parted, 2 * (c + 1))
                            j = NR * c + m - MS
                            if j:
                                pe.wait_ge(hready, j)
                            pe.matmul(g.b6[:], g.sel_pair[0:KR, m - MS, :], cps[0:KR, c % 2, :],
                                      start=True, stop=True).then_inc(bmade, 1)
                        if m == ROUTE_AT and c + 1 < NC:
                            pe.wait_ge(ln.xnT, TC * (c + 2))
                            route(c + 1)
                    if c:
                        down(c - 1)
                down(NC - 1)

            @block.scalar
            def _(act):
                def norm(c):
                    ln.scalar(act, c)
                    act.wait_ge(ln.xnT, TC * (c + 1))
                    cols = slice(CH * c, CH * c + CH)
                    act.activation(xh[:, :, cols], g.xnT[:, :, cols], ACT.Copy).then_inc(x_hi, 1)

                def scores(c):
                    act.wait_ge(logits, c + 1)
                    if c:
                        act.wait_ge(combed, c)
                    act.activation(sc[:].rearrange("p t e -> p (t e)"), g.b7[:, 0:TC * E1],
                                   ACT.Sigmoid).then_inc(scored, 1)

                norm(0)
                scores(0)
                for c in range(NC):
                    for m in range(MH):
                        i = MH * c + m
                        act.wait_ge(gmade, i + 1)
                        if i >= 2:
                            act.wait_ge(hmul, i - 1)
                        act.activation(sg[:, i % 2, :], (g.b0, g.b1)[i % 2][:], ACT.Silu).then_inc(sgd, 1)
                        if c == 0 and m + 1 < NC:
                            norm(m + 1)
                        if m == MS - 1:
                            act.wait_ge(cT, c + 1)
                            act.activation(cp1[:], g.b7[0:E1, :], ACT.Copy).then_inc(c1, 1)
                        if m == ROUTE_AT and c + 1 < NC:
                            scores(c + 1)

            @block.gpsimd
            def _(pool):
                pool.memset(cps[:].rearrange("p a n -> p (a n)"), 0.0).then_inc(zero, 1)
                for c in range(NC):
                    pool.wait_ge(x_hi, c + 1)
                    cols = slice(CH * c, CH * c + CH)
                    pool.tensor_tensor(xl[:, :, cols], g.xnT[:, :, cols], xh[:, :, cols], ALU.subtract).then_inc(x_lo, 1)

            @block.vector
            def _(v):
                ln.vector(v)
                v.wait_ge(zero, 1)
                count = [0]

                def step(ins):
                    count[0] += 1
                    ins.then_inc(chain, 1)
                    v.wait_ge(chain, count[0])

                def wide(ap, e):
                    return ap.unsqueeze(3).broadcast_to([P, TC, G1, e])

                def choose_groups(c):
                    v.wait_ge(scored, c + 1)
                    step(v.tensor_tensor(sb[:], sc[:], cb[:].unsqueeze(1).broadcast_to([P, TC, E1]), ALU.add))
                    sg4 = sb[:].rearrange("p t (q e) -> p (t q) e", q=G1)
                    pv = prs[:].rearrange("p t q s -> p (t q) s")
                    step(v.tensor_tensor(pv[:, :, 0:3], sg4[:, :, 0:3], sg4[:, :, 1:4], ALU.add))
                    step(v.tensor_tensor(pv[:, :, 3:5], sg4[:, :, 0:2], sg4[:, :, 2:4], ALU.add))
                    step(v.tensor_tensor(pv[:, :, 5:6], sg4[:, :, 0:1], sg4[:, :, 3:4], ALU.add))
                    step(v.tensor_reduce(gs[:].rearrange("p t q -> p (t q)"), pv, AX.X, ALU.max))
                    step(rank_select(v, step, gs[:], g.tie16[:, 0:G1, 0:G1], gm[:], gc[:], ge[:], G1, 2))

                def choose_experts(c):
                    step(v.tensor_scalar(gmn[:], gm[:], 1.0, BIG, ALU.subtract, ALU.mult))
                    s4 = sb[:].rearrange("p t (q e) -> p t q e", q=G1)
                    step(v.tensor_tensor(s4, s4, wide(gm[:], EPG), ALU.mult))
                    step(v.tensor_tensor(s4, s4, wide(gmn[:], EPG), ALU.add))
                    step(rank_select(v, step, sb[:], g.tie16[:], sel[:], cmp[:], eq[:], E1, TOP1))

                def weigh(c):
                    step(v.tensor_tensor(sel[:], sel[:], sc[:], ALU.mult))
                    step(v.tensor_reduce(tot[:], sel[:], AX.X, ALU.add))
                    step(v.tensor_scalar(tot[:], tot[:], 1e-20, None, ALU.add))
                    step(v.reciprocal(tot[:], tot[:]))
                    v.tensor_tensor(comb[:, c % 2], sel[:], tot[:].unsqueeze(2).broadcast_to([P, TC, E1]),
                                    ALU.mult).then_inc(combed, 1)

                def parts(c):
                    v.wait_ge(c1, c + 1)
                    v.tensor_tensor(cr[:], g.b7[0:E1, :], cp1[:], ALU.subtract).then_inc(parted, 1)
                    v.wait_ge(parted, 2 * c + 1)
                    step(v.tensor_copy(cp2[:], cr[:]))
                    step(v.tensor_copy(cps[0:E1, c % 2, :], cp1[:]))
                    step(v.tensor_copy(cps[QD:QD + E1, c % 2, :], cp2[:]))
                    v.tensor_tensor(cps[2 * QD:2 * QD + E1, c % 2, :], cr[:], cp2[:], ALU.subtract).then_inc(parted, 1)

                def finish(c):
                    for t in range(TC * c, TC * c + TC):
                        v.wait_ge(ymade, t + 1)
                        v.tensor_tensor(g.x[:, t, :], (g.b4, g.b5)[t % 2][:, 0:D], g.x[:, t, :],
                                        ALU.add).then_inc(xup, 1)

                for part in (choose_groups, choose_experts, weigh):
                    part(0)
                for c in range(NC):
                    for m in range(MH):
                        i = MH * c + m
                        v.wait_ge(sgd, i + 1)
                        v.wait_ge(umade, i + 1)
                        if c >= 2 and m == 0:
                            v.wait_ge(ymade, TC * (c - 1))
                        h = hT[:, c % 2, m, :]
                        ins = v.tensor_tensor(h, sg[:, i % 2, :], (g.b2, g.b3)[i % 2][:], ALU.mult)
                        ins.then_inc(hmul, 1)
                        if m >= MS:
                            v.wait_ge(hmul, i + 1)
                            v.wait_ge(bmade, NR * c + m - MS + 1)
                            v.tensor_tensor(h, h, g.b6[:], ALU.mult).then_inc(hready, 1)
                        if m == MS - 1:
                            parts(c)
                        if 0 <= m - ROUTE_AT < 3 and c + 1 < NC:
                            (choose_groups, choose_experts, weigh)[m - ROUTE_AT](c + 1)
                    if c:
                        finish(c - 1)
                finish(NC - 1)


def decoder(nc, a, out):
    with ExitStack() as ctx:
        g = Prog(nc, ctx)
        g.inputs = a
        g.b0, g.b1, g.b2, g.b3, g.b4, g.b5, g.b6, g.b7 = (
            ctx.enter_context(nc.psum_tensor(f"b{i}", [P, 512], F32)) for i in range(8))
        g.x = g.sb("x", [P, NT, D])
        g.bn = g.sb("bn", [P, NT, 6])
        g.mv = g.sb("mv", [P, NT, 2])
        g.ve = g.sb("ve", [P, NT])
        g.rs = g.sb("rs", [P, NT])
        g.q_scr = nc.dram_tensor("q_scr", (3, D, B * S), BF16)
        g.k_scr = nc.dram_tensor("k_scr", (3, D, B * S), BF16)
        g.kc_scr = nc.dram_tensor("kc_scr", (3, D, B * M2), BF16)
        g.wo_dram = {0: a["L0_attn_wo"], 1: a["L0_xattn_wo"], 4: a["L1_xattn_wo"]}
        constants(g, a["x"])

        with ExitStack() as inner:
            g.stage = "self_"
            g.va = g.sb("va", [P, NT, H, QD], ctx=inner)
            st = Stacks(g, 0, True, None, inner)
            project(g, 0, {"wqkv": a["L0_attn_wqkvT"]}, True, st)
            attention(g, 0, True, st)

        g.stage = "ctx_"
        g.vc = g.sb("vc", [P, B, H, QD])
        rnn_weights = RecurrenceWeights(g, ctx, a)
        with ExitStack() as inner0:
            expert_weights = ExpertWeights0(g, inner0, a)
            w = {"ctxT": a["ctxT"], "wq": a["L0_xattn_Wq"], "wk": a["L0_xattn_Wk"], "wv": a["L0_xattn_Wv"],
                 "bq": None, "bo": None}
            with ExitStack() as inner:
                g.stage = "ctx0_"
                st = Stacks(g, 1, False, a["mask"], inner)
                project(g, 1, w, False, st)
                attention(g, 1, False, st, w, expert_weights)
            linear_experts(g, 2, expert_weights, rnn_weights)

        g.recycle()
        g.stage = "experts1_"
        expert_weights = ExpertWeights1(g, ctx)
        with ExitStack() as history:
            g.hist = g.sb("hist", [P, KD, B, S], ctx=history)
            recurrence(g, 3, rnn_weights, expert_weights)
            g.recycle()
            w = {"ctxT": a["ctxT"], "wq": a["L1_xattn_wq"], "wk": a["L1_xattn_wk"], "wv": a["L1_xattn_wv"],
                 "bq": a["L1_xattn_bq"], "bk": a["L1_xattn_bk"], "bv": a["L1_xattn_bv"], "bo": a["L1_xattn_bo"]}
            with ExitStack() as inner:
                g.stage = "ctx1_"
                st = Stacks(g, 4, False, None, inner)
                project(g, 4, w, False, st)
                attention(g, 4, False, st, w)

        gated_experts(g, 5, expert_weights, out)


def _layout(i):
    def by_feature(w):
        return w.transpose(1, 0, 2).reshape(w.shape[1], -1)

    return {
        "x": i["x"].reshape(B * S, D),
        "ctxT": i["ctx_768"].reshape(B * M2, C2).T,
        "mask": i["mask_BxS2_bf1"].reshape(B * M2).view(np.uint8),
        "L0_attn_wqkvT": i["L0_attn_w_qkv"].T,
        "L0_attn_wo": i["L0_attn_w_proj"].T,
        "L0_xattn_Wq": i["L0_xattn_Wq"], "L0_xattn_Wk": i["L0_xattn_Wk"], "L0_xattn_Wv": i["L0_xattn_Wv"],
        "L0_xattn_wo": i["L0_xattn_Wo"],
        "L0_ffn_Wg": i["L0_ffn_Wg"], "L0_ffn_bg": i["L0_ffn_bg"], "L0_ffn_We": i["L0_ffn_We"], "L0_ffn_be": i["L0_ffn_be"],
        "L1_attn_WiT": i["L1_attn_Wi"].T, "L1_attn_WhT": i["L1_attn_Wh"].T,
        "L1_attn_bi": i["L1_attn_bi"], "L1_attn_bh": i["L1_attn_bh"],
        "L1_xattn_wq": i["L1_xattn_wq"], "L1_xattn_wk": i["L1_xattn_wk"], "L1_xattn_wv": i["L1_xattn_wv"],
        "L1_xattn_bq": i["L1_xattn_bq"], "L1_xattn_bk": i["L1_xattn_bk"], "L1_xattn_bv": i["L1_xattn_bv"],
        "L1_xattn_wo": i["L1_xattn_wo"], "L1_xattn_bo": i["L1_xattn_bo"],
        "router": i["L1_ffn_router_w"].T, "cbias": i["L1_ffn_correction_bias"],
        "gate": np.concatenate([i["L1_ffn_shared_gate_w"].T, by_feature(i["L1_ffn_gate_w"])], axis=1),
        "up": np.concatenate([i["L1_ffn_shared_up_w"].T, by_feature(i["L1_ffn_up_w"])], axis=1),
        "down": np.concatenate([i["L1_ffn_shared_down_w"].T, i["L1_ffn_down_w"].reshape(E1 * 64, D)], axis=0),
    }


def kernel(**inputs):
    import concourse.bacc as bacc
    from concourse.bass_utils import run_bass_kernel_spmd

    nc = bacc.Bacc("TRN2", target_bir_lowering=False, num_devices=1)
    arrays, aps = {}, {}
    for name, value in _layout({k: np.asarray(v) for k, v in inputs.items()}).items():
        value = np.ascontiguousarray(value)
        arrays[f"in_{name}"] = value
        aps[name] = nc.dram_tensor(f"in_{name}", value.shape, mybir.dt.from_np(value.dtype), kind="ExternalInput").ap()
    out = nc.dram_tensor("out", (B * S, D), F32, kind="ExternalOutput").ap()
    decoder(nc, aps, out)
    r = run_bass_kernel_spmd(nc, [arrays], core_ids=[0])
    return r.results[0]["out"].reshape(B, S, D)
```
